# Optimizing a Trainium2 kernel written in Bass

```python
import numpy as np
import jax
import jax.numpy as jnp

def _softmax(x, axis=-1):
    return jax.nn.softmax(x, axis=axis)

def _gelu(x):
    return jax.nn.gelu(x, approximate=True)

def _silu(x):
    return jax.nn.silu(x)

def _sigmoid(x):
    return jax.nn.sigmoid(x)

def _layernorm(x, axis=-1, eps=1e-05):
    m = jnp.mean(x, axis=axis, keepdims=True)
    v = jnp.var(x, axis=axis, keepdims=True)
    return (x - m) / jnp.sqrt(v + eps)

def _scatter_add(tgt, idx, src, axis=0):
    return tgt.at[idx].add(src)

def _segment_sum(src, seg, n):
    return jax.ops.segment_sum(src, seg, n)
kernel_name = 'mk_seq_postln_d2_jaxref_r8_acc20f'

def setup_inputs(seed: int=0):
    np.random.seed(seed)
    _w = jnp.asarray

    def _L0_attn_setup():
        import math
        import jax, jax.numpy as jnp
        import numpy as np
        N_HEADS = 16
        THETA = 10000.0

        def _rope_cos_sin(S, head_dim):
            half = head_dim // 2
            inv_freq = 1.0 / THETA ** (jnp.arange(half, dtype=jnp.float32) / half)
            t = jnp.arange(S, dtype=jnp.float32)
            freqs = t[:, None] * inv_freq[None, :]
            return (jnp.cos(freqs), jnp.sin(freqs))

        def _apply_rope(x, cos, sin):
            half = x.shape[-1] // 2
            x1, x2 = (x[..., :half], x[..., half:])
            c = cos[None, None, :, :]
            s = sin[None, None, :, :]
            return jnp.concatenate([x1 * c - x2 * s, x1 * s + x2 * c], axis=-1)
        key = jax.random.key(seed)
        k1, k2, k3 = jax.random.split(key, 3)
        B, S, D = (4, 256, 128)
        x = jax.random.normal(k1, (B, S, D), dtype=jnp.float32)
        w_qkv = jax.random.normal(k2, (3 * D, D), dtype=jnp.float32) * (1.0 / math.sqrt(D))
        w_out = jax.random.normal(k3, (D, D), dtype=jnp.float32) * (1.0 / math.sqrt(D))
        return {'x': x, 'w_qkv': w_qkv, 'w_out': w_out}
    _L0_attn_in = _L0_attn_setup()

    def _L0_ffn_setup():
        import jax, jax.numpy as jnp
        import numpy as np
        D_IN, D_HID = (128, 512)

        def _ternary(key, shape):
            return jax.random.randint(key, shape, -1, 2).astype(jnp.float32)

        def _tlin(x, w, s):
            return jnp.einsum('bsi,oi->bso', x, w) * s
        key = jax.random.key(seed)
        ks = jax.random.split(key, 12)
        inv = lambda fan: 1.0 / np.sqrt(fan).astype(np.float32)
        return {'x': jax.random.normal(ks[0], (4, 256, D_IN), dtype=jnp.float32), 'w1_w': _ternary(ks[1], (D_HID, D_IN)), 'w1_s': jax.random.uniform(ks[2], (D_HID,), dtype=jnp.float32) * inv(D_IN), 'w2_w': _ternary(ks[3], (D_HID, D_IN)), 'w2_s': jax.random.uniform(ks[4], (D_HID,), dtype=jnp.float32) * inv(D_IN), 'h1_w': _ternary(ks[5], (D_HID, D_HID)), 'h1_s': jax.random.uniform(ks[6], (D_HID,), dtype=jnp.float32) * inv(D_HID), 'h2_w': _ternary(ks[7], (D_HID, D_HID)), 'h2_s': jax.random.uniform(ks[8], (D_HID,), dtype=jnp.float32) * inv(D_HID), 'w3_w': _ternary(ks[9], (D_IN, D_HID)), 'w3_s': jax.random.uniform(ks[10], (D_IN,), dtype=jnp.float32) * inv(D_HID)}
    _L0_ffn_in = _L0_ffn_setup()

    def _L1_attn_setup():
        import jax, jax.numpy as jnp
        import numpy as np
        B, N, DIM = (4, 128, 128)
        H, DH = (16, 64)
        NUM_MEM = 4
        TOPK = 64
        QK_SCALE = 10.0

        def l2norm(t, eps=1e-12):
            return t / jnp.clip(jnp.linalg.norm(t, axis=-1, keepdims=True), eps)
        key = jax.random.key(seed)
        ks = jax.random.split(key, 12)
        s = 0.02
        inp = {'x': jax.random.normal(ks[0], (B, N, DIM), dtype=jnp.float32), 'Wq': jax.random.normal(ks[1], (DIM, H * DH), dtype=jnp.float32) * s, 'Wk': jax.random.normal(ks[2], (DIM, H * DH), dtype=jnp.float32) * s, 'Wv': jax.random.normal(ks[3], (DIM, H * DH), dtype=jnp.float32) * s, 'W_pre_th': jax.random.normal(ks[4], (H, H), dtype=jnp.float32) * (1.0 / H) ** 0.5, 'W_post_th': jax.random.normal(ks[5], (H, H), dtype=jnp.float32) * (1.0 / H) ** 0.5, 'mem_k': jax.random.normal(ks[6], (H, NUM_MEM, DH), dtype=jnp.float32), 'mem_v': jax.random.normal(ks[7], (H, NUM_MEM, DH), dtype=jnp.float32), 'head_scale_params': jnp.ones((1, H, 1, 1), dtype=jnp.float32), 'Wg': jax.random.normal(ks[8], (DIM, H * DH), dtype=jnp.float32) * s, 'bg': jnp.ones((H * DH,), dtype=jnp.float32), 'Wo': jax.random.normal(ks[9], (H * DH, DIM), dtype=jnp.float32) * s}
        return inp
    _L1_attn_in = _L1_attn_setup()

    def _L1_ffn_setup():
        import jax, jax.numpy as jnp
        import numpy as np
        DIM = 128
        HID = 64
        N_EXPERTS = 16
        TOP_K = 4
        key = jax.random.key(seed)
        ks = jax.random.split(key, 8)
        s = 0.02
        x = jax.random.normal(ks[0], (2, 128, DIM), dtype=jnp.float32)
        gate_w = jax.random.normal(ks[1], (N_EXPERTS, DIM), dtype=jnp.float32) * s
        w1 = jax.random.normal(ks[2], (N_EXPERTS, HID, DIM), dtype=jnp.float32) * s
        w3 = jax.random.normal(ks[3], (N_EXPERTS, HID, DIM), dtype=jnp.float32) * s
        w2 = jax.random.normal(ks[4], (N_EXPERTS, DIM, HID), dtype=jnp.float32) * s
        sw1 = jax.random.normal(ks[5], (HID, DIM), dtype=jnp.float32) * s
        sw3 = jax.random.normal(ks[6], (HID, DIM), dtype=jnp.float32) * s
        sw2 = jax.random.normal(ks[7], (DIM, HID), dtype=jnp.float32) * s
        return {'x': x, 'gate_w': gate_w, 'w1': w1, 'w3': w3, 'w2': w2, 'sw1': sw1, 'sw3': sw3, 'sw2': sw2}
    _L1_ffn_in = _L1_ffn_setup()
    _d = {'L0_attn_x': _L0_attn_in['x'], 'L0_attn_w_qkv': _L0_attn_in['w_qkv'], 'L0_attn_w_out': _L0_attn_in['w_out'], 'L0_ffn_w1_w': _L0_ffn_in['w1_w'], 'L0_ffn_w1_s': _L0_ffn_in['w1_s'], 'L0_ffn_w2_w': _L0_ffn_in['w2_w'], 'L0_ffn_w2_s': _L0_ffn_in['w2_s'], 'L0_ffn_h1_w': _L0_ffn_in['h1_w'], 'L0_ffn_h1_s': _L0_ffn_in['h1_s'], 'L0_ffn_h2_w': _L0_ffn_in['h2_w'], 'L0_ffn_h2_s': _L0_ffn_in['h2_s'], 'L0_ffn_w3_w': _L0_ffn_in['w3_w'], 'L0_ffn_w3_s': _L0_ffn_in['w3_s'], 'L1_attn_Wq': _L1_attn_in['Wq'], 'L1_attn_Wk': _L1_attn_in['Wk'], 'L1_attn_Wv': _L1_attn_in['Wv'], 'L1_attn_W_pre_th': _L1_attn_in['W_pre_th'], 'L1_attn_W_post_th': _L1_attn_in['W_post_th'], 'L1_attn_mem_k': _L1_attn_in['mem_k'], 'L1_attn_mem_v': _L1_attn_in['mem_v'], 'L1_attn_head_scale_params': _L1_attn_in['head_scale_params'], 'L1_attn_Wg': _L1_attn_in['Wg'], 'L1_attn_bg': _L1_attn_in['bg'], 'L1_attn_Wo': _L1_attn_in['Wo'], 'L1_ffn_gate_w': _L1_ffn_in['gate_w'], 'L1_ffn_w1': _L1_ffn_in['w1'], 'L1_ffn_w3': _L1_ffn_in['w3'], 'L1_ffn_w2': _L1_ffn_in['w2'], 'L1_ffn_sw1': _L1_ffn_in['sw1'], 'L1_ffn_sw3': _L1_ffn_in['sw3'], 'L1_ffn_sw2': _L1_ffn_in['sw2']}
    _x0 = _d['L0_attn_x']
    _d['L0_attn_x'] = jax.random.normal(jax.random.fold_in(jax.random.key(seed), 1), (8, 512, 128), dtype=_x0.dtype)
    del _x0
    return _d

def reference(L0_attn_x, L0_attn_w_qkv, L0_attn_w_out, L0_ffn_w1_w, L0_ffn_w1_s, L0_ffn_w2_w, L0_ffn_w2_s, L0_ffn_h1_w, L0_ffn_h1_s, L0_ffn_h2_w, L0_ffn_h2_s, L0_ffn_w3_w, L0_ffn_w3_s, L1_attn_Wq, L1_attn_Wk, L1_attn_Wv, L1_attn_W_pre_th, L1_attn_W_post_th, L1_attn_mem_k, L1_attn_mem_v, L1_attn_head_scale_params, L1_attn_Wg, L1_attn_bg, L1_attn_Wo, L1_ffn_gate_w, L1_ffn_w1, L1_ffn_w3, L1_ffn_w2, L1_ffn_sw1, L1_ffn_sw3, L1_ffn_sw2):

    def _L0_attn_ref(x, w_qkv, w_out):
        import math
        import jax, jax.numpy as jnp
        import numpy as np
        N_HEADS = 16
        THETA = 10000.0

        def _rope_cos_sin(S, head_dim):
            half = head_dim // 2
            inv_freq = 1.0 / THETA ** (jnp.arange(half, dtype=jnp.float32) / half)
            t = jnp.arange(S, dtype=jnp.float32)
            freqs = t[:, None] * inv_freq[None, :]
            return (jnp.cos(freqs), jnp.sin(freqs))

        def _apply_rope(x, cos, sin):
            half = x.shape[-1] // 2
            x1, x2 = (x[..., :half], x[..., half:])
            c = cos[None, None, :, :]
            s = sin[None, None, :, :]
            return jnp.concatenate([x1 * c - x2 * s, x1 * s + x2 * c], axis=-1)
        B, S, D = x.shape
        H = N_HEADS
        hd = D // H
        qkv = x @ w_qkv.T
        q, k, v = jnp.split(qkv, 3, axis=-1)

        def reshape(t):
            return t.reshape(B, S, H, hd).transpose(0, 2, 1, 3)
        q, k, v = (reshape(q), reshape(k), reshape(v))
        cos, sin = _rope_cos_sin(S, hd)
        q = _apply_rope(q.astype(jnp.float32), cos, sin).astype(x.dtype)
        k = _apply_rope(k.astype(jnp.float32), cos, sin).astype(x.dtype)
        scale = math.sqrt(hd)
        scores = jnp.einsum('bhsd,bhtd->bhst', q, k) / scale
        causal = jnp.tril(jnp.ones((S, S), dtype=bool))
        scores = jnp.where(causal[None, None], scores, -jnp.inf)
        attn = jax.nn.softmax(scores.astype(jnp.float32), axis=-1).astype(x.dtype)
        out = jnp.einsum('bhst,bhtd->bhsd', attn, v)
        out = out.transpose(0, 2, 1, 3).reshape(B, S, D)
        return out @ w_out.T

    def _L0_ffn_ref(x, w1_w, w1_s, w2_w, w2_s, h1_w, h1_s, h2_w, h2_s, w3_w, w3_s):
        import jax, jax.numpy as jnp
        import numpy as np
        D_IN, D_HID = (128, 512)

        def _ternary(key, shape):
            return jax.random.randint(key, shape, -1, 2).astype(jnp.float32)

        def _tlin(x, w, s):
            return jnp.einsum('bsi,oi->bso', x, w) * s
        h = jax.nn.silu(_tlin(x, w1_w, w1_s)) * _tlin(x, w2_w, w2_s)
        h = jax.nn.gelu(_tlin(h, h1_w, h1_s), approximate=False)
        h = jax.nn.gelu(_tlin(h, h2_w, h2_s), approximate=False)
        return _tlin(h, w3_w, w3_s)

    def _L1_attn_ref(x, Wq, Wk, Wv, W_pre_th, W_post_th, mem_k, mem_v, head_scale_params, Wg, bg, Wo):
        import jax, jax.numpy as jnp
        import numpy as np
        B, N, DIM = (4, 128, 128)
        H, DH = (16, 64)
        NUM_MEM = 4
        TOPK = 64
        QK_SCALE = 10.0

        def l2norm(t, eps=1e-12):
            return t / jnp.clip(jnp.linalg.norm(t, axis=-1, keepdims=True), eps)
        b, n, _ = x.shape
        q = (x @ Wq).reshape(b, n, H, DH).transpose(0, 2, 1, 3)
        k = (x @ Wk).reshape(b, n, H, DH).transpose(0, 2, 1, 3)
        v = (x @ Wv).reshape(b, n, H, DH).transpose(0, 2, 1, 3)
        mk = jnp.broadcast_to(mem_k[None], (b, H, NUM_MEM, DH))
        mv = jnp.broadcast_to(mem_v[None], (b, H, NUM_MEM, DH))
        k = jnp.concatenate([mk, k], axis=2)
        v = jnp.concatenate([mv, v], axis=2)
        q = l2norm(q)
        k = l2norm(k)
        dots = jnp.einsum('bhid,bhjd->bhij', q, k) * QK_SCALE
        dots = jnp.einsum('hg,bgij->bhij', W_pre_th, dots)
        mask_value = -jnp.finfo(dots.dtype).max
        j = n + NUM_MEM
        col_pos = jnp.arange(j) - NUM_MEM
        causal = jnp.arange(n)[:, None] < col_pos[None, :]
        dots = jnp.where(causal[None, None], mask_value, dots)
        top = jax.lax.top_k(dots, TOPK)[0]
        vk = top[..., -1:]
        dots = jnp.where(dots < vk, mask_value, dots)
        attn = jax.nn.softmax(dots, axis=-1)
        attn = jnp.einsum('hg,bgij->bhij', W_post_th, attn)
        out = jnp.einsum('bhij,bhjd->bhid', attn, v)
        out = out * head_scale_params
        out = out.transpose(0, 2, 1, 3).reshape(b, n, H * DH)
        gates = x @ Wg + bg
        out = out * jax.nn.sigmoid(gates)
        return out @ Wo

    def _L1_ffn_ref(x, gate_w, w1, w3, w2, sw1, sw3, sw2):
        import jax, jax.numpy as jnp
        import numpy as np
        DIM = 128
        HID = 64
        N_EXPERTS = 16
        TOP_K = 4
        bsz, seq_len, dim = x.shape
        xf = x.reshape(-1, dim)
        T = xf.shape[0]
        probs = jax.nn.softmax(xf @ gate_w.T, axis=-1)
        top_w, top_idx = jax.lax.top_k(probs, TOP_K)
        top_w = top_w / jnp.sum(top_w, axis=-1, keepdims=True)
        rows = jnp.arange(T)[:, None]
        combine = jnp.zeros((T, N_EXPERTS), dtype=xf.dtype).at[rows, top_idx].set(top_w)
        h1 = jnp.einsum('td,ehd->teh', xf, w1)
        h3 = jnp.einsum('td,ehd->teh', xf, w3)
        act = jax.nn.silu(h1) * h3
        eout = jnp.einsum('teh,edh->ted', act, w2)
        moe_out = jnp.einsum('ted,te->td', eout, combine)
        shared = jax.nn.silu(xf @ sw1.T) * (xf @ sw3.T) @ sw2.T
        return (moe_out + shared).reshape(bsz, seq_len, dim)
    x = L0_attn_x
    x = _layernorm(x + _L0_attn_ref(x, L0_attn_w_qkv, L0_attn_w_out), axis=-1)
    x = _layernorm(x + _L0_ffn_ref(x, L0_ffn_w1_w, L0_ffn_w1_s, L0_ffn_w2_w, L0_ffn_w2_s, L0_ffn_h1_w, L0_ffn_h1_s, L0_ffn_h2_w, L0_ffn_h2_s, L0_ffn_w3_w, L0_ffn_w3_s), axis=-1)
    x = _layernorm(x + _L1_attn_ref(x, L1_attn_Wq, L1_attn_Wk, L1_attn_Wv, L1_attn_W_pre_th, L1_attn_W_post_th, L1_attn_mem_k, L1_attn_mem_v, L1_attn_head_scale_params, L1_attn_Wg, L1_attn_bg, L1_attn_Wo), axis=-1)
    x = _layernorm(x + _L1_ffn_ref(x, L1_ffn_gate_w, L1_ffn_w1, L1_ffn_w3, L1_ffn_w2, L1_ffn_sw1, L1_ffn_sw3, L1_ffn_sw2), axis=-1)
    return x

_drawn_inputs = setup_inputs


def setup_inputs(seed=0):
    import zlib

    import numpy as np

    out = dict(_drawn_inputs(seed))
    spreads = {'L1_attn_head_scale_params': (1.0, 0.6), 'L1_attn_bg': (1.0, 0.6)}
    factors = {'L0_ffn_w1_w': 8.0,
     'L0_ffn_w1_s': 8.0,
     'L0_ffn_w2_w': 8.0,
     'L0_ffn_w2_s': 8.0,
     'L0_ffn_h1_w': 8.0,
     'L0_ffn_h1_s': 8.0,
     'L0_ffn_h2_w': 8.0,
     'L0_ffn_h2_s': 8.0,
     'L0_ffn_w3_w': 8.0,
     'L0_ffn_w3_s': 8.0,
     'L1_attn_Wg': 8.0,
     'L1_ffn_gate_w': 8.0,
     'L1_ffn_w1': 8.0,
     'L1_ffn_w3': 8.0,
     'L1_ffn_w2': 8.0,
     'L1_ffn_sw1': 8.0,
     'L1_ffn_sw3': 8.0,
     'L1_ffn_sw2': 8.0}
    for name, (base, spread) in spreads.items():
        noise = np.random.default_rng([zlib.crc32(name.encode()), seed]).standard_normal(out[name].shape)
        drawn = base * np.exp(spread * noise) if base else spread * noise
        out[name] = jnp.asarray(drawn.astype(out[name].dtype))
    for name, factor in factors.items():
        out[name] = (out[name] * factor).astype(out[name].dtype)
    return out
```

```python
from contextlib import ExitStack
from math import erf, exp, pi, sqrt

import numpy as np

import concourse.bass as bass
from concourse import mybir

F32 = mybir.dt.float32
BF16 = mybir.dt.bfloat16
ALU = mybir.AluOpType
ACT = mybir.ActivationFunctionType
X = mybir.AxisListType.X

P = 128
B, S, D = 8, 512, 128
TT = S // P
EPS = 1e-5
LOW = -1.0e30
LOWEST = -3.0e38

H0, HD0 = 16, 8
PAIRS = H0 // 2
SCALE0 = 1.0 / HD0 ** 0.5
SETS = 2
HS = H0 // SETS
SUM_COLS = 2 * HD0
V_COLS = 3 * SUM_COLS
Q_PARTS = (0, 0, 1, 1, 0, 2)
K_PARTS = (0, 1, 0, 1, 2, 0)
SLOTS = len(Q_PARTS)
MAX_ROW = SLOTS * HD0
STACK = MAX_ROW + 3
E_SLOTS = 3
HID0 = 512
KC = HID0 // P
H1, HD1, MEM, TOPK = 16, 64, 4, 64
NC = H1 * HD1 // P
J = MEM + S
QK_SCALE = 10.0
R8 = P // H1
SUBS = S // R8
PER_TILE = P // R8
GROUP = 4
RB = 64
PER_BLOCK = RB // R8
ROUNDS = TOPK // 8
TILE_ORDER = (1, 0, 2, 3)
SEQ = [PER_TILE * t + u for t in TILE_ORDER for u in range(PER_TILE)]
PAIR = 2
STEPS = SUBS // PAIR
STEPS_TILE, STEPS_BLOCK = PER_TILE // PAIR, PER_BLOCK // PAIR
SCORES_AT = {1: 0, 0: H1 * (MEM + P * 3), 2: 0, 3: 0}
SCORES_N = H1 * (MEM + P * 3) + H1 * (MEM + P)
MIX_SLOTS, X_SLOTS, E1_SLOTS, A_SLOTS = 4, 6, 4, 4
NARROW_FROM = 12
COUNTS = 3
WINDOW = 16
AIM = TOPK - (WINDOW + 1) / 2
DAMP = 0.5
EXPERTS, HID1, TOP_E = 16, 64, 4
MC = EXPERTS * HID1 // P
PAD_E = 8


def width(n):
    return MEM + GROUP * R8 * (n // GROUP + 1)


def narrow(n):
    return n >= NARROW_FROM


def ahead(s):
    out = [("g", TILE_ORDER[0])] + [("qk", TILE_ORDER[0], g) for g in range(H1)] if s < 0 else []
    for o in range(1, TT):
        t, at = TILE_ORDER[o], STEPS_TILE * (o - 1)
        if s == at + STEPS_TILE // 2:
            out.append(("g", t))
        per, begin = (3, at) if o < TT - 1 else (8, at + STEPS_TILE - 2)
        if s >= begin:
            out += [("qk", t, g) for g in range(H1) if g // per == s - begin]
    return out


def pieces(w):
    return [(0, w)] if w <= 512 else [(0, w // 2), (w // 2, w - w // 2)]


class Ring:

    def __init__(self, keys):
        self.order = {k: n for n, k in enumerate(keys)}
        assert len(self.order) == len(keys)

    def bank(self, key):
        return self.order[key] % 2

    def nth(self, key):
        return self.order[key] + 1


def weight_layout():
    sizes = dict(wq=P, wqs=P, wk=P, wks=P, wv=P, wo0=SETS * P, w1s=KC, w2s=KC, h1s=KC, h2s=KC, w3s=P,
                 Wk=H1 * HD1, Wq=H1 * HD1, Wv=H1 * HD1, Wg=H1 * HD1, bg=NC, hs=P, Wo=NC * P, memk=NC * MEM,
                 pre=P, post=P, gate=EXPERTS)
    const = dict(rope_c=S, rope_s=S, ident=P, heads=P, sums=P, first=SUBS, slope=SUBS, rank=WINDOW)
    return sizes, const


def columns(sizes):
    at, out = 0, {}
    for k, n in sizes.items():
        out[k] = (at, at + n)
        at += n
    return out, at


def network(nc, xT_d, x_d, w_d, c_d, cb_d, memv_d, ffn1_d, ffn2_d, moe_d, parts_d, maxes_d, out_d):
    W_AT, W_N = columns(weight_layout()[0])
    C_AT, C_N = columns(weight_layout()[1])
    F1_AT, F1_N = columns(dict(w1=HID0, w2=HID0, h1=KC * HID0))
    F2_AT, F2_N = columns(dict(h2=KC * HID0, w3=KC * P))
    M_AT, M_N = columns(dict(w1=MC * P + HID1, w3=MC * P + HID1, w2=(MC + 1) * P, spread=MC * P))

    with ExitStack() as ctx:
        def sb(name, shape, dt=F32):
            return ctx.enter_context(nc.sbuf_tensor(name, shape, dt))

        def sem(name):
            s = ctx.enter_context(nc.semaphore(name))
            sems.append(s)
            return s

        sems = []
        wts = sb("wts", [P, W_N])
        cst = sb("cst", [P, C_N])
        CB_N = 3 * P + GROUP * GROUP * R8
        cstb = sb("cstb", [P, CB_N], BF16)
        memv = sb("memv", [MEM, H1 * HD1])
        powers = sb("powers", [P, TT + PAIR])

        def w(name):
            a, b = W_AT[name]
            return wts[:, a:b]

        def c(name):
            a, b = C_AT[name]
            return cst[:, a:b]

        ident = c("ident")
        identb, mask_s, mask_t = cstb[:, 0:P], cstb[:, P:2 * P], cstb[:, 2 * P:3 * P]
        mix_mask = cstb[:, 3 * P:].rearrange("p (v j) -> p v j", v=GROUP)
        tokens = sb("tokens", [P, 3 * S])
        xT = tokens[:, 0:S]
        x0, x1 = (tokens[:, S * z:S * z + S].rearrange("p (t d) -> p t d", t=TT) for z in (1, 2))
        res = sb("res", [P, TT, D])
        x2 = sb("x2", [P, TT, D])
        xe = sb("xe", [P, MEM + S])
        stats = sb("stats", [P, TT, 6])
        mv = sb("mv", [P, TT, 2])
        var = sb("var", [P, TT])
        rstd = sb("rstd", [P, TT])
        xT1 = xT
        x3, xT3, x4 = x0, xT, x1

        kT = sb("kT", [P, NC * J])
        qT = sb("qT", [P, NC * S])
        vx = sb("vx", [P, (TT + 1) * H1 * HD1])
        dots = sb("dots", [P, SCORES_N])
        at2 = sb("at2", [P, TT * H1 * RB])
        tail = sb("tail", [MEM, H1, RB // 2])
        gate = sb("gate", [P, 2, NC, P])
        mixin = sb("mixin", [P, MIX_SLOTS, J])
        squares = sb("squares", [P, 4 * S])
        xs_own = sb("xs", [P, X_SLOTS - 2, J])
        xs = [xs_own[:, i] for i in range(X_SLOTS - 2)] + [tokens[:, J * i:J * i + J] for i in range(2)]
        ex_own = sb("ex", [P, E1_SLOTS - 2, J])
        ex = [ex_own[:, i] for i in range(E1_SLOTS - 2)] + [squares[:, J * i:J * i + J] for i in range(2)]
        left_own = sb("left", [P, J])
        left = [left_own[:, :], squares[:, 2 * J:3 * J]]
        attn = sb("attn", [P, A_SLOTS, J])
        wsc = sb("wsc", [P, A_SLOTS, P])
        og = sb("og", [P, NC, P])
        top = sb("top", [P, 2, PAIR, 8])
        negm = sb("negm", [P, 2, PAIR])
        moments = sb("moments", [P, 2, PAIR, 6])
        meanvar = sb("meanvar", [P, 2, PAIR, 2])
        spread_ = sb("spread_", [P, 2, PAIR])
        slope_ = sb("slope_", [P, 2, PAIR])
        shift = sb("shift", [P, 2, PAIR])
        base = sb("base", [P, 2, PAIR])
        thr = sb("thr", [P, 2, PAIR])
        signs = sb("signs", [P, 2, PAIR])
        best = sb("best", [P, PAIR, WINDOW])
        picked = sb("picked", [P, PAIR, WINDOW])
        bound = sb("bound", [P, PAIR])
        ssum = sb("ssum", [P, 2, PAIR])
        above = sb("above", [P, SUBS])
        off = sb("off", [P, SUBS])
        worst = sb("worst", [P, 1])
        flag_f = sb("flag_f", [1, 1])
        flag = sb("flag", [1, 1], mybir.dt.int32)
        rq = sb("rq", [P, TT, H1])
        sq, nr = (squares[:, 2 * S * z:2 * S * z + 2 * S].rearrange("p (z s) -> p z s", z=2) for z in range(2))
        kT_v = kT[:, :].rearrange("p (c j) -> p c j", c=NC)
        qT_v = qT[:, :].rearrange("p (c s) -> p c s", c=NC)
        vx_v = vx[:, :].rearrange("p (c n) -> p c n", c=TT + 1)
        at_v = at2[:, :].rearrange("p (c h i) -> p c h i", c=TT, h=H1)
        memk_n = sb("memk_n", [P, NC * MEM])
        pre_b = sb("pre_b", [P, P])
        post_b = sb("post_b", [P, P])

        stacks = kT[:, 0:PAIRS * S].bitcast(BF16).rearrange("p (z a s) -> p z a s", z=2, a=PAIRS)
        q_stack, k_stack = stacks[:, 0], stacks[:, 1]
        rope_t = qT[:, 0:2 * S].rearrange("p (z s) -> p z s", z=2)
        rot = qT[:, 2 * S:4 * S].rearrange("p (z s) -> p z s", z=2)
        parts = qT[:, 4 * S:7 * S].bitcast(BF16).rearrange("p (z k s) -> p z k s", z=2, k=3)
        part_t = qT[:, 7 * S:8 * S]
        E_N = S + 3 * P + 2 * P + P
        E_OFF = [0, S, S + 3 * P, S + 5 * P]
        exps = vx[:, 0:E_SLOTS * E_N].rearrange("p (z n) -> p z n", z=E_SLOTS)
        v_pad = dots[:, F1_N:F1_N + TT * PAIRS * V_COLS].rearrange("p (k a n) -> p k a n", k=TT, a=PAIRS)
        sums_in = og[:, :, :].rearrange("p (g c) s -> p g (c s)", g=SETS)
        out0 = gate[:, 0].rearrange("p (g c) s -> p g (c s)", g=SETS)
        row_max = gate[:, 1, 0, 0:TT * H0].rearrange("p (t h) -> p t h", t=TT)
        rec0 = gate[:, 1, 2:6].rearrange("p c s -> p (c s)")
        max_parts = squares[0:HS, 0:SETS * 3 * S // 2].bitcast(BF16).rearrange("h (g k s) -> h g k s", g=SETS, k=3)
        neg_rows = squares[0:HS, SETS * 3 * S // 2:]
        neg_left = rec0[0:HS]

        def f1(name):
            a, b = F1_AT[name]
            return dots[:, a:b]

        def f2(name):
            a, b = F2_AT[name]
            return at2[:, a:b]

        silu0 = kT[:, 0:KC * S].rearrange("p (c s) -> p c s", c=KC)
        hid = qT[:, 0:KC * S].rearrange("p (c s) -> p c s", c=KC)
        gelu1 = kT[:, KC * S:2 * KC * S].rearrange("p (c s) -> p c s", c=KC)
        gelu2 = qT[:, KC * S:2 * KC * S].rearrange("p (c s) -> p c s", c=KC)

        def mw(name):
            a, b = M_AT[name]
            return dots[:, a:b]

        silu1 = qT[:, 0:2 * S].rearrange("p (z s) -> p z s", z=2)
        gated = qT[:, 2 * S:4 * S].rearrange("p (z s) -> p z s", z=2)
        acts = vx[:, 0:(MC + 1) * S].rearrange("p (c s) -> p c s", c=MC + 1)
        comb_T = qT[0:EXPERTS, 4 * S:5 * S]
        logit_m = sb("logit_m", [P, TT])
        logits = kT[:, 0:TT * EXPERTS].rearrange("p (t e) -> p t e", t=TT)
        comb = kT[:, S:S + TT * EXPERTS].rearrange("p (t e) -> p t e", t=TT)
        top_e = kT[:, 2 * S:2 * S + TT * 8].rearrange("p (t e) -> p t e", t=TT)
        rest_e = kT[:, 3 * S:3 * S + TT * (EXPERTS + PAD_E)].rearrange("p (t e) -> p t e", t=TT)
        gates_e = sb("gates_e", [P, TT, EXPERTS + PAD_E])
        sum_e = sb("sum_e", [P, TT])
        rec_e = sb("rec_e", [P, TT])

        banks_a = [ctx.enter_context(nc.psum_tensor(f"pa{i}", [P, 512], F32)) for i in range(2)]
        banks_o = [ctx.enter_context(nc.psum_tensor(f"po{i}", [P, 512], F32)) for i in range(2)]
        banks_m = [ctx.enter_context(nc.psum_tensor(f"pm{i}", [P, 512], F32)) for i in range(2)]
        banks_t = [ctx.enter_context(nc.psum_tensor(f"pt{i}", [P, 512], F32)) for i in range(2)]
        def scores_keys():
            a = []
            for s in range(-1, STEPS + 2):
                for what in ahead(s):
                    if what[0] == "g":
                        a += [what + (z,) for z in range(2)]
                    else:
                        a += [what + (z,) for z in range(len(pieces(MEM + P * (what[1] + 1))))]
                if s >= 2 and has_tail(s - 2):
                    a.append(("tail", s - 2))
            o = [x for r in range(S // RB) for x in [("av", r)] + ([("wo", r // 2)] if r % 2 else [])]
            m = [("mix", i, z) for i in range(SUBS) for z in range(len(pieces(width(SEQ[i]))))]
            return a, o, m, [("post", i) for i in range(SUBS)]

        def has_tail(s):
            return SEQ[PAIR * s] % PER_TILE >= PER_TILE - GROUP

        KEYS = scores_keys()
        FRONT_A = (["v"] + [("st", h, k) for h in range(H0) for k in range(TT)] + ["x1T"]
                   + [("f1", k) for k in range(KC)] + [("h1", k) for k in range(KC)] + [("h2", k) for k in range(KC)] + ["x2T"]
                   + [x for k in range(NC + 1) for x in ([("k", k)] if k < NC else []) + ([("kn", k - 1)] if k else [])]
                   + [("vx", k, z) for k in range(TT + 1) for z in range(2)] + [("q", k) for k in range(NC)] + ["qn"])
        S_FIRST = [(i, h) for i in range(TT) for h in range(HS)]
        S_SECOND = [(i, h) for i in range(TT) for h in range(HS, H0)]
        FRONT_O = (["rq", "rqs", "rk", "rks"] + [("s",) + k for k in S_FIRST] + [("mT", 0)] + [("s",) + k for k in S_SECOND] + [("mT", 1)]
                   + [("den", 0), ("den", 1), "y0"]
                   + [("f2", k) for k in range(KC)] + ["y1"])
        EXPERTS_A = ["x3T"] + [("m1", k) for k in range(MC + 1)]
        EXPERTS_O = ["lg", "cT"] + [x for k in range(MC + 1) for x in [("m3", k)] + ([("cb", k)] if k < MC else [])] + ["y3"]
        RINGS = [Ring(FRONT_A + KEYS[0]), Ring(FRONT_O + KEYS[1] + ["bad"]), Ring(KEYS[2]), Ring(KEYS[3])]
        RINGS_AGAIN = [Ring(k) for k in KEYS]
        RINGS_EXPERTS = [Ring(EXPERTS_A), Ring(EXPERTS_O)]

        w_in = sem("w_in")
        init_done = sem("init_done")
        pre_done = sem("pre_done")
        x_in = sem("x_in")
        a_full, a_free = sem("a_full"), sem("a_free")
        o_full, o_free = sem("o_full"), sem("o_free")
        m_full, m_free = sem("m_full"), sem("m_free")
        t_full, t_free = sem("t_full"), sem("t_free")
        v_chain = sem("v_chain")
        g_chain = sem("g_chain")
        rot_done = sem("rot_done")
        parts_done = sem("parts_done")
        parts_out = sem("parts_out")
        stack_in = sem("stack_in")
        rows_done = sem("rows_done")
        rows_out = sem("rows_out")
        rows_in = sem("rows_in")
        av0_done = sem("av0_done")
        sums_done = sem("sums_done")
        out0_done = sem("out0_done")
        var_done = sem("var_done")
        rstd_done = sem("rstd_done")
        x1_done, x2_done, x3_done, x4_done = (sem(f"x{i}_done") for i in range(1, 5))
        ffn_in = sem("ffn_in")
        moe_in = sem("moe_in")
        k_sq = sem("k_sq")
        k_done = sem("k_done")
        q_sq = sem("q_sq")
        q_summed = sem("q_summed")
        rq_done = sem("rq_done")
        mix_in = [sem(f"mix_in{i}") for i in range(MIX_SLOTS)]
        zero_done = sem("zero_done")
        negm_done = sem("negm_done")
        moments_done = sem("moments_done")
        thr_ready = sem("thr_ready")
        worst_done = sem("worst_done")
        counted = sem("counted")
        ex_done = sem("ex_done")
        attn_done = sem("attn_done")
        og_done = sem("og_done")
        ex_e_done = sem("ex_e_done")
        comb_done = sem("comb_done")
        y_out = sem("y_out")

        class Chain:

            def __init__(self, eng, s):
                self.eng, self.sem, self.n = eng, s, 0

            def mark(self, ins):
                self.n += 1
                ins.then_inc(self.sem, 1)
                return self.n

            def after(self, n):
                self.eng.wait_ge(self.sem, n)

            def link(self, ins):
                self.after(self.mark(ins))

        with nc.Block() as block:
            @block.sync
            def _(sp):
                sp.dma_start(wts[:, :], w_d).then_inc(w_in, 16)
                sp.dma_start(cst[:, :], c_d).then_inc(w_in, 16)
                sp.dma_start(dots[:, 0:CB_N + 2 * P], cb_d).then_inc(w_in, 16)
                sp.dma_start(memv[:, :], memv_d).then_inc(w_in, 16)

            @block.gpsimd
            def _(pool):
                nc.gpsimd.memset(xe[:, 0:MEM], 0.0)
                nc.gpsimd.memset(powers[:, 0:TT], -0.5)
                nc.gpsimd.memset(powers[:, TT:], 0.5)
                nc.gpsimd.memset(gates_e[:, :, :], -1.0).then_inc(init_done, 1)
                pool.wait_ge(w_in, 64)
                nc.gpsimd.tensor_tensor(sq[:, 0, 0:NC * MEM], w("memk"), w("memk"), ALU.mult).then_inc(pre_done, 1)

            @block.tensor
            def _(pe):
                pe.wait_ge(w_in, 64)
                pe.wait_ge(pre_done, 1)
                nc.tensor.matmul(banks_a[0][:, 0:NC * MEM], c("heads"), sq[:, 0, 0:NC * MEM], start=True,
                                 stop=True).then_inc(a_full, 1)

            @block.scalar
            def _(act):
                act.wait_ge(a_full, 1)
                nc.scalar.activation(nr[:, 0, 0:NC * MEM], banks_a[0][:, 0:NC * MEM], ACT.Sqrt).then_inc(a_free, 1)

            @block.vector
            def _(dve):
                chain = Chain(dve, v_chain)
                dve.wait_ge(w_in, 64)
                nc.vector.tensor_copy(cstb[:, :], dots[:, 0:CB_N])
                nc.vector.tensor_tensor(pre_b[:, :], w("pre"), dots[:, CB_N:CB_N + P], ALU.mult)
                chain.link(nc.vector.tensor_tensor(post_b[:, :], w("post"), dots[:, CB_N + P:CB_N + 2 * P], ALU.mult))
                nc.vector.tensor_tensor(post_b[:, :], post_b[:, :], w("hs"), ALU.mult)
                dve.wait_ge(a_free, 1)
                n = nr[:, 0, 0:NC * MEM]
                chain.link(nc.vector.tensor_scalar(n, n, 1e-12, None, ALU.max))
                chain.link(nc.vector.reciprocal(n, n))
                chain.link(nc.vector.tensor_tensor(memk_n[:, :], w("memk"), n, ALU.mult))

        def clear_semaphores():
            for s in sems:
                nc.sync.sem_clear(s)
            nc.all_engine_barrier()

        clear_semaphores()

        def empty_banks(pe, A, O):
            def a_bank(key):
                if A.nth(key) > 2:
                    pe.wait_ge(a_free, A.nth(key) - 2)
                return banks_a[A.bank(key)]

            def o_bank(key):
                if O.nth(key) > 2:
                    pe.wait_ge(o_free, O.nth(key) - 2)
                return banks_o[O.bank(key)]

            return a_bank, o_bank

        def turned(bank, src):
            for t in range(TT):
                ins = nc.tensor.transpose(bank[:, P * t:P * t + P], src[:, t, :], ident)
            ins.then_inc(a_full, 1)

        def inverse_root(pool, k):
            pool.wait_ge(var_done, k + 1)
            nc.gpsimd.tensor_tensor(rstd[:, :], var[:, :], powers[:, 0:TT], ALU.pow).then_inc(rstd_done, 1)

        def norm(dve, chain, k, dst, done):
            for t in range(TT):
                ins = nc.vector.bn_stats(stats[:, t], res[:, t])
            chain.link(ins)
            for t in range(TT):
                ins = nc.vector.bn_aggr(mv[:, t], stats[:, t])
            chain.link(ins)
            nc.vector.tensor_scalar(var[:, :], mv[:, :, 1], EPS, None, ALU.add).then_inc(var_done, 1)
            dve.wait_ge(rstd_done, k + 1)
            for t in range(TT):
                ins = nc.vector.tensor_scalar(dst[:, t], res[:, t], mv[:, t, 0:1], rstd[:, t:t + 1], ALU.subtract, ALU.mult)
            ins.then_inc(done, 1)
            dve.wait_ge(done, 1)

        def rows(bank):
            return bank[:, :].rearrange("p (t d) -> p t d", t=TT)

        def pair_of(s):
            return [(z, PAIR * s + z, SEQ[PAIR * s + z]) for z in range(PAIR)]

        def last_piece(n):
            return len(pieces(width(n))) - 1

        SEARCHED = [s for s in range(STEPS) if narrow(SEQ[PAIR * s])]

        def searched(s, full):
            return not full and s in SEARCHED

        def scores_sync(sp, R):
            A, O, M, T = R
            for m, n in enumerate(SEQ):
                t, u = divmod(n, PER_TILE)
                wt, wn = MEM + P * (t + 1), width(n)
                if u == 0:
                    sp.wait_ge(a_free, A.nth(("qk", t, H1 - 1, len(pieces(wt)) - 1)))
                if m >= MIX_SLOTS:
                    sp.wait_ge(m_full, M.nth(("mix", m - MIX_SLOTS, last_piece(SEQ[m - MIX_SLOTS]))))
                tile = dots[R8 * u:R8 * u + R8, SCORES_AT[t]:SCORES_AT[t] + H1 * wt].rearrange("p (g j) -> p g j", g=H1)
                sp.dma_start(mixin[:, m % MIX_SLOTS, 0:wn], tile[:, :, 0:wn]).then_inc(mix_in[m % MIX_SLOTS], 16)

        def scores_gpsimd(pool, chain, full):
            nc.gpsimd.memset(attn[:, :, :], 0.0).then_inc(zero_done, 1)
            if full:
                return
            for q, s in enumerate(SEARCHED):
                p, n = s % 2, SEQ[PAIR * s]
                ready = (COUNTS + 1) * q
                pool.wait_ge(moments_done, q + 1)
                chain.link(nc.gpsimd.tensor_tensor(spread_[:, p], meanvar[:, p, :, 1], powers[:, TT:TT + PAIR], ALU.pow))
                nc.gpsimd.tensor_tensor(slope_[:, p], spread_[:, p], c("slope")[:, n:n + PAIR], ALU.mult)
                chain.link(nc.gpsimd.tensor_tensor(shift[:, p], spread_[:, p], c("first")[:, n:n + PAIR], ALU.mult))
                nc.gpsimd.tensor_tensor(thr[:, p], meanvar[:, p, :, 0], shift[:, p], ALU.add).then_inc(thr_ready, 1)
                chain.link(nc.gpsimd.tensor_scalar(base[:, p], slope_[:, p], 2 * AIM - width(n), None, ALU.mult))
                for r in range(COUNTS):
                    pool.wait_ge(thr_ready, ready + r + 1)
                    chain.link(nc.gpsimd.tensor_tensor(shift[:, p], thr[:, p], base[:, p], ALU.add))
                    pool.wait_ge(counted, COUNTS * q + r + 1)
                    chain.link(nc.gpsimd.tensor_tensor(spread_[:, p], signs[:, p], slope_[:, p], ALU.mult))
                    nc.gpsimd.tensor_tensor(thr[:, p], shift[:, p], spread_[:, p], ALU.add).then_inc(thr_ready, 1)

        def scores_tensor(pe, R):
            A, O, M, T = R
            a_bank, o_bank = empty_banks(pe, A, O)

            def gates_and_heads(s):
                for what in ahead(s):
                    t = what[1]
                    if what[0] == "g":
                        rows = slice(MEM + P * t, MEM + P * t + P)
                        for z in range(2):
                            bank = a_bank(("g", t, z))
                            for k in range(NC // 2):
                                kk = NC // 2 * z + k
                                ins = nc.tensor.matmul(bank[:, P * k:P * k + P], w("Wg")[:, P * kk:P * kk + P], xe[:, rows],
                                                       start=True, stop=True)
                            ins.then_inc(a_full, 1)
                    else:
                        g = what[2]
                        at = HD1 * (g % 2)
                        for z, (j0, jn) in enumerate(pieces(MEM + P * (t + 1))):
                            nc.tensor.matmul(a_bank(("qk", t, g, z))[:, 0:jn], qT_v[at:at + HD1, g // 2, P * t:P * t + P],
                                             kT_v[at:at + HD1, g // 2, j0:j0 + jn], start=True, stop=True).then_inc(a_full, 1)

            def mix(m, n):
                pe.wait_ge(mix_in[m % MIX_SLOTS], 16 * (m // MIX_SLOTS + 1))
                for z, (j0, jn) in enumerate(pieces(width(n))):
                    last = z == last_piece(n)
                    if M.nth(("mix", m, z)) > 2:
                        pe.wait_ge(m_free, M.nth(("mix", m, z)) - 2)
                    bank = banks_m[M.bank(("mix", m, z))]
                    ins = nc.tensor.matmul(bank[:, 0:jn], pre_b[:, :], mixin[:, m % MIX_SLOTS, j0:j0 + jn], start=True, stop=not last)
                    if last:
                        ins = nc.tensor.matmul(bank[:, jn - GROUP * R8:jn], identb, mix_mask[:, n % GROUP], start=False, stop=True)
                    ins.then_inc(m_full, 1)

            def post(s):
                for z, m, n in pair_of(s):
                    pe.wait_ge(attn_done, m + 1)
                    if T.nth(("post", m)) > 2:
                        pe.wait_ge(t_free, T.nth(("post", m)) - 2)
                    bank = banks_t[T.bank(("post", m))]
                    for k in range(n // PER_TILE + 1):
                        ins = nc.tensor.matmul(bank[:, P * k:P * k + P], attn[:, m % A_SLOTS, P * k:P * k + P], wsc[:, m % A_SLOTS],
                                               start=True, stop=True)
                    ins.then_inc(t_full, 1)
                if has_tail(s):
                    bank = a_bank(("tail", s))
                    for z, m, n in pair_of(s):
                        j0 = P * (n // PER_TILE + 1)
                        ins = nc.tensor.matmul(bank[0:MEM, P * z:P * z + P], attn[:, m % A_SLOTS, j0:j0 + MEM], wsc[:, m % A_SLOTS],
                                               start=True, stop=True)
                    ins.then_inc(a_full, 1)

            def values(r):
                t, odd = divmod(SEQ[PER_BLOCK * r] // PER_BLOCK, 2)
                pe.wait_ge(t_free, T.nth(("post", PER_BLOCK * r + PER_BLOCK - 1)))
                if odd:
                    pe.wait_ge(a_free, A.nth(("tail", STEPS_BLOCK * (r + 1) - 1)))
                bank = o_bank(("av", r))
                for h in range(H1):
                    at, col = HD1 * (h % 2), RB * (h // 2)
                    for k in range(t + 1):
                        ins = nc.tensor.matmul(bank[at:at + HD1, col:col + RB], vx_v[:, k, HD1 * h:HD1 * h + HD1], at_v[:, k, h, :],
                                               start=k == 0, stop=k == t and not odd)
                    if odd:
                        ins = nc.tensor.matmul(bank[at:at + HD1, col + RB // 2:col + RB], vx_v[0:MEM, t + 1, HD1 * h:HD1 * h + HD1],
                                               tail[:, h, :], start=False, stop=True)
                ins.then_inc(o_full, 1)

            def project(o):
                pe.wait_ge(o_free, O.nth(("av", 2 * o + 1)))
                bank = o_bank(("wo", o))
                for k in range(NC):
                    ins = nc.tensor.matmul(bank[:, 0:P], og[:, k, :], w("Wo")[:, P * k:P * k + P], start=k == 0, stop=k == NC - 1)
                ins.then_inc(o_full, 1)

            gates_and_heads(-1)
            for s in range(STEPS + STEPS_BLOCK + 1):
                if s < STEPS:
                    for z, m, n in pair_of(s):
                        mix(m, n)
                gates_and_heads(s)
                if s >= STEPS_BLOCK + 2 and (s - 2) % STEPS_BLOCK == 0:
                    values((s - 2) // STEPS_BLOCK - 1)
                if 2 <= s < STEPS + 2:
                    post(s - 2)
                if s > STEPS_TILE and (s - 4) % STEPS_TILE == 0:
                    project((s - 4) // STEPS_TILE - 1)

        def scores_scalar(act, R, full):
            A, O, M, T = R

            def gates(t):
                o = TILE_ORDER.index(t)
                if o >= 2:
                    act.wait_ge(o_free, O.nth(("av", 2 * o - 3)))
                for z in range(2):
                    act.wait_ge(a_full, A.nth(("g", t, z)))
                    bank = banks_a[A.bank(("g", t, z))]
                    for k in range(NC // 2):
                        kk = NC // 2 * z + k
                        ins = nc.scalar.activation(gate[:, o % 2, kk], bank[:, P * k:P * k + P], ACT.Sigmoid, bias=w("bg")[:, kk:kk + 1])
                    ins.then_inc(a_free, 1)

            def head(t, g):
                o = TILE_ORDER.index(t)
                wt = MEM + P * (t + 1)
                if g == 0 and o >= 2:
                    through = o - 1 if o < TT - 1 else o
                    for s in mix_in:
                        act.wait_ge(s, 16 * through * PER_TILE // MIX_SLOTS)
                for z, (j0, jn) in enumerate(pieces(wt)):
                    key = ("qk", t, g, z)
                    act.wait_ge(a_full, A.nth(key))
                    at = SCORES_AT[t] + g * wt + j0
                    nc.scalar.activation(dots[:, at:at + jn], banks_a[A.bank(key)][:, 0:jn], ACT.Copy,
                                         scale=rq[:, t, g:g + 1]).then_inc(a_free, 1)

            def gates_and_heads(s):
                for what in ahead(s):
                    if what[0] == "g":
                        gates(what[1])
                    else:
                        head(what[1], what[2])

            def mixed(s):
                if PAIR * s >= X_SLOTS:
                    act.wait_ge(attn_done, PAIR * s + PAIR - X_SLOTS)
                for y, m, n in pair_of(s):
                    for z, (j0, jn) in enumerate(pieces(width(n))):
                        act.wait_ge(m_full, M.nth(("mix", m, z)))
                        nc.scalar.copy(xs[m % X_SLOTS][:, j0:j0 + jn], banks_m[M.bank(("mix", m, z))][:, 0:jn]).then_inc(m_free, 1)

            def count(s, r):
                q = SEARCHED.index(s)
                act.wait_ge(thr_ready, (COUNTS + 1) * q + r + 1)
                if r == 0 and PAIR * s >= E1_SLOTS:
                    act.wait_ge(attn_done, PAIR * s + PAIR - E1_SLOTS)
                for z, m, n in pair_of(s):
                    ins = nc.scalar.activation(ex[m % E1_SLOTS][:, 0:width(n)], xs[m % X_SLOTS][:, 0:width(n)], ACT.Sign, scale=-1.0,
                                               bias=thr[:, s % 2, z:z + 1], accum_out=signs[:, s % 2, z:z + 1])
                ins.then_inc(counted, 1)

            def exponentials(s):
                act.wait_ge(negm_done, s + 1)
                if searched(s, full):
                    act.wait_ge(thr_ready, (COUNTS + 1) * (SEARCHED.index(s) + 1))
                elif PAIR * s >= E1_SLOTS:
                    act.wait_ge(attn_done, PAIR * s + PAIR - E1_SLOTS)
                for z, m, n in pair_of(s):
                    nc.scalar.activation(ex[m % E1_SLOTS][:, 0:width(n)], xs[m % X_SLOTS][:, 0:width(n)], ACT.Exp,
                                         bias=negm[:, s % 2, z:z + 1]).then_inc(ex_done, 1)

            def posted(s):
                r = s // STEPS_BLOCK
                if s % STEPS_BLOCK == 0 and r:
                    act.wait_ge(o_full, O.nth(("av", r - 1)))
                for z, m, n in pair_of(s):
                    t, u = n // PER_TILE, n % PER_BLOCK
                    act.wait_ge(t_full, T.nth(("post", m)))
                    bank = banks_t[T.bank(("post", m))]
                    nc.scalar.copy(at_v[:, 0:t + 1, :, R8 * u:R8 * u + R8],
                                   bank[:, 0:P * (t + 1)].rearrange("p (k h i) -> p k h i", k=t + 1, h=H1)).then_inc(t_free, 1)
                if has_tail(s):
                    act.wait_ge(a_full, A.nth(("tail", s)))
                    bank = banks_a[A.bank(("tail", s))]
                    v = R8 * (SEQ[PAIR * s] % GROUP)
                    nc.scalar.copy(tail[:, :, v:v + PAIR * R8].rearrange("p h (z i) -> p z h i", z=PAIR),
                                   bank[0:MEM, 0:PAIR * P].rearrange("p (z h i) -> p z h i", z=PAIR, h=H1)).then_inc(a_free, 1)

            gates_and_heads(-1)
            for s in range(STEPS + 3):
                search = 1 <= s <= STEPS and searched(s - 1, full)
                if search:
                    count(s - 1, 0)
                if s < STEPS:
                    mixed(s)
                if search:
                    count(s - 1, 1)
                if s >= 3:
                    posted(s - 3)
                if search:
                    count(s - 1, 2)
                gates_and_heads(s)
                if 1 <= s <= STEPS:
                    exponentials(s - 1)

        def scores_vector(dve, chain, R, full):
            A, O, M, T = R

            def maxima(s):
                p, search = s % 2, searched(s, full)
                for z, m, n in pair_of(s):
                    dve.wait_ge(m_free, M.nth(("mix", m, last_piece(n))))
                    found = chain.mark(nc.vector.max(out=top[:, p, z], in_=xs[m % X_SLOTS][:, 0:width(n)]))
                    if search:
                        seen = chain.mark(nc.vector.bn_stats(moments[:, p, z], xs[m % X_SLOTS][:, 0:width(n) - GROUP * R8]))
                chain.after(found)
                nc.vector.tensor_scalar(negm[:, p], top[:, p, :, 0], -1.0, None, ALU.mult).then_inc(negm_done, 1)
                if search:
                    chain.after(seen)
                    for z in range(PAIR):
                        ins = nc.vector.bn_aggr(meanvar[:, p, z], moments[:, p, z])
                    ins.then_inc(moments_done, 1)

            def in_turn(s):
                wn = width(SEQ[PAIR * s])
                src = [xs[m % X_SLOTS][:, 0:wn] for z, m, n in pair_of(s)]
                t8 = [top[:, s % 2, z] for z in range(PAIR)]
                done = [None] * PAIR
                for _ in range(ROUNDS - 1):
                    for z in range(PAIR):
                        if done[z]:
                            chain.after(done[z])
                        done[z] = chain.mark(nc.vector.match_replace(out=left[z][:, 0:wn], in_to_replace=t8[z], in_values=src[z], imm_value=LOWEST))
                        src[z], t8[z] = left[z][:, 0:wn], best[:, z, 0:8]
                    for z in range(PAIR):
                        chain.after(done[z])
                        done[z] = chain.mark(nc.vector.max(out=t8[z], in_=src[z]))
                chain.after(done[-1])
                return [best[:, z, 7:8] for z in range(PAIR)]

            def near_threshold(s):
                wn = width(SEQ[PAIR * s])
                dve.wait_ge(thr_ready, (COUNTS + 1) * (SEARCHED.index(s) + 1))
                done = [None] * PAIR
                for z, m, n in pair_of(s):
                    done[z] = chain.mark(nc.vector.tensor_scalar(left[z][:, 0:wn], xs[m % X_SLOTS][:, 0:wn], thr[:, s % 2, z:z + 1], None,
                                                                 ALU.is_gt, ALU.add, accum_out=above[:, n:n + 1]))
                for z, m, n in pair_of(s):
                    chain.after(done[z])
                    done[z] = chain.mark(nc.vector.scalar_tensor_tensor(out=left[z][:, 0:wn], in0=left[z][:, 0:wn], scalar=LOWEST,
                                                                        in1=xs[m % X_SLOTS][:, 0:wn], op0=ALU.mult, op1=ALU.add))
                for k in range(WINDOW // 8):
                    for z in range(PAIR):
                        chain.after(done[z])
                        done[z] = chain.mark(nc.vector.max(out=best[:, z, 8 * k:8 * k + 8], in_=left[z][:, 0:wn]))
                    if k < WINDOW // 8 - 1:
                        for z in range(PAIR):
                            chain.after(done[z])
                            done[z] = chain.mark(nc.vector.match_replace(out=left[z][:, 0:wn], in_to_replace=best[:, z, 8 * k:8 * k + 8],
                                                                         in_values=left[z][:, 0:wn], imm_value=LOWEST))
                for z, m, n in pair_of(s):
                    chain.after(done[z])
                    done[z] = chain.mark(nc.vector.scalar_tensor_tensor(out=picked[:, z], in0=c("rank"), scalar=above[:, n:n + 1], in1=best[:, z],
                                                                        op0=ALU.is_equal, op1=ALU.mult, accum_out=bound[:, z:z + 1]))
                chain.after(done[-1])
                return [bound[:, z:z + 1] for z in range(PAIR)]

            def select(s):
                if searched(s, full):
                    bounds = near_threshold(s)
                else:
                    bounds = in_turn(s) if width(SEQ[PAIR * s]) >= TOPK else [LOWEST] * PAIR
                for z, m, n in pair_of(s):
                    wn = width(n)
                    dve.wait_ge(ex_done, m + 1)
                    if m >= A_SLOTS:
                        before = m - A_SLOTS
                        dve.wait_ge(t_full, T.nth(("post", before)))
                        if has_tail(before // PAIR):
                            dve.wait_ge(a_full, A.nth(("tail", before // PAIR)))
                    if wn < P:
                        nc.vector.memset(attn[:, m % A_SLOTS, wn:P + MEM], 0.0)
                    done = chain.mark(nc.vector.scalar_tensor_tensor(out=attn[:, m % A_SLOTS, 0:wn], in0=xs[m % X_SLOTS][:, 0:wn], scalar=bounds[z],
                                                                     in1=ex[m % E1_SLOTS][:, 0:wn], op0=ALU.is_ge, op1=ALU.mult,
                                                                     accum_out=ssum[:, 0, z:z + 1]))
                chain.after(done)
                if searched(s, full):
                    chain.link(nc.vector.tensor_scalar(ssum[:, 0], ssum[:, 0], 0.5, None, ALU.max))
                chain.link(nc.vector.reciprocal(ssum[:, 1], ssum[:, 0]))
                for z, m, n in pair_of(s):
                    nc.vector.tensor_scalar(wsc[:, m % A_SLOTS], post_b[:, :], ssum[:, 1, z:z + 1], None, ALU.mult).then_inc(attn_done, 1)

            def gated_rows(r):
                o, odd = divmod(r, 2)
                dve.wait_ge(o_full, O.nth(("av", r)))
                dve.wait_ge(a_free, A.nth(("g", TILE_ORDER[o], 1)))
                bank = banks_o[O.bank(("av", r))]
                nc.vector.tensor_tensor(og[:, :, RB * odd:RB * odd + RB], bank[:, :].rearrange("p (c i) -> p c i", c=NC),
                                        gate[:, o % 2, :, RB * odd:RB * odd + RB], ALU.mult).then_inc(o_free, 1)

            def residual(o):
                t = TILE_ORDER[o]
                dve.wait_ge(o_full, O.nth(("wo", o)))
                nc.vector.tensor_tensor(res[:, t], banks_o[O.bank(("wo", o))][:, 0:P], x2[:, t], ALU.add).then_inc(o_free, 1)

            dve.wait_ge(zero_done, 1)
            for s in range(STEPS + STEPS_BLOCK + 2):
                if s < STEPS:
                    maxima(s)
                if 1 <= s <= STEPS:
                    select(s - 1)
                if s >= STEPS_BLOCK + 3 and (s - 3) % STEPS_BLOCK == 0:
                    gated_rows((s - 3) // STEPS_BLOCK - 1)
                if s > STEPS_TILE and (s - 5) % STEPS_TILE == 0:
                    residual((s - 5) // STEPS_TILE - 1)

        def front(b, block):
            A, O, M, T = RINGS

            @block.sync
            def _(sp):
                sp.dma_start(xT, xT_d[b]).then_inc(x_in, 16)
                sp.dma_start(x0[:, :, :], x_d[b].rearrange("p (t d) -> p t d", t=TT)).then_inc(x_in, 16)
                sp.dma_start(dots[:, 0:F1_N], ffn1_d).then_inc(ffn_in, 16)
                sp.dma_start(at2[:, 0:F2_N], ffn2_d).then_inc(ffn_in, 16)
                for z, (stack, slots) in enumerate(((q_stack, Q_PARTS), (k_stack, K_PARTS))):
                    sp.wait_ge(parts_done, z + 1)
                    sp.dma_start(parts_d[z], parts[:, z].rearrange("p k s -> p (k s)")).then_inc(parts_out, 16)
                    sp.wait_ge(parts_out, 16 * (z + 1))
                    for slot, part in enumerate(slots):
                        heads = parts_d[z][:, part * S:(part + 1) * S].rearrange("(a h d) s -> h d a s", h=2, d=HD0)
                        for hp in range(2):
                            at = RB * hp + HD0 * slot
                            sp.dma_start(stack[at:at + HD0], heads[hp]).then_inc(stack_in, 16)
                for g in range(SETS):
                    sp.wait_ge(rows_done, g + 1)
                    sp.dma_start(maxes_d[g], max_parts[:, g].rearrange("h k s -> h (k s)")).then_inc(rows_out, 16)
                    sp.wait_ge(rows_out, 16 * (g + 1))
                    rows = maxes_d[g].rearrange("(a h) (k s) -> h k a s", h=2, k=3)
                    for hp in range(2):
                        at = RB * hp + MAX_ROW
                        sp.dma_start(q_stack[at:at + 3, HS // 2 * g:HS // 2 * (g + 1)], rows[hp]).then_inc(rows_in, 16)
                scores_sync(sp, RINGS)

            @block.gpsimd
            def _(pool):
                chain = Chain(pool, g_chain)

                nc.gpsimd.memset(v_pad[:, :, :, SUM_COLS:2 * SUM_COLS], 0.0)
                nc.gpsimd.memset(v_pad[:, :, :, HD0:SUM_COLS], 1.0)
                nc.gpsimd.memset(v_pad[:, :, :, 2 * SUM_COLS + HD0:V_COLS], 1.0)
                nc.gpsimd.memset(k_stack, 1.0).then_inc(init_done, 1)
                for z in range(2):
                    pool.wait_ge(rot_done, z + 1)
                    chain.link(nc.gpsimd.tensor_copy(parts[:, z, 0], rot[:, z]))
                    chain.link(nc.gpsimd.tensor_tensor(part_t, rot[:, z], parts[:, z, 0], ALU.subtract))
                    chain.link(nc.gpsimd.tensor_copy(parts[:, z, 1], part_t))
                    chain.link(nc.gpsimd.tensor_tensor(part_t, part_t, parts[:, z, 1], ALU.subtract))
                    nc.gpsimd.tensor_copy(parts[:, z, 2], part_t).then_inc(parts_done, 1)
                inverse_root(pool, 0)
                inverse_root(pool, 1)
                for k in range(NC):
                    pool.wait_ge(a_free, A.nth(("k", k)))
                    if k >= 2:
                        pool.wait_ge(a_full, A.nth(("kn", k - 2)))
                    kc = kT_v[:, k, MEM:J]
                    nc.gpsimd.tensor_tensor(sq[:, k % 2], kc, kc, ALU.mult).then_inc(k_sq, 1)
                for k in range(NC):
                    pool.wait_ge(a_free, A.nth(("q", k)))
                    qc = qT_v[:, k, :]
                    if k == 0:
                        pool.wait_ge(a_full, A.nth(("kn", NC - 1)))
                    if k >= 2:
                        pool.wait_ge(q_summed, k - 1)
                    nc.gpsimd.tensor_tensor(sq[:, k % 2], qc, qc, ALU.mult).then_inc(q_sq, 1)
                scores_gpsimd(pool, chain, False)

            @block.tensor
            def _(pe):
                a_bank, o_bank = empty_banks(pe, A, O)

                pe.wait_ge(x_in, 32)
                for key, name in (("rq", "wq"), ("rqs", "wqs"), ("rk", "wk"), ("rks", "wks")):
                    nc.tensor.matmul(o_bank(key)[:, :], w(name), xT[:, :], start=True, stop=True).then_inc(o_full, 1)
                bank = a_bank("v")
                for t in range(TT):
                    ins = nc.tensor.matmul(bank[:, P * t:P * t + P], xT[:, P * t:P * t + P], w("wv"), start=True, stop=True)
                ins.then_inc(a_full, 1)
                pe.wait_ge(stack_in, 16 * 4 * SLOTS)
                def rows_scores(i, h):
                    bank = o_bank(("s", i, h))
                    at = RB * (h % 2)
                    nc.tensor.matmul(bank[:, 0:P * (i + 1)], q_stack[at:at + MAX_ROW, h // 2, P * i:P * i + P],
                                     k_stack[at:at + MAX_ROW, h // 2, 0:P * (i + 1)], start=True, stop=False)
                    nc.tensor.matmul(bank[:, P * i:P * i + P], identb, mask_s, start=False, stop=True).then_inc(o_full, 1)

                def maxima(g):
                    pe.wait_ge(o_free, O.nth(("s", TT - 1, HS * (g + 1) - 1)))
                    bank = o_bank(("mT", g))
                    for i in range(TT):
                        ins = nc.tensor.transpose(bank[0:HS, P * i:P * i + P], row_max[:, i, HS * g:HS * (g + 1)], ident)
                    ins.then_inc(o_full, 1)

                def columns_scores(h):
                    at = RB * (h % 2)
                    for k in range(TT):
                        bank = a_bank(("st", h, k))
                        nc.tensor.matmul(bank[:, 0:S - P * k], k_stack[at:at + STACK, h // 2, P * k:P * k + P],
                                         q_stack[at:at + STACK, h // 2, P * k:S], start=True, stop=False)
                        nc.tensor.matmul(bank[:, 0:P], identb, mask_t, start=False, stop=True).then_inc(a_full, 1)

                def values0(h):
                    pe.wait_ge(a_free, A.nth(("st", h, TT - 1)))
                    a, odd = divmod(h, 2)
                    at = 2 * SUM_COLS * (a % (HS // 2))
                    for k in range(TT):
                        ins = nc.tensor.matmul(banks_t[h // HS][at:at + 2 * SUM_COLS, P * k:S],
                                               v_pad[:, k, a, SUM_COLS * odd:SUM_COLS * odd + 2 * SUM_COLS],
                                               exps[:, h % E_SLOTS, E_OFF[k]:E_OFF[k] + S - P * k],
                                               start=not odd and k == 0, stop=odd == 1 and k == TT - 1)
                    ins.then_inc(av0_done, 1)

                def sums_beside(g):
                    pe.wait_ge(sums_done, g + 1)
                    nc.tensor.matmul(o_bank(("den", g))[:, :], c("sums"), sums_in[:, g], start=True, stop=True).then_inc(o_full, 1)

                for i, h in S_FIRST:
                    rows_scores(i, h)
                maxima(0)
                half = len(S_SECOND) // 2
                for i, h in S_SECOND[:half]:
                    rows_scores(i, h)
                pe.wait_ge(init_done, 1)
                for h in range(H0 + 1):
                    if h < H0:
                        if h % HS == 0:
                            pe.wait_ge(rows_in, 32 * (h // HS + 1))
                        columns_scores(h)
                    if h < HS // 2:
                        for i, h2 in S_SECOND[half + 4 * h:half + 4 * h + 4]:
                            rows_scores(i, h2)
                    if h == HS // 2:
                        maxima(1)
                    if h:
                        values0(h - 1)
                    if h == HS + 1:
                        sums_beside(0)
                sums_beside(1)
                pe.wait_ge(out0_done, SETS)
                bank = o_bank("y0")
                for t in range(TT):
                    for g in range(SETS):
                        ins = nc.tensor.matmul(bank[:, P * t:P * t + P], out0[:, g, P * t:P * t + P], w("wo0")[:, P * g:P * g + P],
                                               start=g == 0, stop=g == SETS - 1)
                ins.then_inc(o_full, 1)
                pe.wait_ge(x1_done, 1)
                turned(a_bank("x1T"), x1)

                pe.wait_ge(ffn_in, 32)
                pe.wait_ge(a_free, A.nth("x1T"))
                for k in range(KC):
                    nc.tensor.matmul(a_bank(("f1", k))[:, :], f1("w1")[:, P * k:P * k + P], xT1[:, :], start=True,
                                     stop=True).then_inc(a_full, 1)
                    nc.tensor.matmul(o_bank(("f2", k))[:, :], f1("w2")[:, P * k:P * k + P], xT1[:, :], start=True,
                                     stop=True).then_inc(o_full, 1)
                pe.wait_ge(o_free, O.nth(("f2", KC - 1)))

                def hidden(name, wgt, src):
                    for k in range(KC):
                        bank = a_bank((name, k))
                        for j in range(KC):
                            ins = nc.tensor.matmul(bank[:, :], wgt[:, HID0 * j + P * k:HID0 * j + P * k + P], src[:, j, :],
                                                   start=j == 0, stop=j == KC - 1)
                        ins.then_inc(a_full, 1)

                hidden("h1", f1("h1"), hid)
                pe.wait_ge(a_free, A.nth(("h1", KC - 1)))
                hidden("h2", f2("h2"), gelu1)
                pe.wait_ge(a_free, A.nth(("h2", KC - 1)))
                bank = o_bank("y1")
                for t in range(TT):
                    for j in range(KC):
                        ins = nc.tensor.matmul(bank[:, P * t:P * t + P], gelu2[:, j, P * t:P * t + P], f2("w3")[:, P * j:P * j + P],
                                               start=j == 0, stop=j == KC - 1)
                ins.then_inc(o_full, 1)
                pe.wait_ge(x2_done, 1)
                turned(a_bank("x2T"), x2)

                pe.wait_ge(a_free, A.nth("x2T"))
                for k in range(NC + 1):
                    if k < NC:
                        nc.tensor.matmul(a_bank(("k", k))[:, :], w("Wk")[:, P * k:P * k + P], xe[:, MEM:J], start=True,
                                         stop=True).then_inc(a_full, 1)
                    if k:
                        pe.wait_ge(k_sq, k)
                        nc.tensor.matmul(a_bank(("kn", k - 1))[:, :], c("heads"), sq[:, (k - 1) % 2], start=True,
                                         stop=True).then_inc(a_full, 1)
                for k in range(TT + 1):
                    rows = min(P, J - P * k)
                    for z in range(2):
                        bank = a_bank(("vx", k, z))
                        half = slice(512 * z, 512 * z + 512)
                        ins = nc.tensor.matmul(bank[0:rows, :], xe[:, P * k:P * k + rows], w("Wv")[:, half], start=True, stop=k > 0)
                        if k == 0:
                            ins = nc.tensor.matmul(bank[:, :], ident[0:MEM, :], memv[:, half], start=False, stop=True)
                        ins.then_inc(a_full, 1)
                for k in range(NC):
                    nc.tensor.matmul(a_bank(("q", k))[:, :], w("Wq")[:, P * k:P * k + P], xe[:, MEM:J], start=True,
                                     stop=True).then_inc(a_full, 1)
                bank = a_bank("qn")
                for k in range(NC):
                    pe.wait_ge(q_sq, k + 1)
                    for t in range(TT):
                        ins = nc.tensor.matmul(bank[:, H1 * t + 2 * k:H1 * t + 2 * k + 2], sq[:, k % 2, P * t:P * t + P],
                                               c("heads")[:, 0:P:HD1], start=True, stop=True)
                    ins.then_inc(q_summed if k < NC - 1 else a_full, 1)
                pe.wait_ge(k_done, NC)
                pe.wait_ge(rq_done, 1)

                scores_tensor(pe, RINGS)
                pe.wait_ge(worst_done, 1)
                nc.tensor.matmul(o_bank("bad")[0:1, 0:P], worst[:, :], ident, start=True, stop=True).then_inc(o_full, 1)

            @block.scalar
            def _(act):
                def filled(key):
                    act.wait_ge(a_full, A.nth(key))
                    return banks_a[A.bank(key)]

                def copied(key, dst, src=slice(0, 512)):
                    nc.scalar.copy(dst, filled(key)[:, src]).then_inc(a_free, 1)

                copied_v = filled("v")
                for odd in range(2):
                    ins = nc.scalar.copy(v_pad[:, :, :, 2 * SUM_COLS * odd:2 * SUM_COLS * odd + HD0],
                                         copied_v[:, :].rearrange("p (k a n) -> p k a n", k=TT, a=PAIRS)[:, :, :, HD0 * odd:HD0 * odd + HD0])
                ins.then_inc(a_free, 1)
                for h in range(H0):
                    if h >= E_SLOTS:
                        act.wait_ge(av0_done, h - E_SLOTS + 1)
                    for k in range(TT):
                        bank = filled(("st", h, k))
                        nc.scalar.activation(exps[:, h % E_SLOTS, E_OFF[k]:E_OFF[k] + S - P * k], bank[:, 0:S - P * k], ACT.Exp,
                                             scale=SCALE0).then_inc(a_free, 1)
                copied("x1T", xT1[:, :])
                for k in range(KC):
                    nc.scalar.activation(silu0[:, k], filled(("f1", k))[:, :], ACT.Silu, scale=w("w1s")[:, k:k + 1]).then_inc(a_free, 1)
                for k in range(KC):
                    nc.scalar.activation(gelu1[:, k], filled(("h1", k))[:, :], ACT.Gelu, scale=w("h1s")[:, k:k + 1]).then_inc(a_free, 1)
                for k in range(KC):
                    nc.scalar.activation(gelu2[:, k], filled(("h2", k))[:, :], ACT.Gelu, scale=w("h2s")[:, k:k + 1]).then_inc(a_free, 1)
                copied("x2T", xe[:, MEM:J])
                for k in range(NC + 1):
                    if k < NC:
                        copied(("k", k), kT_v[:, k, MEM:J])
                    if k:
                        bank = filled(("kn", k - 1))
                        if k >= 3:
                            act.wait_ge(k_done, k - 2)
                        nc.scalar.activation(nr[:, (k - 1) % 2], bank[:, :], ACT.Sqrt).then_inc(a_free, 1)
                for k in range(TT + 1):
                    rows = min(P, J - P * k)
                    for z in range(2):
                        bank = filled(("vx", k, z))
                        nc.scalar.copy(vx_v[0:rows, k, 512 * z:512 * z + 512], bank[0:rows, :]).then_inc(a_free, 1)
                for k in range(NC):
                    copied(("q", k), qT_v[:, k, :])
                nc.scalar.activation(rq[:, :, :].rearrange("p t h -> p (t h)"), filled("qn")[:, 0:TT * H1], ACT.Sqrt).then_inc(a_free, 1)
                act.wait_ge(rq_done, 1)

                scores_scalar(act, RINGS, False)

            @block.vector
            def _(dve):
                chain = Chain(dve, v_chain)

                def filled(key):
                    dve.wait_ge(o_full, O.nth(key))
                    return banks_o[O.bank(key)]

                for z, (k0, k1) in enumerate((("rq", "rqs"), ("rk", "rks"))):
                    bank = filled(k0)
                    if z:
                        dve.wait_ge(rot_done, z)
                    nc.vector.tensor_tensor(rope_t[:, 0], bank[:, :], c("rope_c"), ALU.mult).then_inc(o_free, 1)
                    bank = filled(k1)
                    nc.vector.tensor_tensor(rope_t[:, 1], bank[:, :], c("rope_s"), ALU.mult).then_inc(o_free, 1)
                    dve.wait_ge(o_free, O.nth(k1))
                    nc.vector.tensor_tensor(rot[:, z], rope_t[:, 0], rope_t[:, 1], ALU.add).then_inc(rot_done, 1)
                def split_maxima(g):
                    bank = filled(("mT", g))
                    nc.vector.tensor_scalar(neg_rows, bank[0:HS, :], -1.0, None, ALU.mult).then_inc(o_free, 1)
                    dve.wait_ge(o_free, O.nth(("mT", g)))
                    chain.link(nc.vector.tensor_copy(max_parts[:, g, 0], neg_rows))
                    chain.link(nc.vector.tensor_tensor(neg_left, neg_rows, max_parts[:, g, 0], ALU.subtract))
                    chain.link(nc.vector.tensor_copy(max_parts[:, g, 1], neg_left))
                    chain.link(nc.vector.tensor_tensor(neg_left, neg_left, max_parts[:, g, 1], ALU.subtract))
                    nc.vector.tensor_copy(max_parts[:, g, 2], neg_left).then_inc(rows_done, 1)

                for g, order in enumerate((S_FIRST, S_SECOND)):
                    for i, h in order:
                        bank = filled(("s", i, h))
                        nc.vector.tensor_reduce(row_max[:, i, h:h + 1], bank[:, 0:P * (i + 1)], X, ALU.max).then_inc(o_free, 1)
                    split_maxima(g)
                for g in range(SETS):
                    dve.wait_ge(av0_done, HS * (g + 1))
                    nc.vector.tensor_copy(sums_in[:, g], banks_t[g][:, :]).then_inc(sums_done, 1)
                    bank = filled(("den", g))
                    nc.vector.reciprocal(rec0, bank[:, :]).then_inc(o_free, 1)
                    dve.wait_ge(o_free, O.nth(("den", g)))
                    nc.vector.tensor_tensor(out0[:, g], sums_in[:, g], rec0, ALU.mult).then_inc(out0_done, 1)
                    dve.wait_ge(out0_done, g + 1)
                bank = filled("y0")
                dve.wait_ge(x_in, 32)
                nc.vector.tensor_tensor(res[:, :, :], rows(bank), x0[:, :, :], ALU.add).then_inc(o_free, 1)
                dve.wait_ge(o_free, O.nth("y0"))
                norm(dve, chain, 0, x1, x1_done)
                for k in range(KC):
                    bank = filled(("f2", k))
                    dve.wait_ge(a_free, A.nth(("f1", k)))
                    nc.vector.scalar_tensor_tensor(out=hid[:, k], in0=bank[:, :], scalar=w("w2s")[:, k:k + 1], in1=silu0[:, k],
                                                   op0=ALU.mult, op1=ALU.mult).then_inc(o_free, 1)
                bank = filled("y1")
                nc.vector.tensor_tensor(res[:, :, :], rows(bank), w("w3s").unsqueeze(1).to_broadcast([P, TT, D]),
                                        ALU.mult).then_inc(o_free, 1)
                dve.wait_ge(o_free, O.nth("y1"))
                chain.link(nc.vector.tensor_tensor(res[:, :, :], res[:, :, :], x1[:, :, :], ALU.add))
                norm(dve, chain, 1, x2, x2_done)
                nc.vector.tensor_copy(kT_v[:, :, 0:MEM], memk_n[:, :].rearrange("p (c m) -> p c m", c=NC))
                for k in range(NC):
                    dve.wait_ge(a_free, A.nth(("kn", k)))
                    n = nr[:, k % 2]
                    chain.link(nc.vector.tensor_scalar(n, n, 1e-12, None, ALU.max))
                    chain.link(nc.vector.reciprocal(n, n))
                    nc.vector.tensor_tensor(kT_v[:, k, MEM:J], kT_v[:, k, MEM:J], n, ALU.mult).then_inc(k_done, 1)
                dve.wait_ge(a_free, A.nth("qn"))
                r = rq[:, :, :].rearrange("p t h -> p (t h)")
                chain.link(nc.vector.tensor_scalar(r, r, 1e-12, None, ALU.max))
                chain.link(nc.vector.reciprocal(r, r))
                nc.vector.tensor_scalar(r, r, QK_SCALE, None, ALU.mult).then_inc(rq_done, 1)

                nc.vector.memset(above[:, 0:NARROW_FROM], AIM)
                scores_vector(dve, chain, RINGS, False)
                chain.link(nc.vector.tensor_scalar(off[:, :], above[:, :], -AIM, None, ALU.add))
                chain.link(nc.vector.tensor_tensor(off[:, :], off[:, :], off[:, :], ALU.mult))
                nc.vector.tensor_reduce(worst[:, :], off[:, :], X, ALU.max).then_inc(worst_done, 1)
                bank = filled("bad")
                chain.link(nc.vector.tensor_reduce(flag_f[:, :], bank[0:1, 0:P], X, ALU.max))
                chain.link(nc.vector.tensor_scalar(flag[:, :], flag_f[:, :], (WINDOW / 2) ** 2, None, ALU.is_gt))

        def again(block):
            @block.sync
            def _(sp):
                scores_sync(sp, RINGS_AGAIN)

            @block.gpsimd
            def _(pool):
                scores_gpsimd(pool, Chain(pool, g_chain), True)

            @block.tensor
            def _(pe):
                scores_tensor(pe, RINGS_AGAIN)

            @block.scalar
            def _(act):
                scores_scalar(act, RINGS_AGAIN, True)

            @block.vector
            def _(dve):
                scores_vector(dve, Chain(dve, v_chain), RINGS_AGAIN, True)

        def experts(b, block):
            A, O = RINGS_EXPERTS

            @block.sync
            def _(sp):
                sp.dma_start(dots[:, 0:M_N], moe_d).then_inc(moe_in, 16)
                sp.wait_ge(x4_done, 1)
                sp.dma_start(out_d[b].rearrange("(t p) d -> p t d", p=P), x4[:, :, :]).then_inc(y_out, 16)
                sp.wait_ge(y_out, 16)

            @block.gpsimd
            def _(pool):
                inverse_root(pool, 0)
                inverse_root(pool, 1)

            @block.tensor
            def _(pe):
                a_bank, o_bank = empty_banks(pe, A, O)
                pe.wait_ge(x3_done, 1)
                turned(a_bank("x3T"), x3)
                pe.wait_ge(a_free, A.nth("x3T"))
                bank = o_bank("lg")
                for t in range(TT):
                    ins = nc.tensor.matmul(bank[:, EXPERTS * t:EXPERTS * (t + 1)], xT3[:, P * t:P * t + P], w("gate"), start=True, stop=True)
                ins.then_inc(o_full, 1)
                pe.wait_ge(moe_in, 16)
                pe.wait_ge(comb_done, 1)
                bank = o_bank("cT")
                for t in range(TT):
                    ins = nc.tensor.transpose(bank[0:EXPERTS, P * t:P * t + P], comb[:, t, :], ident)
                ins.then_inc(o_full, 1)
                pe.wait_ge(o_free, O.nth("cT"))
                for k in range(MC + 1):
                    n = P if k < MC else HID1
                    nc.tensor.matmul(a_bank(("m1", k))[0:n, :], mw("w1")[:, P * k:P * k + n], xT3[:, :], start=True,
                                     stop=True).then_inc(a_full, 1)
                    nc.tensor.matmul(o_bank(("m3", k))[0:n, :], mw("w3")[:, P * k:P * k + n], xT3[:, :], start=True,
                                     stop=True).then_inc(o_full, 1)
                    if k < MC:
                        nc.tensor.matmul(o_bank(("cb", k))[:, :], mw("spread")[0:EXPERTS, P * k:P * k + P], comb_T, start=True,
                                         stop=True).then_inc(o_full, 1)
                pe.wait_ge(o_free, O.nth(("m3", MC)))
                bank = o_bank("y3")
                for t in range(TT):
                    for k in range(MC + 1):
                        n = P if k < MC else HID1
                        ins = nc.tensor.matmul(bank[:, P * t:P * t + P], acts[0:n, k, P * t:P * t + P], mw("w2")[0:n, P * k:P * k + P],
                                               start=k == 0, stop=k == MC)
                ins.then_inc(o_full, 1)

            @block.scalar
            def _(act):
                def filled(key):
                    act.wait_ge(a_full, A.nth(key))
                    return banks_a[A.bank(key)]

                nc.scalar.copy(xT3[:, :], filled("x3T")[:, :]).then_inc(a_free, 1)
                act.wait_ge(o_free, O.nth("lg"))
                nc.scalar.activation(gates_e[:, :, 0:EXPERTS], logits[:, :, :], ACT.Exp).then_inc(ex_e_done, 1)
                for k in range(MC + 1):
                    n = P if k < MC else HID1
                    bank = filled(("m1", k))
                    if k >= 2:
                        act.wait_ge(o_free, O.nth(("m3", k - 2)))
                    nc.scalar.activation(silu1[0:n, k % 2], bank[0:n, :], ACT.Silu).then_inc(a_free, 1)

            @block.vector
            def _(dve):
                chain = Chain(dve, v_chain)

                def filled(key):
                    dve.wait_ge(o_full, O.nth(key))
                    return banks_o[O.bank(key)]

                norm(dve, chain, 0, x3, x3_done)
                bank = filled("lg")
                lg = bank[:, 0:TT * EXPERTS].rearrange("p (t e) -> p t e", t=TT)
                chain.link(nc.vector.tensor_reduce(logit_m[:, :], lg, X, ALU.max))
                nc.vector.tensor_tensor(logits[:, :, :], lg, logit_m[:, :].unsqueeze(2).to_broadcast([P, TT, EXPERTS]),
                                        ALU.subtract).then_inc(o_free, 1)
                dve.wait_ge(ex_e_done, 1)
                for t in range(TT):
                    ins = nc.vector.max(out=top_e[:, t], in_=gates_e[:, t, 0:EXPERTS])
                chain.link(ins)
                chain.link(nc.vector.memset(top_e[:, :, TOP_E:8], -1.0))
                for t in range(TT):
                    ins = nc.vector.match_replace(out=rest_e[:, t], in_to_replace=top_e[:, t], in_values=gates_e[:, t], imm_value=0.0)
                chain.link(ins)
                chain.link(nc.vector.tensor_tensor(comb[:, :, :], gates_e[:, :, 0:EXPERTS], rest_e[:, :, 0:EXPERTS], ALU.subtract))
                chain.link(nc.vector.tensor_reduce(sum_e[:, :], comb[:, :, :], X, ALU.add))
                chain.link(nc.vector.reciprocal(rec_e[:, :], sum_e[:, :]))
                nc.vector.tensor_tensor(comb[:, :, :], comb[:, :, :], rec_e[:, :].unsqueeze(2).to_broadcast([P, TT, EXPERTS]),
                                        ALU.mult).then_inc(comb_done, 1)
                bank = filled("cT")
                nc.vector.tensor_copy(comb_T, bank[0:EXPERTS, :]).then_inc(o_free, 1)
                for k in range(MC + 1):
                    n = P if k < MC else HID1
                    bank = filled(("m3", k))
                    dve.wait_ge(a_free, A.nth(("m1", k)))
                    dst = gated[:, k % 2] if k < MC else acts[0:n, k]
                    nc.vector.tensor_tensor(dst, bank[0:n, :], silu1[0:n, k % 2], ALU.mult).then_inc(o_free, 1)
                    if k < MC:
                        bank = filled(("cb", k))
                        dve.wait_ge(o_free, O.nth(("m3", k)))
                        nc.vector.tensor_tensor(acts[:, k], bank[:, :], gated[:, k % 2], ALU.mult).then_inc(o_free, 1)
                bank = filled("y3")
                nc.vector.tensor_tensor(res[:, :, :], rows(bank), x3[:, :, :], ALU.add).then_inc(o_free, 1)
                dve.wait_ge(o_free, O.nth("y3"))
                norm(dve, chain, 1, x4, x4_done)

        with nc.Fori(0, B) as b:
            with nc.Block() as block:
                front(b, block)
            clear_semaphores()
            missed = nc.values_load(flag[:, :], min_val=0, max_val=1)
            with nc.If(missed > 0):
                with nc.Block() as block:
                    again(block)
                clear_semaphores()
            with nc.Block() as block:
                experts(b, block)
            clear_semaphores()


def constants():
    f = np.float32
    half = HD0 // 2
    inv = (1.0 / f(10000.0) ** (np.arange(half, dtype=f) / f(half))).astype(f)
    freqs = np.arange(S, dtype=f)[:, None] * inv[None, :]
    d = np.arange(P) % HD0
    cos, sin = np.cos(freqs)[:, d % half].T, np.sin(freqs)[:, d % half].T
    sin = np.where((d < half)[:, None], -sin, sin)
    q = np.arange(P)
    sums = q[:, None] == q[None, :] // SUM_COLS * SUM_COLS + HD0 + q[None, :] % HD0
    heads = (q[:, None] // HD1 == q[None, :] // HD1)
    dpre = (q[:, None] // H1 == q[None, :] // H1)
    dpost = (q[:, None] // H1 == q[None, :] % R8)
    spread = np.zeros((P, MC * P))
    spread[:EXPERTS] = np.arange(EXPERTS)[:, None] == np.arange(MC * P)[None, :] // HID1
    rank = np.broadcast_to(TOPK - 1 - np.arange(WINDOW), (P, WINDOW))
    c = np.concatenate([cos, sin, np.eye(P), heads, sums, *thresholds(), rank], 1).astype(f)
    mask_s = np.where(q[None, :] > q[:, None], LOW, 0.0)
    mix = [np.where(np.arange(GROUP * R8)[None, :] > R8 * v + q[:, None] // H1, LOW, 0.0) for v in range(GROUP)]
    cb = np.concatenate([np.eye(P), mask_s, mask_s.T] + mix + [dpre, dpost], 1).astype(f)
    return c, cb, spread.astype(f)


def thresholds():
    first, slope = np.zeros((P, SUBS), np.float32), np.zeros((P, SUBS), np.float32)

    def quantile(share):
        lo, hi = -10.0, 10.0
        for _ in range(60):
            mid = (lo + hi) / 2
            lo, hi = (mid, hi) if (1 + erf(mid / sqrt(2))) / 2 < share else (lo, mid)
        return lo

    for n in range(NARROW_FROM, SUBS):
        for q in range(P):
            seen = R8 * n + q // H1 + 1 + MEM
            first[q, n] = quantile(1 - (AIM + 0.5) / seen)
            slope[q, n] = -DAMP / (2 * seen * exp(-first[q, n] ** 2 / 2) / sqrt(2 * pi))
    return first, slope


def laid_out(a):
    x = a["L0_attn_x"]
    qkv = a["L0_attn_w_qkv"]
    wq, wk, wv = qkv[:D], qkv[D:2 * D], qkv[2 * D:]
    swap = (np.arange(D) // HD0) * HD0 + (np.arange(D) + HD0 // 2) % HD0

    def cols(v):
        return v.reshape(-1, P).T

    def chunked(m):
        return m.reshape(-1, P, m.shape[1]).transpose(1, 0, 2).reshape(P, -1)

    hs = np.broadcast_to(np.repeat(a["L1_attn_head_scale_params"].reshape(H1), R8), (P, P))
    wo0 = np.pad(a["L0_attn_w_out"].T.reshape(SETS, HS, HD0, D), ((0, 0), (0, 0), (0, SUM_COLS - HD0), (0, 0)))
    wo0 = wo0.reshape(SETS, P, D).transpose(1, 0, 2).reshape(P, SETS * D)
    memk = a["L1_attn_mem_k"].reshape(NC, 2, MEM, HD1).transpose(1, 3, 0, 2).reshape(P, NC * MEM)
    pre = np.tile(a["L1_attn_W_pre_th"].T, (R8, R8))
    post = np.tile(np.repeat(a["L1_attn_W_post_th"].T, R8, axis=1), (R8, 1))
    w = [wq.T, wq[swap].T, wk.T, wk[swap].T, wv.T, wo0,
         cols(a["L0_ffn_w1_s"]), cols(a["L0_ffn_w2_s"]), cols(a["L0_ffn_h1_s"]), cols(a["L0_ffn_h2_s"]),
         np.broadcast_to(a["L0_ffn_w3_s"], (P, D)),
         a["L1_attn_Wk"], a["L1_attn_Wq"], a["L1_attn_Wv"], a["L1_attn_Wg"], cols(a["L1_attn_bg"]), hs,
         chunked(a["L1_attn_Wo"]), memk, pre, post, a["L1_ffn_gate_w"].T]
    memv = a["L1_attn_mem_v"].transpose(1, 0, 2).reshape(MEM, H1 * HD1)
    ffn1 = [a["L0_ffn_w1_w"].T, a["L0_ffn_w2_w"].T, chunked(a["L0_ffn_h1_w"].T)]
    ffn2 = [chunked(a["L0_ffn_h2_w"].T), chunked(a["L0_ffn_w3_w"].T)]
    up = [np.concatenate([a[f"L1_ffn_{n}"].reshape(MC * P, D), a[f"L1_ffn_s{n}"]]).T for n in ("w1", "w3")]
    down = np.concatenate([a["L1_ffn_w2"].transpose(0, 2, 1).reshape(MC * P, D), a["L1_ffn_sw2"].T, np.zeros((HID1, D), np.float32)])
    return {
        "xT": x.transpose(0, 2, 1),
        "x": x.reshape(B, TT, P, D).transpose(0, 2, 1, 3).reshape(B, P, TT * D),
        "w": np.concatenate(w, 1), "memv": memv,
        "ffn1": np.concatenate(ffn1, 1), "ffn2": np.concatenate(ffn2, 1),
        "moe": np.concatenate(up + [chunked(down), constants()[2]], 1),
    }


def kernel(**inputs):
    import concourse.bacc as bacc
    from concourse.bass_utils import run_bass_kernel_spmd

    arrays = {k: np.ascontiguousarray(v) for k, v in laid_out({k: np.asarray(v) for k, v in inputs.items()}).items()}
    arrays["c"], arrays["cb"], _ = constants()
    nc = bacc.Bacc("TRN2", target_bir_lowering=False, num_devices=1)
    d = {k: nc.dram_tensor(f"{k}_dram", v.shape, mybir.dt.from_np(v.dtype), kind="ExternalInput").ap() for k, v in arrays.items()}
    parts = nc.dram_tensor("parts_dram", [2, P, 3 * S], BF16, kind="Internal").ap()
    maxes = nc.dram_tensor("maxes_dram", [SETS, HS, 3 * S], BF16, kind="Internal").ap()
    out = nc.dram_tensor("out_dram", [B, S, D], F32, kind="ExternalOutput").ap()
    network(nc, d["xT"], d["x"], d["w"], d["c"], d["cb"], d["memv"], d["ffn1"], d["ffn2"], d["moe"], parts, maxes, out)
    r = run_bass_kernel_spmd(nc, [{f"{k}_dram": v for k, v in arrays.items()}], core_ids=[0])
    return r.results[0]["out_dram"]
```

```python
from contextlib import ExitStack
from math import erf, exp, pi, sqrt

import numpy as np

import concourse.bass as bass
from concourse import mybir

F32 = mybir.dt.float32
BF16 = mybir.dt.bfloat16
ALU = mybir.AluOpType
ACT = mybir.ActivationFunctionType
X = mybir.AxisListType.X

P = 128
B, S, D = 8, 512, 128
TT = S // P
EPS = 1e-5
LOW = -1.0e30
LOWEST = -3.0e38

H0, HD0 = 16, 8
PAIRS = H0 // 2
SCALE0 = 1.0 / HD0 ** 0.5
SETS = 2
HS = H0 // SETS
SUM_COLS = 2 * HD0
V_COLS = 3 * SUM_COLS
Q_PARTS = (0, 0, 1, 1, 0, 2)
K_PARTS = (0, 1, 0, 1, 2, 0)
SLOTS = len(Q_PARTS)
MAX_ROW = SLOTS * HD0
STACK = MAX_ROW + 3
E_SLOTS = 3
HID0 = 512
KC = HID0 // P
H1, HD1, MEM, TOPK = 16, 64, 4, 64
NC = H1 * HD1 // P
J = MEM + S
QK_SCALE = 10.0
R8 = P // H1
SUBS = S // R8
PER_TILE = P // R8
GROUP = 4
RB = 64
PER_BLOCK = RB // R8
ROUNDS = TOPK // 8
TILE_ORDER = (3, 1, 0, 2)
SEQ = [PER_TILE * t + u for t in TILE_ORDER for u in range(PER_TILE)]
PAIR = 2
STEPS = SUBS // PAIR
STEPS_TILE, STEPS_BLOCK = PER_TILE // PAIR, PER_BLOCK // PAIR
SCORES_AT = {1: 0, 0: H1 * (MEM + P * 3), 2: 0, 3: 0}
SCORES_N = H1 * (MEM + P * 3) + H1 * (MEM + P)
MIX_SLOTS, X_SLOTS, E1_SLOTS, A_SLOTS = 4, 8, 4, 4
LIVE = 3
NARROW_FROM = 12
WINDOW = 16
AIM = TOPK - (WINDOW + 1) / 2
DAMP = (0.8, 0.6, 0.4)
COUNTS = len(DAMP)
EXPERTS, HID1, TOP_E = 16, 64, 4
MC = EXPERTS * HID1 // P
PAD_E = 8


def width(n):
    return MEM + GROUP * R8 * (n // GROUP + 1)


def narrow(n):
    return n >= NARROW_FROM


def ahead(s):
    out = [("qk", TILE_ORDER[0], g) for g in range(H1)] if s < 0 else []
    if 0 <= s <= TT:
        out.append(("vx", s))
    for o in range(TT):
        t, at = TILE_ORDER[o], STEPS_TILE * (o - 1)
        if s == STEPS_TILE * o + STEPS_TILE // 2 + 1:
            out.append(("g", t))
        per, begin = (3, at) if o > 1 else (8, at + STEPS_TILE - 3)
        if o and s >= begin:
            out += [("qk", t, g) for g in range(H1) if g // per == s - begin]
    return out


def pieces(w):
    return [(0, w)] if w <= 512 else [(0, w // 2), (w // 2, w - w // 2)]


class Ring:

    def __init__(self, keys):
        self.order = {k: n for n, k in enumerate(keys)}
        assert len(self.order) == len(keys)

    def bank(self, key):
        return self.order[key] % 2

    def nth(self, key):
        return self.order[key] + 1


def weight_layout():
    sizes = dict(wq=P, wqs=P, wk=P, wks=P, wv=P, wo0=SETS * P, w1s=KC, w2s=KC, h1s=KC, h2s=KC, w3s=P,
                 Wk=H1 * HD1, Wq=H1 * HD1, Wv=H1 * HD1, Wg=H1 * HD1, bg=NC, hs=P, Wo=NC * P, memk=NC * MEM,
                 pre=P, post=P, gate=EXPERTS)
    const = dict(rope_c=S, rope_s=S, ident=P, heads=P, sums=P, pick=2 * H1 - 2, first=SUBS, slope=SUBS, rank=WINDOW)
    return sizes, const


def columns(sizes):
    at, out = 0, {}
    for k, n in sizes.items():
        out[k] = (at, at + n)
        at += n
    return out, at


def network(nc, xT_d, x_d, w_d, c_d, cb_d, memv_d, ffn1_d, ffn2_d, moe_d, parts_d, maxes_d, out_d):
    W_AT, W_N = columns(weight_layout()[0])
    C_AT, C_N = columns(weight_layout()[1])
    F1_AT, F1_N = columns(dict(w1=HID0, w2=HID0, h1=KC * HID0))
    F2_AT, F2_N = columns(dict(h2=KC * HID0, w3=KC * P))
    M_AT, M_N = columns(dict(w1=MC * P + HID1, w3=MC * P + HID1, w2=(MC + 1) * P, spread=MC * P))

    with ExitStack() as ctx:
        def sb(name, shape, dt=F32):
            return ctx.enter_context(nc.sbuf_tensor(name, shape, dt))

        def sem(name):
            s = ctx.enter_context(nc.semaphore(name))
            sems.append(s)
            return s

        sems = []
        wts = sb("wts", [P, W_N])
        cst = sb("cst", [P, C_N])
        CB_N = 3 * P + GROUP * GROUP * R8
        cstb = sb("cstb", [P, CB_N], BF16)
        memv = sb("memv", [MEM, H1 * HD1])
        powers = sb("powers", [P, TT + 2 * PAIR])

        def w(name):
            a, b = W_AT[name]
            return wts[:, a:b]

        def c(name):
            a, b = C_AT[name]
            return cst[:, a:b]

        ident = c("ident")
        identb, mask_s, mask_t = cstb[:, 0:P], cstb[:, P:2 * P], cstb[:, 2 * P:3 * P]
        mix_mask = cstb[:, 3 * P:].rearrange("p (v j) -> p v j", v=GROUP)
        tokens = sb("tokens", [P, 3 * S])
        xT = tokens[:, 0:S]
        x0, x1 = (tokens[:, S * z:S * z + S].rearrange("p (t d) -> p t d", t=TT) for z in (1, 2))
        res = sb("res", [P, TT, D])
        x2 = sb("x2", [P, TT, D])
        xe = sb("xe", [P, MEM + S])
        stats = sb("stats", [P, TT, 6])
        mv = sb("mv", [P, TT, 2])
        var = sb("var", [P, TT])
        rstd = sb("rstd", [P, TT])
        xT1 = xT

        kT = sb("kT", [P, NC * J])
        qT = sb("qT", [P, NC * S])
        vx = sb("vx", [P, (TT + 1) * H1 * HD1])
        dots = sb("dots", [P, SCORES_N])
        at2 = sb("at2", [P, TT * H1 * RB])
        tail = sb("tail", [MEM, H1, RB // 2])
        gate = sb("gate", [P, NC, P])
        mixin = sb("mixin", [P, MIX_SLOTS, J])
        squares = sb("squares", [P, 4 * S])
        xs_own = sb("xs", [P, X_SLOTS - 2, J])
        xs = [xs_own[:, i] for i in range(X_SLOTS - 2)] + [tokens[:, J * i:J * i + J] for i in range(2)]
        ex_own = sb("ex", [P, E1_SLOTS - 2, J])
        ex = [ex_own[:, i] for i in range(E1_SLOTS - 2)] + [squares[:, J * i:J * i + J] for i in range(2)]
        left_own = sb("left", [P, J])
        left = [left_own[:, :], squares[:, 2 * J:3 * J]]
        attn = sb("attn", [P, A_SLOTS, J])
        wsc = sb("wsc", [P, A_SLOTS, P])
        og = sb("og", [P, NC, P])
        top = sb("top", [P, LIVE, PAIR, 8])
        negm = sb("negm", [P, LIVE, PAIR])
        moments = sb("moments", [P, LIVE, PAIR, 6])
        meanvar = sb("meanvar", [P, LIVE, PAIR, 2])
        spread_ = sb("spread_", [P, LIVE, PAIR])
        slope_ = sb("slope_", [P, LIVE, PAIR])
        shift = sb("shift", [P, LIVE, PAIR])
        thr = sb("thr", [P, LIVE, PAIR])
        signs = sb("signs", [P, LIVE, PAIR])
        best = sb("best", [P, PAIR, WINDOW])
        picked = sb("picked", [P, PAIR, WINDOW])
        bound = sb("bound", [P, PAIR])
        ssum = sb("ssum", [P, LIVE, PAIR])
        rsum = sb("rsum", [P, LIVE, PAIR])
        above = sb("above", [P, SUBS])
        off = sb("off", [P, SUBS])
        worst = sb("worst", [P, 1])
        flag_f = sb("flag_f", [1, 1])
        flag = sb("flag", [1, 1], mybir.dt.int32)
        rq = sb("rq", [P, TT, H1])
        sq, nr = (squares[:, 2 * S * z:2 * S * z + 2 * S].rearrange("p (z s) -> p z s", z=2) for z in range(2))
        kT_v = kT[:, :].rearrange("p (c j) -> p c j", c=NC)
        qT_v = qT[:, :].rearrange("p (c s) -> p c s", c=NC)
        vx_v = vx[:, :].rearrange("p (c n) -> p c n", c=TT + 1)
        at_v = at2[:, :].rearrange("p (c h i) -> p c h i", c=TT, h=H1)
        memk_n = sb("memk_n", [P, NC * MEM])
        pre_b = sb("pre_b", [P, P])
        post_b = sb("post_b", [P, P])

        x3, xT3 = og[:, 0:NC // 2], og[:, NC // 2:].rearrange("p c s -> p (c s)")
        x4 = gate[:, 0:NC // 2]

        stacks = kT[:, 0:PAIRS * S].bitcast(BF16).rearrange("p (z a s) -> p z a s", z=2, a=PAIRS)
        q_stack, k_stack = stacks[:, 0], stacks[:, 1]
        rope_t = at2[:, 0:2 * S].rearrange("p (z s) -> p z s", z=2)
        rot = at2[:, 2 * S:4 * S].rearrange("p (z s) -> p z s", z=2)
        parts = at2[:, 4 * S:7 * S].bitcast(BF16).rearrange("p (z k s) -> p z k s", z=2, k=3)
        part_t = at2[:, 7 * S:8 * S]
        E_N = S + 3 * P + 2 * P + P
        E_OFF = [0, S, S + 3 * P, S + 5 * P]
        exps = vx[:, 0:E_SLOTS * E_N].rearrange("p (z n) -> p z n", z=E_SLOTS)
        v_pad = dots[:, F1_N:F1_N + TT * PAIRS * V_COLS].rearrange("p (k a n) -> p k a n", k=TT, a=PAIRS)
        sums_in = og[:, :, :].rearrange("p (g c) s -> p g (c s)", g=SETS)
        free = F1_N + TT * PAIRS * V_COLS
        out0 = dots[:, free:free + SETS * S].rearrange("p (g s) -> p g s", g=SETS)
        rec0 = dots[:, free + SETS * S:free + 3 * S]
        row_max = dots[:, free + 3 * S:free + 3 * S + TT * H0].rearrange("p (t h) -> p t h", t=TT)
        K_SLOTS, Q_SLOTS = 2, 4
        assert (H1, HD1) == (EXPERTS, HID1)
        norms_in = og[0:H1, :, :].rearrange("h c s -> h (c s)")
        k_norm, q_norm = norms_in[:, 0:S], norms_in[:, S:2 * S]
        spread_h = dots[0:H1, free + 4 * S:free + 4 * S + NC * P]

        def squares_of(name, k):
            if name == "ks":
                return squares[:, S * (k % K_SLOTS):S * (k % K_SLOTS) + S]
            z = k % Q_SLOTS
            return squares[:, S * (2 + z):S * (3 + z)] if z < 2 else gate[:, 4 * z - 8:4 * z - 4].rearrange("p c s -> p (c s)")

        max_parts = squares[0:HS, 0:SETS * 3 * S // 2].bitcast(BF16).rearrange("h (g k s) -> h g k s", g=SETS, k=3)
        neg_rows = squares[0:HS, SETS * 3 * S // 2:]
        neg_left = rec0[0:HS]

        def f1(name):
            a, b = F1_AT[name]
            return dots[:, a:b]

        def f2(name):
            a, b = F2_AT[name]
            return at2[:, a:b]

        silu0 = kT[:, 0:KC * S].rearrange("p (c s) -> p c s", c=KC)
        hid = qT[:, 0:KC * S].rearrange("p (c s) -> p c s", c=KC)
        gelu1 = kT[:, KC * S:2 * KC * S].rearrange("p (c s) -> p c s", c=KC)
        gelu2 = qT[:, KC * S:2 * KC * S].rearrange("p (c s) -> p c s", c=KC)

        def mw(name):
            a, b = M_AT[name]
            return dots[:, a:b]

        silu1 = qT[:, 0:2 * S].rearrange("p (z s) -> p z s", z=2)
        gated = qT[:, 2 * S:4 * S].rearrange("p (z s) -> p z s", z=2)
        acts = vx[:, 0:(MC + 1) * S].rearrange("p (c s) -> p c s", c=MC + 1)
        comb_T = qT[0:EXPERTS, 4 * S:5 * S]
        logit_m = sb("logit_m", [P, TT])
        def small(z, n):
            return dots[:, M_N + P * z:M_N + P * z + TT * n].rearrange("p (t e) -> p t e", t=TT)

        logits, comb, top_e, rest_e = small(0, EXPERTS), small(1, EXPERTS), small(2, 8), small(3, EXPERTS + PAD_E)
        gates_e = sb("gates_e", [P, TT, EXPERTS + PAD_E])
        sum_e = sb("sum_e", [P, TT])
        rec_e = sb("rec_e", [P, TT])

        banks_a = [ctx.enter_context(nc.psum_tensor(f"pa{i}", [P, 512], F32)) for i in range(2)]
        banks_o = [ctx.enter_context(nc.psum_tensor(f"po{i}", [P, 512], F32)) for i in range(2)]
        banks_m = [ctx.enter_context(nc.psum_tensor(f"pm{i}", [P, 512], F32)) for i in range(2)]
        banks_t = [ctx.enter_context(nc.psum_tensor(f"pt{i}", [P, 512], F32)) for i in range(2)]
        def scores_keys():
            a = []
            for s in range(-1, STEPS + 3):
                for what in ahead(s):
                    if what[0] != "qk":
                        a += [what + (z,) for z in range(2)]
                    else:
                        a += [what + (z,) for z in range(len(pieces(MEM + P * (what[1] + 1))))]
                if s >= 3 and has_tail(s - 3):
                    a.append(("tail", s - 3))
            o = [x for r in range(S // RB) for x in [("av", r)] + ([("wo", r // 2)] if r % 2 else [])]
            m = [("mix", i, z) for i in range(SUBS) for z in range(len(pieces(width(SEQ[i]))))]
            return a, o, m, [("post", i) for i in range(SUBS)]

        def has_tail(s):
            return SEQ[PAIR * s] % PER_TILE >= PER_TILE - GROUP

        KEYS = scores_keys()
        FRONT_A = (["v"] + [("st", h, k) for h in range(H0) for k in range(TT)] + ["x1T"]
                   + [("f1", k) for k in range(KC)] + [("h1", k) for k in range(KC)] + [("h2", k) for k in range(KC)] + ["x2T"]
                   + [("k", k) for k in range(NC)] + [("q", k) for k in range(NC)] + ["ks", "qs"])
        S_FIRST = [(i, h) for i in range(TT) for h in range(HS)]
        S_SECOND = [(i, h) for i in range(TT) for h in range(HS, H0)]
        START_O = ["rq", "rqs", "rk", "rks"]
        FRONT_O = ([("s",) + k for k in S_FIRST] + [("mT", 0)] + [("s",) + k for k in S_SECOND] + [("mT", 1)]
                   + [("den", 0), ("den", 1), "y0"]
                   + [("f2", k) for k in range(KC)] + ["y1"] + [("kinv", 0), ("kinv", 1), "qnorm"] + [("kinv", k) for k in range(2, NC)])
        EXPERTS_A = ["x3T"] + [("m1", k) for k in range(MC + 1)]
        EXPERTS_O = ["lg", "cT"] + [x for k in range(MC + 1) for x in [("m3", k)] + ([("cb", k)] if k < MC else [])] + ["y3"]
        RINGS = [Ring(FRONT_A + KEYS[0]), Ring(FRONT_O + KEYS[1] + ["bad"]), Ring(KEYS[2]), Ring(KEYS[3])]
        RINGS_AGAIN = [Ring(k) for k in KEYS]
        RING_START = Ring(START_O)
        RINGS_EXPERTS = [Ring(EXPERTS_A), Ring(START_O + EXPERTS_O)]

        w_in = sem("w_in")
        init_done = sem("init_done")
        pre_done = sem("pre_done")
        x_in = sem("x_in")
        a_full, a_free = sem("a_full"), sem("a_free")
        o_full, o_free = sem("o_full"), sem("o_free")
        m_full, m_free = sem("m_full"), sem("m_free")
        t_full, t_free = sem("t_full"), sem("t_free")
        v_chain = sem("v_chain")
        g_chain = sem("g_chain")
        rot_done = sem("rot_done")
        parts_done = sem("parts_done")
        parts_out = sem("parts_out")
        stack_in = sem("stack_in")
        rows_done = sem("rows_done")
        rows_out = sem("rows_out")
        rows_in = sem("rows_in")
        av0_done = sem("av0_done")
        sums_done = sem("sums_done")
        out0_done = sem("out0_done")
        var_done = sem("var_done")
        rstd_done = sem("rstd_done")
        x1_done, x2_done, x3_done, x4_done = (sem(f"x{i}_done") for i in range(1, 5))
        ffn_in = sem("ffn_in")
        moe_in = sem("moe_in")
        k_sq = sem("k_sq")
        k_summed = sem("k_summed")
        kinv_done = sem("kinv_done")
        spread_in = sem("spread_in")
        q_sq = sem("q_sq")
        q_summed = sem("q_summed")
        rq_done = sem("rq_done")
        mix_in = [sem(f"mix_in{i}") for i in range(MIX_SLOTS)]
        zero_done = sem("zero_done")
        negm_done = sem("negm_done")
        moments_done = sem("moments_done")
        thr_ready = sem("thr_ready")
        thr_done = [sem(f"thr_done{r}") for r in range(COUNTS)]
        worst_done = sem("worst_done")
        counted = [sem(f"counted{r}") for r in range(COUNTS)]
        ex_done = sem("ex_done")
        summed = sem("summed")
        attn_done = sem("attn_done")
        og_done = sem("og_done")
        ex_e_done = sem("ex_e_done")
        comb_done = sem("comb_done")
        y_out = sem("y_out")

        class Chain:

            def __init__(self, eng, s):
                self.eng, self.sem, self.n = eng, s, 0

            def mark(self, ins):
                self.n += 1
                ins.then_inc(self.sem, 1)
                return self.n

            def after(self, n):
                self.eng.wait_ge(self.sem, n)

            def link(self, ins):
                self.after(self.mark(ins))

        with nc.Block() as block:
            @block.sync
            def _(sp):
                sp.dma_start(wts[:, :], w_d).then_inc(w_in, 16)
                sp.dma_start(cst[:, :], c_d).then_inc(w_in, 16)
                sp.dma_start(dots[:, 0:CB_N + 2 * P], cb_d).then_inc(w_in, 16)
                sp.dma_start(memv[:, :], memv_d).then_inc(w_in, 16)

            @block.gpsimd
            def _(pool):
                nc.gpsimd.memset(xe[:, 0:MEM], 0.0)
                nc.gpsimd.memset(powers[:, 0:TT], -0.5)
                nc.gpsimd.memset(powers[:, TT:TT + PAIR], 0.5)
                nc.gpsimd.memset(powers[:, TT + PAIR:], -1.0)
                nc.gpsimd.memset(gates_e[:, :, :], -1.0).then_inc(init_done, 1)
                pool.wait_ge(w_in, 64)
                nc.gpsimd.tensor_tensor(sq[:, 0, 0:NC * MEM], w("memk"), w("memk"), ALU.mult).then_inc(pre_done, 1)

            @block.tensor
            def _(pe):
                pe.wait_ge(w_in, 64)
                pe.wait_ge(pre_done, 1)
                nc.tensor.matmul(banks_a[0][:, 0:NC * MEM], c("heads"), sq[:, 0, 0:NC * MEM], start=True,
                                 stop=True).then_inc(a_full, 1)

            @block.scalar
            def _(act):
                act.wait_ge(a_full, 1)
                nc.scalar.activation(nr[:, 0, 0:NC * MEM], banks_a[0][:, 0:NC * MEM], ACT.Sqrt).then_inc(a_free, 1)

            @block.vector
            def _(dve):
                chain = Chain(dve, v_chain)
                dve.wait_ge(w_in, 64)
                nc.vector.tensor_copy(cstb[:, :], dots[:, 0:CB_N])
                nc.vector.tensor_tensor(pre_b[:, :], w("pre"), dots[:, CB_N:CB_N + P], ALU.mult)
                nc.vector.tensor_scalar(w("bg"), w("bg"), 0.5, None, ALU.mult)
                chain.link(nc.vector.tensor_tensor(post_b[:, :], w("post"), dots[:, CB_N + P:CB_N + 2 * P], ALU.mult))
                nc.vector.scalar_tensor_tensor(out=post_b[:, :], in0=post_b[:, :], scalar=0.5, in1=w("hs"), op0=ALU.mult, op1=ALU.mult)
                dve.wait_ge(a_free, 1)
                n = nr[:, 0, 0:NC * MEM]
                chain.link(nc.vector.tensor_scalar(n, n, 1e-12, None, ALU.max))
                chain.link(nc.vector.reciprocal(n, n))
                chain.link(nc.vector.tensor_tensor(memk_n[:, :], w("memk"), n, ALU.mult))

        def clear_semaphores():
            for s in sems:
                nc.sync.sem_clear(s)
            nc.all_engine_barrier()

        clear_semaphores()

        def empty_banks(pe, A, O):
            def a_bank(key):
                if A.nth(key) > 2:
                    pe.wait_ge(a_free, A.nth(key) - 2)
                return banks_a[A.bank(key)]

            def o_bank(key):
                if O.nth(key) > 2:
                    pe.wait_ge(o_free, O.nth(key) - 2)
                return banks_o[O.bank(key)]

            return a_bank, o_bank

        def turned(bank, src):
            for t in range(TT):
                ins = nc.tensor.transpose(bank[:, P * t:P * t + P], src[:, t, :], ident)
            ins.then_inc(a_full, 1)

        def inverse_root(pool, k):
            pool.wait_ge(var_done, k + 1)
            nc.gpsimd.tensor_tensor(rstd[:, :], var[:, :], powers[:, 0:TT], ALU.pow).then_inc(rstd_done, 1)

        def norm(dve, chain, k, dst, done):
            for t in range(TT):
                ins = nc.vector.bn_stats(stats[:, t], res[:, t])
            chain.link(ins)
            for t in range(TT):
                ins = nc.vector.bn_aggr(mv[:, t], stats[:, t])
            chain.link(ins)
            nc.vector.tensor_scalar(var[:, :], mv[:, :, 1], EPS, None, ALU.add).then_inc(var_done, 1)
            dve.wait_ge(rstd_done, k + 1)
            for t in range(TT):
                ins = nc.vector.tensor_scalar(dst[:, t], res[:, t], mv[:, t, 0:1], rstd[:, t:t + 1], ALU.subtract, ALU.mult)
            ins.then_inc(done, 1)
            dve.wait_ge(done, 1)

        def rows(bank):
            return bank[:, :].rearrange("p (t d) -> p t d", t=TT)

        def pair_of(s):
            return [(z, PAIR * s + z, SEQ[PAIR * s + z]) for z in range(PAIR)]

        def last_piece(n):
            return len(pieces(width(n))) - 1

        SEARCHED = [s for s in range(STEPS) if narrow(SEQ[PAIR * s])]

        def searched(s, full):
            return not full and s in SEARCHED

        def scores_sync(sp, R):
            A, O, M, T = R
            for m, n in enumerate(SEQ):
                t, u = divmod(n, PER_TILE)
                wt, wn = MEM + P * (t + 1), width(n)
                if u == 0:
                    sp.wait_ge(a_free, A.nth(("qk", t, H1 - 1, len(pieces(wt)) - 1)))
                if m >= MIX_SLOTS:
                    sp.wait_ge(m_full, M.nth(("mix", m - MIX_SLOTS, last_piece(SEQ[m - MIX_SLOTS]))))
                tile = dots[R8 * u:R8 * u + R8, SCORES_AT[t]:SCORES_AT[t] + H1 * wt].rearrange("p (g j) -> p g j", g=H1)
                sp.dma_start(mixin[:, m % MIX_SLOTS, 0:wn], tile[:, :, 0:wn]).then_inc(mix_in[m % MIX_SLOTS], 16)

        def scores_gpsimd(pool, chain, R, full):
            nc.gpsimd.memset(attn[:, :, :], 0.0).then_inc(zero_done, 1)

            def scale(s):
                pool.wait_ge(summed, s + 1)
                p = s % LIVE
                if searched(s, full):
                    chain.link(nc.gpsimd.tensor_scalar(ssum[:, p], ssum[:, p], 0.5, None, ALU.max))
                chain.link(nc.gpsimd.tensor_tensor(rsum[:, p], ssum[:, p], powers[:, TT + PAIR:], ALU.pow))
                if PAIR * s >= A_SLOTS:
                    before = s - A_SLOTS // PAIR
                    pool.wait_ge(t_full, R[3].nth(("post", PAIR * before + PAIR - 1)))
                    if has_tail(before):
                        pool.wait_ge(a_full, R[0].nth(("tail", before)))
                for z, m, n in pair_of(s):
                    nc.gpsimd.tensor_scalar(wsc[:, m % A_SLOTS], post_b[:, :], rsum[:, p, z:z + 1], 1.0, ALU.mult, ALU.mult).then_inc(attn_done, 1)

            def first_threshold(s):
                q, p, n = SEARCHED.index(s), s % LIVE, SEQ[PAIR * s]
                pool.wait_ge(moments_done, q + 1)
                chain.link(nc.gpsimd.tensor_tensor(spread_[:, p], meanvar[:, p, :, 1], powers[:, TT:TT + PAIR], ALU.pow))
                nc.gpsimd.tensor_tensor(slope_[:, p], spread_[:, p], c("slope")[:, n:n + PAIR], ALU.mult)
                chain.link(nc.gpsimd.tensor_tensor(shift[:, p], spread_[:, p], c("first")[:, n:n + PAIR], ALU.mult))
                nc.gpsimd.tensor_tensor(thr[:, p], meanvar[:, p, :, 0], shift[:, p], ALU.add).then_inc(thr_ready, 1)

            def corrected(s, r):
                q, p, n = SEARCHED.index(s), s % LIVE, SEQ[PAIR * s]
                pool.wait_ge(counted[r], q + 1)
                chain.link(nc.gpsimd.tensor_scalar(shift[:, p], signs[:, p], 2 * AIM - width(n), DAMP[r], ALU.add, ALU.mult))
                chain.link(nc.gpsimd.tensor_tensor(shift[:, p], shift[:, p], slope_[:, p], ALU.mult))
                nc.gpsimd.tensor_tensor(thr[:, p], thr[:, p], shift[:, p], ALU.add).then_inc(thr_done[r], 1)

            for s in range(STEPS + 2):
                if s >= 2 and searched(s - 2, full):
                    corrected(s - 2, 2)
                if 1 <= s <= STEPS and searched(s - 1, full):
                    corrected(s - 1, 0)
                if s < STEPS and searched(s, full):
                    first_threshold(s)
                if 1 <= s <= STEPS and searched(s - 1, full):
                    corrected(s - 1, 1)
                if s >= 2:
                    scale(s - 2)

        def scores_tensor(pe, R, full):
            A, O, M, T = R
            a_bank, o_bank = empty_banks(pe, A, O)

            def gates_and_heads(s):
                for what in ahead(s):
                    t = what[1]
                    if what[0] == "vx":
                        rows = slice(P * t, min(P * t + P, J))
                        for z in range(2):
                            bank = a_bank(("vx", t, z))[0:rows.stop - rows.start, :]
                            half = slice(512 * z, 512 * z + 512)
                            ins = nc.tensor.matmul(bank, xe[:, rows], w("Wv")[:, half], start=True, stop=t > 0)
                            if t == 0:
                                ins = nc.tensor.matmul(bank, ident[0:MEM, :], memv[:, half], start=False, stop=True)
                            ins.then_inc(a_full, 1)
                    elif what[0] == "g":
                        rows = slice(MEM + P * t, MEM + P * t + P)
                        for z in range(2):
                            bank = a_bank(("g", t, z))
                            for k in range(NC // 2):
                                kk = NC // 2 * z + k
                                ins = nc.tensor.matmul(bank[:, P * k:P * k + P], w("Wg")[:, P * kk:P * kk + P], xe[:, rows],
                                                       start=True, stop=True)
                            ins.then_inc(a_full, 1)
                    else:
                        g = what[2]
                        at = HD1 * (g % 2)
                        if s < 0 and not full:
                            pe.wait_ge(o_free, O.nth(("kinv", g // 2)))
                        for z, (j0, jn) in enumerate(pieces(MEM + P * (t + 1))):
                            nc.tensor.matmul(a_bank(("qk", t, g, z))[:, 0:jn], qT_v[at:at + HD1, g // 2, P * t:P * t + P],
                                             kT_v[at:at + HD1, g // 2, j0:j0 + jn], start=True, stop=True).then_inc(a_full, 1)

            def mix(m, n):
                pe.wait_ge(mix_in[m % MIX_SLOTS], 16 * (m // MIX_SLOTS + 1))
                for z, (j0, jn) in enumerate(pieces(width(n))):
                    last = z == last_piece(n)
                    if M.nth(("mix", m, z)) > 2:
                        pe.wait_ge(m_free, M.nth(("mix", m, z)) - 2)
                    bank = banks_m[M.bank(("mix", m, z))]
                    ins = nc.tensor.matmul(bank[:, 0:jn], pre_b[:, :], mixin[:, m % MIX_SLOTS, j0:j0 + jn], start=True, stop=not last)
                    if last:
                        ins = nc.tensor.matmul(bank[:, jn - GROUP * R8:jn], identb, mix_mask[:, n % GROUP], start=False, stop=True)
                    ins.then_inc(m_full, 1)

            def post(s):
                for z, m, n in pair_of(s):
                    pe.wait_ge(attn_done, m + 1)
                    if T.nth(("post", m)) > 2:
                        pe.wait_ge(t_free, T.nth(("post", m)) - 2)
                    bank = banks_t[T.bank(("post", m))]
                    for k in range(n // PER_TILE + 1):
                        ins = nc.tensor.matmul(bank[:, P * k:P * k + P], attn[:, m % A_SLOTS, P * k:P * k + P], wsc[:, m % A_SLOTS],
                                               start=True, stop=True)
                    ins.then_inc(t_full, 1)
                if has_tail(s):
                    bank = a_bank(("tail", s))
                    for z, m, n in pair_of(s):
                        j0 = P * (n // PER_TILE + 1)
                        ins = nc.tensor.matmul(bank[0:MEM, P * z:P * z + P], attn[:, m % A_SLOTS, j0:j0 + MEM], wsc[:, m % A_SLOTS],
                                               start=True, stop=True)
                    ins.then_inc(a_full, 1)

            def values(r):
                t, odd = divmod(SEQ[PER_BLOCK * r] // PER_BLOCK, 2)
                pe.wait_ge(t_free, T.nth(("post", PER_BLOCK * r + PER_BLOCK - 1)))
                if odd:
                    pe.wait_ge(a_free, A.nth(("tail", STEPS_BLOCK * (r + 1) - 1)))
                if r == 0:
                    pe.wait_ge(a_free, A.nth(("vx", TT, 1)))
                bank = o_bank(("av", r))
                for h in range(H1):
                    at, col = HD1 * (h % 2), RB * (h // 2)
                    for k in range(t + 1):
                        ins = nc.tensor.matmul(bank[at:at + HD1, col:col + RB], vx_v[:, k, HD1 * h:HD1 * h + HD1], at_v[:, k, h, :],
                                               start=k == 0, stop=k == t and not odd)
                    if odd:
                        ins = nc.tensor.matmul(bank[at:at + HD1, col + RB // 2:col + RB], vx_v[0:MEM, t + 1, HD1 * h:HD1 * h + HD1],
                                               tail[:, h, :], start=False, stop=True)
                ins.then_inc(o_full, 1)

            def project(o):
                pe.wait_ge(o_free, O.nth(("av", 2 * o + 1)))
                bank = o_bank(("wo", o))
                for k in range(NC):
                    ins = nc.tensor.matmul(bank[:, 0:P], og[:, k, :], w("Wo")[:, P * k:P * k + P], start=k == 0, stop=k == NC - 1)
                ins.then_inc(o_full, 1)

            gates_and_heads(-1)
            for s in range(-1, STEPS + STEPS_BLOCK + 2):
                first = s + 1 < STEPS and last_piece(SEQ[PAIR * (s + 1)]) == 0
                if s >= 0 and not first:
                    gates_and_heads(s)
                if s + 1 < STEPS:
                    for z, m, n in pair_of(s + 1):
                        mix(m, n)
                if s >= 0 and first:
                    gates_and_heads(s)
                if s >= STEPS_BLOCK + 3 and (s - 3) % STEPS_BLOCK == 0:
                    values((s - 3) // STEPS_BLOCK - 1)
                if 3 <= s < STEPS + 3:
                    post(s - 3)
                if s > STEPS_TILE and (s - 5) % STEPS_TILE == 0:
                    project((s - 5) // STEPS_TILE - 1)

        def scores_scalar(act, R, full):
            A, O, M, T = R

            def gates(t):
                o = TILE_ORDER.index(t)
                if o:
                    act.wait_ge(o_free, O.nth(("av", 2 * o - 1)))
                for z in range(2):
                    act.wait_ge(a_full, A.nth(("g", t, z)))
                    bank = banks_a[A.bank(("g", t, z))]
                    for k in range(NC // 2):
                        kk = NC // 2 * z + k
                        ins = nc.scalar.activation(gate[:, kk], bank[:, P * k:P * k + P], ACT.Tanh, scale=0.5, bias=w("bg")[:, kk:kk + 1])
                    ins.then_inc(a_free, 1)

            def values(k):
                rows = min(P, J - P * k)
                for z in range(2):
                    act.wait_ge(a_full, A.nth(("vx", k, z)))
                    nc.scalar.copy(vx_v[0:rows, k, 512 * z:512 * z + 512], banks_a[A.bank(("vx", k, z))][0:rows, :]).then_inc(a_free, 1)

            def head(t, g):
                o = TILE_ORDER.index(t)
                wt = MEM + P * (t + 1)
                if g == 0 and o:
                    for s in mix_in:
                        act.wait_ge(s, 16 * max(o - 1, 1) * PER_TILE // MIX_SLOTS)
                for z, (j0, jn) in enumerate(pieces(wt)):
                    key = ("qk", t, g, z)
                    act.wait_ge(a_full, A.nth(key))
                    at = SCORES_AT[t] + g * wt + j0
                    nc.scalar.activation(dots[:, at:at + jn], banks_a[A.bank(key)][:, 0:jn], ACT.Copy,
                                         scale=rq[:, t, g:g + 1]).then_inc(a_free, 1)

            def gates_and_heads(s):
                for what in ahead(s):
                    if what[0] == "g":
                        gates(what[1])
                    elif what[0] == "vx":
                        values(what[1])
                    else:
                        head(what[1], what[2])

            def mixed(s):
                if PAIR * s >= X_SLOTS:
                    act.wait_ge(summed, s + 1 - X_SLOTS // PAIR)
                for y, m, n in pair_of(s):
                    for z, (j0, jn) in enumerate(pieces(width(n))):
                        act.wait_ge(m_full, M.nth(("mix", m, z)))
                        nc.scalar.copy(xs[m % X_SLOTS][:, j0:j0 + jn], banks_m[M.bank(("mix", m, z))][:, 0:jn]).then_inc(m_free, 1)

            def count(s, r):
                q = SEARCHED.index(s)
                act.wait_ge(thr_done[r - 1] if r else thr_ready, q + 1)
                if r == 0 and PAIR * s >= E1_SLOTS:
                    act.wait_ge(summed, s + 1 - E1_SLOTS // PAIR)
                for z, m, n in pair_of(s):
                    ins = nc.scalar.activation(ex[m % E1_SLOTS][:, 0:width(n)], xs[m % X_SLOTS][:, 0:width(n)], ACT.Sign, scale=-1.0,
                                               bias=thr[:, s % LIVE, z:z + 1], accum_out=signs[:, s % LIVE, z:z + 1])
                ins.then_inc(counted[r], 1)

            def exponentials(s):
                act.wait_ge(negm_done, s + 1)
                if searched(s, full):
                    act.wait_ge(thr_done[-1], SEARCHED.index(s) + 1)
                elif PAIR * s >= E1_SLOTS:
                    act.wait_ge(summed, s + 1 - E1_SLOTS // PAIR)
                for z, m, n in pair_of(s):
                    nc.scalar.activation(ex[m % E1_SLOTS][:, 0:width(n)], xs[m % X_SLOTS][:, 0:width(n)], ACT.Exp,
                                         bias=negm[:, s % LIVE, z:z + 1]).then_inc(ex_done, 1)

            def posted(s):
                r = s // STEPS_BLOCK
                if s % STEPS_BLOCK == 0 and r:
                    act.wait_ge(o_full, O.nth(("av", r - 1)))
                for z, m, n in pair_of(s):
                    t, u = n // PER_TILE, n % PER_BLOCK
                    act.wait_ge(t_full, T.nth(("post", m)))
                    bank = banks_t[T.bank(("post", m))]
                    nc.scalar.copy(at_v[:, 0:t + 1, :, R8 * u:R8 * u + R8],
                                   bank[:, 0:P * (t + 1)].rearrange("p (k h i) -> p k h i", k=t + 1, h=H1)).then_inc(t_free, 1)
                if has_tail(s):
                    act.wait_ge(a_full, A.nth(("tail", s)))
                    bank = banks_a[A.bank(("tail", s))]
                    v = R8 * (SEQ[PAIR * s] % GROUP)
                    nc.scalar.copy(tail[:, :, v:v + PAIR * R8].rearrange("p h (z i) -> p z h i", z=PAIR),
                                   bank[0:MEM, 0:PAIR * P].rearrange("p (z h i) -> p z h i", z=PAIR, h=H1)).then_inc(a_free, 1)

            gates_and_heads(-1)
            for s in range(STEPS + 4):
                if s < STEPS:
                    mixed(s)
                if 2 <= s < STEPS + 2 and searched(s - 2, full):
                    count(s - 2, 2)
                if 1 <= s <= STEPS and searched(s - 1, full):
                    count(s - 1, 0)
                if s >= 4:
                    posted(s - 4)
                if 2 <= s < STEPS + 2:
                    exponentials(s - 2)
                gates_and_heads(s)
                if 1 <= s <= STEPS and searched(s - 1, full):
                    count(s - 1, 1)

        def scores_vector(dve, chain, R, full):
            A, O, M, T = R

            def maxima(s):
                p, search = s % LIVE, searched(s, full)
                for z, m, n in pair_of(s):
                    dve.wait_ge(m_free, M.nth(("mix", m, last_piece(n))))
                    found = chain.mark(nc.vector.max(out=top[:, p, z], in_=xs[m % X_SLOTS][:, 0:width(n)]))
                    if search:
                        seen = chain.mark(nc.vector.bn_stats(moments[:, p, z], xs[m % X_SLOTS][:, 0:width(n) - GROUP * R8:2]))
                chain.after(found)
                nc.vector.tensor_scalar(negm[:, p], top[:, p, :, 0], -1.0, None, ALU.mult).then_inc(negm_done, 1)
                if search:
                    chain.after(seen)
                    for z in range(PAIR):
                        ins = nc.vector.bn_aggr(meanvar[:, p, z], moments[:, p, z])
                    ins.then_inc(moments_done, 1)

            def in_turn(s):
                wn = width(SEQ[PAIR * s])
                src = [xs[m % X_SLOTS][:, 0:wn] for z, m, n in pair_of(s)]
                t8 = [top[:, s % LIVE, z] for z in range(PAIR)]
                done = [None] * PAIR
                for _ in range(ROUNDS - 1):
                    for z in range(PAIR):
                        if done[z]:
                            chain.after(done[z])
                        done[z] = chain.mark(nc.vector.match_replace(out=left[z][:, 0:wn], in_to_replace=t8[z], in_values=src[z], imm_value=LOWEST))
                        src[z], t8[z] = left[z][:, 0:wn], best[:, z, 0:8]
                    for z in range(PAIR):
                        chain.after(done[z])
                        done[z] = chain.mark(nc.vector.max(out=t8[z], in_=src[z]))
                chain.after(done[-1])
                return [best[:, z, 7:8] for z in range(PAIR)]

            def near_threshold(s):
                wn = width(SEQ[PAIR * s])
                dve.wait_ge(thr_done[-1], SEARCHED.index(s) + 1)
                done = [None] * PAIR
                for z, m, n in pair_of(s):
                    done[z] = chain.mark(nc.vector.tensor_scalar(left[z][:, 0:wn], xs[m % X_SLOTS][:, 0:wn], thr[:, s % LIVE, z:z + 1], None,
                                                                 ALU.is_gt, ALU.add, accum_out=above[:, n:n + 1]))
                for z, m, n in pair_of(s):
                    chain.after(done[z])
                    done[z] = chain.mark(nc.vector.scalar_tensor_tensor(out=left[z][:, 0:wn], in0=left[z][:, 0:wn], scalar=LOWEST,
                                                                        in1=xs[m % X_SLOTS][:, 0:wn], op0=ALU.mult, op1=ALU.add))
                for k in range(WINDOW // 8):
                    for z in range(PAIR):
                        chain.after(done[z])
                        done[z] = chain.mark(nc.vector.max(out=best[:, z, 8 * k:8 * k + 8], in_=left[z][:, 0:wn]))
                    if k < WINDOW // 8 - 1:
                        for z in range(PAIR):
                            chain.after(done[z])
                            done[z] = chain.mark(nc.vector.match_replace(out=left[z][:, 0:wn], in_to_replace=best[:, z, 8 * k:8 * k + 8],
                                                                         in_values=left[z][:, 0:wn], imm_value=LOWEST))
                for z, m, n in pair_of(s):
                    chain.after(done[z])
                    done[z] = chain.mark(nc.vector.scalar_tensor_tensor(out=picked[:, z], in0=c("rank"), scalar=above[:, n:n + 1], in1=best[:, z],
                                                                        op0=ALU.is_equal, op1=ALU.mult, accum_out=bound[:, z:z + 1]))
                chain.after(done[-1])
                return [bound[:, z:z + 1] for z in range(PAIR)]

            def select(s):
                if searched(s, full):
                    bounds = near_threshold(s)
                else:
                    bounds = in_turn(s) if width(SEQ[PAIR * s]) >= TOPK else [LOWEST] * PAIR
                for z, m, n in pair_of(s):
                    wn = width(n)
                    dve.wait_ge(ex_done, m + 1)
                    if m >= A_SLOTS:
                        before = m - A_SLOTS
                        dve.wait_ge(t_full, T.nth(("post", before)))
                        if has_tail(before // PAIR):
                            dve.wait_ge(a_full, A.nth(("tail", before // PAIR)))
                    full_width = MEM + P * (n // PER_TILE + 1)
                    if m >= PER_TILE and wn < full_width:
                        nc.vector.memset(attn[:, m % A_SLOTS, wn:full_width], 0.0)
                    ins = nc.vector.scalar_tensor_tensor(out=attn[:, m % A_SLOTS, 0:wn], in0=xs[m % X_SLOTS][:, 0:wn], scalar=bounds[z],
                                                         in1=ex[m % E1_SLOTS][:, 0:wn], op0=ALU.is_ge, op1=ALU.mult,
                                                         accum_out=ssum[:, s % LIVE, z:z + 1])
                ins.then_inc(summed, 1)

            def gated_rows(r):
                o, odd = divmod(r, 2)
                dve.wait_ge(o_full, O.nth(("av", r)))
                dve.wait_ge(a_free, A.nth(("g", TILE_ORDER[o], 1)))
                bank = banks_o[O.bank(("av", r))]
                nc.vector.scalar_tensor_tensor(out=og[:, :, RB * odd:RB * odd + RB], in0=gate[:, :, RB * odd:RB * odd + RB], scalar=1.0,
                                               in1=bank[:, :].rearrange("p (c i) -> p c i", c=NC), op0=ALU.add, op1=ALU.mult).then_inc(o_free, 1)

            def residual(o):
                t = TILE_ORDER[o]
                dve.wait_ge(o_full, O.nth(("wo", o)))
                nc.vector.tensor_tensor(res[:, t], banks_o[O.bank(("wo", o))][:, 0:P], x2[:, t], ALU.add).then_inc(o_free, 1)

            dve.wait_ge(zero_done, 1)
            for s in range(STEPS + STEPS_BLOCK + 3):
                if s < STEPS:
                    maxima(s)
                if 2 <= s < STEPS + 2:
                    select(s - 2)
                if s >= STEPS_BLOCK + 4 and (s - 4) % STEPS_BLOCK == 0:
                    gated_rows((s - 4) // STEPS_BLOCK - 1)
                if s > STEPS_TILE and (s - 6) % STEPS_TILE == 0:
                    residual((s - 6) // STEPS_TILE - 1)

        def start_sync(sp, b):
            sp.dma_start(xT, xT_d[b]).then_inc(x_in, 16)
            sp.dma_start(x0, x_d[b].rearrange("p (t d) -> p t d", t=TT)).then_inc(x_in, 16)

        def stack_sync(sp):
            for z, (stack, slots) in enumerate(((q_stack, Q_PARTS), (k_stack, K_PARTS))):
                sp.wait_ge(parts_done, z + 1)
                sp.dma_start(parts_d[z], parts[:, z].rearrange("p k s -> p (k s)")).then_inc(parts_out, 16)
                sp.wait_ge(parts_out, 16 * (z + 1))
                for slot, part in enumerate(slots):
                    heads = parts_d[z][:, part * S:(part + 1) * S].rearrange("(a h d) s -> h d a s", h=2, d=HD0)
                    for hp in range(2):
                        at = RB * hp + HD0 * slot
                        sp.dma_start(stack[at:at + HD0], heads[hp]).then_inc(stack_in, 16)
            sp.wait_ge(stack_in, 16 * 4 * SLOTS)

        def start_gpsimd(chain, pool):
            for z in range(2):
                pool.wait_ge(rot_done, z + 1)
                chain.link(nc.gpsimd.tensor_copy(parts[:, z, 0], rot[:, z]))
                chain.link(nc.gpsimd.tensor_tensor(part_t, rot[:, z], parts[:, z, 0], ALU.subtract))
                chain.link(nc.gpsimd.tensor_copy(parts[:, z, 1], part_t))
                chain.link(nc.gpsimd.tensor_tensor(part_t, part_t, parts[:, z, 1], ALU.subtract))
                nc.gpsimd.tensor_copy(parts[:, z, 2], part_t).then_inc(parts_done, 1)

        def start_tensor(pe, o_bank):
            pe.wait_ge(x_in, 32)
            for key, name in (("rq", "wq"), ("rqs", "wqs"), ("rk", "wk"), ("rks", "wks")):
                nc.tensor.matmul(o_bank(key)[:, :], w(name), xT[:, :], start=True, stop=True).then_inc(o_full, 1)

        def start_vector(dve, filled, O):
            for z, (k0, k1) in enumerate((("rq", "rqs"), ("rk", "rks"))):
                bank = filled(k0)
                if z:
                    dve.wait_ge(rot_done, z)
                nc.vector.tensor_tensor(rope_t[:, 0], bank[:, :], c("rope_c"), ALU.mult).then_inc(o_free, 1)
                bank = filled(k1)
                nc.vector.tensor_tensor(rope_t[:, 1], bank[:, :], c("rope_s"), ALU.mult).then_inc(o_free, 1)
                dve.wait_ge(o_free, O.nth(k1))
                nc.vector.tensor_tensor(rot[:, z], rope_t[:, 0], rope_t[:, 1], ALU.add).then_inc(rot_done, 1)

        def start(block):
            @block.sync
            def _(sp):
                start_sync(sp, 0)
                stack_sync(sp)

            @block.gpsimd
            def _(pool):
                nc.gpsimd.memset(k_stack, 1.0)
                start_gpsimd(Chain(pool, g_chain), pool)

            @block.tensor
            def _(pe):
                start_tensor(pe, empty_banks(pe, None, RING_START)[1])

            @block.vector
            def _(dve):
                def filled(key):
                    dve.wait_ge(o_full, RING_START.nth(key))
                    return banks_o[RING_START.bank(key)]

                start_vector(dve, filled, RING_START)

        def front(block):
            A, O, M, T = RINGS

            @block.sync
            def _(sp):
                sp.dma_start(spread_h, moe_d[0:H1, M_AT["spread"][0]:M_AT["spread"][1]]).then_inc(spread_in, 16)
                sp.dma_start(dots[:, 0:F1_N], ffn1_d).then_inc(ffn_in, 16)
                sp.dma_start(at2[:, 0:F2_N], ffn2_d).then_inc(ffn_in, 16)
                for g in range(SETS):
                    sp.wait_ge(rows_done, g + 1)
                    sp.dma_start(maxes_d[g], max_parts[:, g].rearrange("h k s -> h (k s)")).then_inc(rows_out, 16)
                    sp.wait_ge(rows_out, 16 * (g + 1))
                    rows = maxes_d[g].rearrange("(a h) (k s) -> h k a s", h=2, k=3)
                    for hp in range(2):
                        at = RB * hp + MAX_ROW
                        sp.dma_start(q_stack[at:at + 3, HS // 2 * g:HS // 2 * (g + 1)], rows[hp]).then_inc(rows_in, 16)
                scores_sync(sp, RINGS)

            @block.gpsimd
            def _(pool):
                chain = Chain(pool, g_chain)

                nc.gpsimd.memset(v_pad[:, :, :, SUM_COLS:2 * SUM_COLS], 0.0)
                nc.gpsimd.memset(v_pad[:, :, :, HD0:SUM_COLS], 1.0)
                nc.gpsimd.memset(v_pad[:, :, :, 2 * SUM_COLS + HD0:V_COLS], 1.0).then_inc(init_done, 1)
                inverse_root(pool, 0)
                inverse_root(pool, 1)
                for k in range(NC):
                    pool.wait_ge(a_free, A.nth(("q", k)))
                    if k >= Q_SLOTS:
                        pool.wait_ge(q_summed, k - Q_SLOTS + 1)
                    nc.gpsimd.tensor_tensor(squares_of("qs", k), qT_v[:, k, :], qT_v[:, k, :], ALU.mult).then_inc(q_sq, 1)

                scores_gpsimd(pool, chain, RINGS, False)

            @block.tensor
            def _(pe):
                a_bank, o_bank = empty_banks(pe, A, O)

                bank = a_bank("v")
                for t in range(TT):
                    ins = nc.tensor.matmul(bank[:, P * t:P * t + P], xT[:, P * t:P * t + P], w("wv"), start=True, stop=True)
                ins.then_inc(a_full, 1)
                def rows_scores(i, h):
                    bank = o_bank(("s", i, h))
                    at = RB * (h % 2)
                    nc.tensor.matmul(bank[:, 0:P * (i + 1)], q_stack[at:at + MAX_ROW, h // 2, P * i:P * i + P],
                                     k_stack[at:at + MAX_ROW, h // 2, 0:P * (i + 1)], start=True, stop=False)
                    nc.tensor.matmul(bank[:, P * i:P * i + P], identb, mask_s, start=False, stop=True).then_inc(o_full, 1)

                def maxima(g):
                    pe.wait_ge(o_free, O.nth(("s", TT - 1, HS * (g + 1) - 1)))
                    bank = o_bank(("mT", g))
                    for i in range(TT):
                        ins = nc.tensor.transpose(bank[0:HS, P * i:P * i + P], row_max[:, i, HS * g:HS * (g + 1)], ident)
                    ins.then_inc(o_full, 1)

                def columns_scores(h):
                    at = RB * (h % 2)
                    for k in range(TT):
                        bank = a_bank(("st", h, k))
                        nc.tensor.matmul(bank[:, 0:S - P * k], k_stack[at:at + STACK, h // 2, P * k:P * k + P],
                                         q_stack[at:at + STACK, h // 2, P * k:S], start=True, stop=False)
                        nc.tensor.matmul(bank[:, 0:P], identb, mask_t, start=False, stop=True).then_inc(a_full, 1)

                def values0(h):
                    pe.wait_ge(a_free, A.nth(("st", h, TT - 1)))
                    a, odd = divmod(h, 2)
                    at = 2 * SUM_COLS * (a % (HS // 2))
                    for k in range(TT):
                        ins = nc.tensor.matmul(banks_t[h // HS][at:at + 2 * SUM_COLS, P * k:S],
                                               v_pad[:, k, a, SUM_COLS * odd:SUM_COLS * odd + 2 * SUM_COLS],
                                               exps[:, h % E_SLOTS, E_OFF[k]:E_OFF[k] + S - P * k],
                                               start=not odd and k == 0, stop=odd == 1 and k == TT - 1)
                    ins.then_inc(av0_done, 1)

                def sums_beside(g):
                    pe.wait_ge(sums_done, g + 1)
                    nc.tensor.matmul(o_bank(("den", g))[:, :], c("sums"), sums_in[:, g], start=True, stop=True).then_inc(o_full, 1)

                for i, h in S_FIRST:
                    rows_scores(i, h)
                maxima(0)
                half = len(S_SECOND) // 2
                for i, h in S_SECOND[:half]:
                    rows_scores(i, h)
                pe.wait_ge(init_done, 1)
                for h in range(H0 + 1):
                    if h < H0:
                        if h % HS == 0:
                            pe.wait_ge(rows_in, 32 * (h // HS + 1))
                        columns_scores(h)
                    if h < HS // 2:
                        for i, h2 in S_SECOND[half + 4 * h:half + 4 * h + 4]:
                            rows_scores(i, h2)
                    if h == HS // 2:
                        maxima(1)
                    if h:
                        values0(h - 1)
                    if h == HS + 1:
                        sums_beside(0)
                sums_beside(1)
                pe.wait_ge(out0_done, SETS)
                bank = o_bank("y0")
                for t in range(TT):
                    for g in range(SETS):
                        ins = nc.tensor.matmul(bank[:, P * t:P * t + P], out0[:, g, P * t:P * t + P], w("wo0")[:, P * g:P * g + P],
                                               start=g == 0, stop=g == SETS - 1)
                ins.then_inc(o_full, 1)
                pe.wait_ge(x1_done, 1)
                turned(a_bank("x1T"), x1)

                pe.wait_ge(ffn_in, 32)
                pe.wait_ge(a_free, A.nth("x1T"))
                for k in range(KC):
                    nc.tensor.matmul(a_bank(("f1", k))[:, :], f1("w1")[:, P * k:P * k + P], xT1[:, :], start=True,
                                     stop=True).then_inc(a_full, 1)
                    nc.tensor.matmul(o_bank(("f2", k))[:, :], f1("w2")[:, P * k:P * k + P], xT1[:, :], start=True,
                                     stop=True).then_inc(o_full, 1)
                pe.wait_ge(o_free, O.nth(("f2", KC - 1)))

                def hidden(name, wgt, src):
                    for k in range(KC):
                        bank = a_bank((name, k))
                        for j in range(KC):
                            ins = nc.tensor.matmul(bank[:, :], wgt[:, HID0 * j + P * k:HID0 * j + P * k + P], src[:, j, :],
                                                   start=j == 0, stop=j == KC - 1)
                        ins.then_inc(a_full, 1)

                hidden("h1", f1("h1"), hid)
                pe.wait_ge(a_free, A.nth(("h1", KC - 1)))
                hidden("h2", f2("h2"), gelu1)
                pe.wait_ge(a_free, A.nth(("h2", KC - 1)))
                bank = o_bank("y1")
                for t in range(TT):
                    for j in range(KC):
                        ins = nc.tensor.matmul(bank[:, P * t:P * t + P], gelu2[:, j, P * t:P * t + P], f2("w3")[:, P * j:P * j + P],
                                               start=j == 0, stop=j == KC - 1)
                ins.then_inc(o_full, 1)
                pe.wait_ge(x2_done, 1)
                turned(a_bank("x2T"), x2)

                pe.wait_ge(a_free, A.nth("x2T"))
                for name in ("k", "q"):
                    for k in range(NC):
                        nc.tensor.matmul(a_bank((name, k))[:, :], w("W" + name)[:, P * k:P * k + P], xe[:, MEM:J], start=True,
                                         stop=True).then_inc(a_full, 1)
                for name, squared, summed_up in (("ks", k_sq, k_summed), ("qs", q_sq, q_summed)):
                    bank = a_bank(name)
                    for k in range(NC):
                        pe.wait_ge(squared, k + 1)
                        at = H1 - 2 - 2 * k
                        ins = nc.tensor.matmul(bank[0:H1, :], c("pick")[:, at:at + H1], squares_of(name, k), start=k == 0, stop=k == NC - 1)
                        ins.then_inc(summed_up if k < NC - 1 else a_full, 1)
                pe.wait_ge(spread_in, 16)
                pe.wait_ge(kinv_done, 1)

                def to_columns(k):
                    nc.tensor.matmul(o_bank(("kinv", k))[:, :], spread_h[:, P * k:P * k + P], k_norm, start=True, stop=True).then_inc(o_full, 1)

                to_columns(0)
                to_columns(1)
                pe.wait_ge(a_free, A.nth("qs"))
                bank = o_bank("qnorm")
                for t in range(TT):
                    ins = nc.tensor.transpose(bank[:, H1 * t:H1 * t + H1], q_norm[:, P * t:P * t + P], ident[0:H1, 0:H1])
                ins.then_inc(o_full, 1)
                for k in range(2, NC):
                    to_columns(k)

                scores_tensor(pe, RINGS, False)
                pe.wait_ge(worst_done, 1)
                nc.tensor.matmul(o_bank("bad")[0:1, 0:P], worst[:, :], ident, start=True, stop=True).then_inc(o_full, 1)

            @block.scalar
            def _(act):
                def filled(key):
                    act.wait_ge(a_full, A.nth(key))
                    return banks_a[A.bank(key)]

                def copied(key, dst, src=slice(0, 512)):
                    nc.scalar.copy(dst, filled(key)[:, src]).then_inc(a_free, 1)

                copied_v = filled("v")
                for odd in range(2):
                    ins = nc.scalar.copy(v_pad[:, :, :, 2 * SUM_COLS * odd:2 * SUM_COLS * odd + HD0],
                                         copied_v[:, :].rearrange("p (k a n) -> p k a n", k=TT, a=PAIRS)[:, :, :, HD0 * odd:HD0 * odd + HD0])
                ins.then_inc(a_free, 1)
                for h in range(H0):
                    if h >= E_SLOTS:
                        act.wait_ge(av0_done, h - E_SLOTS + 1)
                    for k in range(TT):
                        bank = filled(("st", h, k))
                        nc.scalar.activation(exps[:, h % E_SLOTS, E_OFF[k]:E_OFF[k] + S - P * k], bank[:, 0:S - P * k], ACT.Exp,
                                             scale=SCALE0).then_inc(a_free, 1)
                copied("x1T", xT1[:, :])
                for k in range(KC):
                    nc.scalar.activation(silu0[:, k], filled(("f1", k))[:, :], ACT.Silu, scale=w("w1s")[:, k:k + 1]).then_inc(a_free, 1)
                for k in range(KC):
                    nc.scalar.activation(gelu1[:, k], filled(("h1", k))[:, :], ACT.Gelu, scale=w("h1s")[:, k:k + 1]).then_inc(a_free, 1)
                for k in range(KC):
                    nc.scalar.activation(gelu2[:, k], filled(("h2", k))[:, :], ACT.Gelu, scale=w("h2s")[:, k:k + 1]).then_inc(a_free, 1)
                copied("x2T", xe[:, MEM:J])
                for k in range(NC):
                    copied(("k", k), kT_v[:, k, MEM:J])
                for k in range(NC):
                    copied(("q", k), qT_v[:, k, :])
                for name, dst in (("ks", k_norm), ("qs", q_norm)):
                    nc.scalar.activation(dst, filled(name)[0:H1, :], ACT.Sqrt).then_inc(a_free, 1)
                act.wait_ge(rq_done, 1)

                scores_scalar(act, RINGS, False)

            @block.vector
            def _(dve):
                chain = Chain(dve, v_chain)

                def filled(key):
                    dve.wait_ge(o_full, O.nth(key))
                    return banks_o[O.bank(key)]

                def split_maxima(g):
                    bank = filled(("mT", g))
                    nc.vector.tensor_scalar(neg_rows, bank[0:HS, :], -1.0, None, ALU.mult).then_inc(o_free, 1)
                    dve.wait_ge(o_free, O.nth(("mT", g)))
                    chain.link(nc.vector.tensor_copy(max_parts[:, g, 0], neg_rows))
                    chain.link(nc.vector.tensor_tensor(neg_left, neg_rows, max_parts[:, g, 0], ALU.subtract))
                    chain.link(nc.vector.tensor_copy(max_parts[:, g, 1], neg_left))
                    chain.link(nc.vector.tensor_tensor(neg_left, neg_left, max_parts[:, g, 1], ALU.subtract))
                    nc.vector.tensor_copy(max_parts[:, g, 2], neg_left).then_inc(rows_done, 1)

                for g, order in enumerate((S_FIRST, S_SECOND)):
                    for i, h in order:
                        bank = filled(("s", i, h))
                        nc.vector.tensor_reduce(row_max[:, i, h:h + 1], bank[:, 0:P * (i + 1)], X, ALU.max).then_inc(o_free, 1)
                    split_maxima(g)
                for g in range(SETS):
                    dve.wait_ge(av0_done, HS * (g + 1))
                    nc.vector.tensor_copy(sums_in[:, g], banks_t[g][:, :]).then_inc(sums_done, 1)
                    bank = filled(("den", g))
                    nc.vector.reciprocal(rec0, bank[:, :]).then_inc(o_free, 1)
                    dve.wait_ge(o_free, O.nth(("den", g)))
                    nc.vector.tensor_tensor(out0[:, g], sums_in[:, g], rec0, ALU.mult).then_inc(out0_done, 1)
                    dve.wait_ge(out0_done, g + 1)
                bank = filled("y0")
                nc.vector.tensor_tensor(res[:, :, :], rows(bank), x0[:, :, :], ALU.add).then_inc(o_free, 1)
                dve.wait_ge(o_free, O.nth("y0"))
                norm(dve, chain, 0, x1, x1_done)
                for k in range(KC):
                    bank = filled(("f2", k))
                    dve.wait_ge(a_free, A.nth(("f1", k)))
                    nc.vector.scalar_tensor_tensor(out=hid[:, k], in0=bank[:, :], scalar=w("w2s")[:, k:k + 1], in1=silu0[:, k],
                                                   op0=ALU.mult, op1=ALU.mult).then_inc(o_free, 1)
                bank = filled("y1")
                nc.vector.tensor_tensor(res[:, :, :], rows(bank), w("w3s").unsqueeze(1).to_broadcast([P, TT, D]),
                                        ALU.mult).then_inc(o_free, 1)
                dve.wait_ge(o_free, O.nth("y1"))
                chain.link(nc.vector.tensor_tensor(res[:, :, :], res[:, :, :], x1[:, :, :], ALU.add))
                norm(dve, chain, 1, x2, x2_done)
                nc.vector.tensor_copy(kT_v[:, :, 0:MEM], memk_n[:, :].rearrange("p (c m) -> p c m", c=NC))
                for k in range(NC):
                    dve.wait_ge(a_free, A.nth(("k", k)))
                    if k >= K_SLOTS:
                        dve.wait_ge(k_summed, k - K_SLOTS + 1)
                    nc.vector.tensor_tensor(squares_of("ks", k), kT_v[:, k, MEM:J], kT_v[:, k, MEM:J], ALU.mult).then_inc(k_sq, 1)
                dve.wait_ge(a_free, A.nth("ks"))
                chain.link(nc.vector.tensor_scalar(k_norm, k_norm, 1e-12, None, ALU.max))
                nc.vector.reciprocal(k_norm, k_norm).then_inc(kinv_done, 1)
                for k in range(NC):
                    bank = filled(("kinv", k))
                    nc.vector.tensor_tensor(kT_v[:, k, MEM:J], kT_v[:, k, MEM:J], bank[:, :], ALU.mult).then_inc(o_free, 1)
                    if k == 1:
                        r = rq[:, :, :].rearrange("p t h -> p (t h)")
                        bank = filled("qnorm")
                        nc.vector.tensor_scalar(r, bank[:, 0:TT * H1], 1e-12, None, ALU.max).then_inc(o_free, 1)
                        dve.wait_ge(o_free, O.nth("qnorm"))
                        chain.link(nc.vector.reciprocal(r, r))
                        nc.vector.tensor_scalar(r, r, QK_SCALE, None, ALU.mult).then_inc(rq_done, 1)
                nc.vector.memset(above[:, 0:NARROW_FROM], AIM)
                scores_vector(dve, chain, RINGS, False)
                chain.link(nc.vector.tensor_scalar(off[:, :], above[:, :], -AIM, None, ALU.add))
                chain.link(nc.vector.tensor_tensor(off[:, :], off[:, :], off[:, :], ALU.mult))
                nc.vector.tensor_reduce(worst[:, :], off[:, :], X, ALU.max).then_inc(worst_done, 1)
                bank = filled("bad")
                chain.link(nc.vector.tensor_reduce(flag_f[:, :], bank[0:1, 0:P], X, ALU.max))
                chain.link(nc.vector.tensor_scalar(flag[:, :], flag_f[:, :], (WINDOW / 2) ** 2, None, ALU.is_gt))

        def again(block):
            @block.sync
            def _(sp):
                scores_sync(sp, RINGS_AGAIN)

            @block.gpsimd
            def _(pool):
                scores_gpsimd(pool, Chain(pool, g_chain), RINGS_AGAIN, True)

            @block.tensor
            def _(pe):
                scores_tensor(pe, RINGS_AGAIN, True)

            @block.scalar
            def _(act):
                scores_scalar(act, RINGS_AGAIN, True)

            @block.vector
            def _(dve):
                scores_vector(dve, Chain(dve, v_chain), RINGS_AGAIN, True)

        def experts(b, block):
            A, O = RINGS_EXPERTS

            @block.sync
            def _(sp):
                start_sync(sp, b + 1)
                sp.dma_start(dots[:, 0:M_N], moe_d).then_inc(moe_in, 16)
                stack_sync(sp)
                sp.wait_ge(x4_done, 1)
                sp.dma_start(out_d[b].rearrange("(t p) d -> p t d", p=P), x4[:, :, :]).then_inc(y_out, 16)
                sp.wait_ge(y_out, 16)

            @block.gpsimd
            def _(pool):
                nc.gpsimd.memset(k_stack, 1.0)
                inverse_root(pool, 0)
                start_gpsimd(Chain(pool, g_chain), pool)
                inverse_root(pool, 1)

            @block.tensor
            def _(pe):
                a_bank, o_bank = empty_banks(pe, A, O)
                start_tensor(pe, o_bank)
                pe.wait_ge(x3_done, 1)
                turned(a_bank("x3T"), x3)
                pe.wait_ge(a_free, A.nth("x3T"))
                bank = o_bank("lg")
                for t in range(TT):
                    ins = nc.tensor.matmul(bank[:, EXPERTS * t:EXPERTS * (t + 1)], xT3[:, P * t:P * t + P], w("gate"), start=True, stop=True)
                ins.then_inc(o_full, 1)
                pe.wait_ge(moe_in, 16)
                pe.wait_ge(comb_done, 1)
                bank = o_bank("cT")
                for t in range(TT):
                    ins = nc.tensor.transpose(bank[0:EXPERTS, P * t:P * t + P], comb[:, t, :], ident)
                ins.then_inc(o_full, 1)
                pe.wait_ge(o_free, O.nth("cT"))
                for k in range(MC + 1):
                    n = P if k < MC else HID1
                    nc.tensor.matmul(a_bank(("m1", k))[0:n, :], mw("w1")[:, P * k:P * k + n], xT3[:, :], start=True,
                                     stop=True).then_inc(a_full, 1)
                    nc.tensor.matmul(o_bank(("m3", k))[0:n, :], mw("w3")[:, P * k:P * k + n], xT3[:, :], start=True,
                                     stop=True).then_inc(o_full, 1)
                    if k < MC:
                        nc.tensor.matmul(o_bank(("cb", k))[:, :], mw("spread")[0:EXPERTS, P * k:P * k + P], comb_T, start=True,
                                         stop=True).then_inc(o_full, 1)
                pe.wait_ge(o_free, O.nth(("m3", MC)))
                bank = o_bank("y3")
                for t in range(TT):
                    for k in range(MC + 1):
                        n = P if k < MC else HID1
                        ins = nc.tensor.matmul(bank[:, P * t:P * t + P], acts[0:n, k, P * t:P * t + P], mw("w2")[0:n, P * k:P * k + P],
                                               start=k == 0, stop=k == MC)
                ins.then_inc(o_full, 1)

            @block.scalar
            def _(act):
                def filled(key):
                    act.wait_ge(a_full, A.nth(key))
                    return banks_a[A.bank(key)]

                nc.scalar.copy(xT3[:, :], filled("x3T")[:, :]).then_inc(a_free, 1)
                act.wait_ge(o_free, O.nth("lg"))
                nc.scalar.activation(gates_e[:, :, 0:EXPERTS], logits[:, :, :], ACT.Exp).then_inc(ex_e_done, 1)
                for k in range(MC + 1):
                    n = P if k < MC else HID1
                    bank = filled(("m1", k))
                    if k >= 2:
                        act.wait_ge(o_free, O.nth(("m3", k - 2)))
                    nc.scalar.activation(silu1[0:n, k % 2], bank[0:n, :], ACT.Silu).then_inc(a_free, 1)

            @block.vector
            def _(dve):
                chain = Chain(dve, v_chain)

                def filled(key):
                    dve.wait_ge(o_full, O.nth(key))
                    return banks_o[O.bank(key)]

                norm(dve, chain, 0, x3, x3_done)
                start_vector(dve, filled, O)
                bank = filled("lg")
                lg = bank[:, 0:TT * EXPERTS].rearrange("p (t e) -> p t e", t=TT)
                chain.link(nc.vector.tensor_reduce(logit_m[:, :], lg, X, ALU.max))
                nc.vector.tensor_tensor(logits[:, :, :], lg, logit_m[:, :].unsqueeze(2).to_broadcast([P, TT, EXPERTS]),
                                        ALU.subtract).then_inc(o_free, 1)
                dve.wait_ge(ex_e_done, 1)
                for t in range(TT):
                    ins = nc.vector.max(out=top_e[:, t], in_=gates_e[:, t, 0:EXPERTS])
                chain.link(ins)
                chain.link(nc.vector.memset(top_e[:, :, TOP_E:8], -1.0))
                for t in range(TT):
                    ins = nc.vector.match_replace(out=rest_e[:, t], in_to_replace=top_e[:, t], in_values=gates_e[:, t], imm_value=0.0)
                chain.link(ins)
                chain.link(nc.vector.tensor_tensor(comb[:, :, :], gates_e[:, :, 0:EXPERTS], rest_e[:, :, 0:EXPERTS], ALU.subtract))
                chain.link(nc.vector.tensor_reduce(sum_e[:, :], comb[:, :, :], X, ALU.add))
                chain.link(nc.vector.reciprocal(rec_e[:, :], sum_e[:, :]))
                nc.vector.tensor_tensor(comb[:, :, :], comb[:, :, :], rec_e[:, :].unsqueeze(2).to_broadcast([P, TT, EXPERTS]),
                                        ALU.mult).then_inc(comb_done, 1)
                bank = filled("cT")
                nc.vector.tensor_copy(comb_T, bank[0:EXPERTS, :]).then_inc(o_free, 1)
                for k in range(MC + 1):
                    n = P if k < MC else HID1
                    bank = filled(("m3", k))
                    dve.wait_ge(a_free, A.nth(("m1", k)))
                    dst = gated[:, k % 2] if k < MC else acts[0:n, k]
                    nc.vector.tensor_tensor(dst, bank[0:n, :], silu1[0:n, k % 2], ALU.mult).then_inc(o_free, 1)
                    if k < MC:
                        bank = filled(("cb", k))
                        dve.wait_ge(o_free, O.nth(("m3", k)))
                        nc.vector.tensor_tensor(acts[:, k], bank[:, :], gated[:, k % 2], ALU.mult).then_inc(o_free, 1)
                bank = filled("y3")
                nc.vector.tensor_tensor(res[:, :, :], rows(bank), x3[:, :, :], ALU.add).then_inc(o_free, 1)
                dve.wait_ge(o_free, O.nth("y3"))
                norm(dve, chain, 1, x4, x4_done)

        with nc.Block() as block:
            start(block)
        clear_semaphores()
        with nc.Fori(0, B) as b:
            with nc.Block() as block:
                front(block)
            clear_semaphores()
            missed = nc.values_load(flag[:, :], min_val=0, max_val=1)
            with nc.If(missed > 0):
                with nc.Block() as block:
                    again(block)
                clear_semaphores()
            with nc.Block() as block:
                experts(b, block)
            clear_semaphores()


def constants():
    f = np.float32
    half = HD0 // 2
    inv = (1.0 / f(10000.0) ** (np.arange(half, dtype=f) / f(half))).astype(f)
    freqs = np.arange(S, dtype=f)[:, None] * inv[None, :]
    d = np.arange(P) % HD0
    cos, sin = np.cos(freqs)[:, d % half].T, np.sin(freqs)[:, d % half].T
    sin = np.where((d < half)[:, None], -sin, sin)
    q = np.arange(P)
    pick = q[:, None] // HD1 == np.arange(2 * H1 - 2)[None, :] - (H1 - 2)
    sums = q[:, None] == q[None, :] // SUM_COLS * SUM_COLS + HD0 + q[None, :] % HD0
    heads = (q[:, None] // HD1 == q[None, :] // HD1)
    dpre = (q[:, None] // H1 == q[None, :] // H1)
    dpost = (q[:, None] // H1 == q[None, :] % R8)
    spread = np.zeros((P, MC * P))
    spread[:EXPERTS] = np.arange(EXPERTS)[:, None] == np.arange(MC * P)[None, :] // HID1
    rank = np.broadcast_to(TOPK - 1 - np.arange(WINDOW), (P, WINDOW))
    c = np.concatenate([cos, sin, np.eye(P), heads, sums, pick, *thresholds(), rank], 1).astype(f)
    mask_s = np.where(q[None, :] > q[:, None], LOW, 0.0)
    mix = [np.where(np.arange(GROUP * R8)[None, :] > R8 * v + q[:, None] // H1, LOW, 0.0) for v in range(GROUP)]
    cb = np.concatenate([np.eye(P), mask_s, mask_s.T] + mix + [dpre, dpost], 1).astype(f)
    return c, cb, spread.astype(f)


def thresholds():
    first, slope = np.zeros((P, SUBS), np.float32), np.zeros((P, SUBS), np.float32)

    def quantile(share):
        lo, hi = -10.0, 10.0
        for _ in range(60):
            mid = (lo + hi) / 2
            lo, hi = (mid, hi) if (1 + erf(mid / sqrt(2))) / 2 < share else (lo, mid)
        return lo

    for n in range(NARROW_FROM, SUBS):
        for q in range(P):
            seen = R8 * n + q // H1 + 1 + MEM
            first[q, n] = quantile(1 - (AIM + 0.5) / seen)
            slope[q, n] = -1 / (2 * seen * exp(-first[q, n] ** 2 / 2) / sqrt(2 * pi))
    return first, slope


def laid_out(a):
    x = a["L0_attn_x"]
    qkv = a["L0_attn_w_qkv"]
    wq, wk, wv = qkv[:D], qkv[D:2 * D], qkv[2 * D:]
    swap = (np.arange(D) // HD0) * HD0 + (np.arange(D) + HD0 // 2) % HD0

    def cols(v):
        return v.reshape(-1, P).T

    def chunked(m):
        return m.reshape(-1, P, m.shape[1]).transpose(1, 0, 2).reshape(P, -1)

    hs = np.broadcast_to(np.repeat(a["L1_attn_head_scale_params"].reshape(H1), R8), (P, P))
    wo0 = np.pad(a["L0_attn_w_out"].T.reshape(SETS, HS, HD0, D), ((0, 0), (0, 0), (0, SUM_COLS - HD0), (0, 0)))
    wo0 = wo0.reshape(SETS, P, D).transpose(1, 0, 2).reshape(P, SETS * D)
    memk = a["L1_attn_mem_k"].reshape(NC, 2, MEM, HD1).transpose(1, 3, 0, 2).reshape(P, NC * MEM)
    pre = np.tile(a["L1_attn_W_pre_th"].T, (R8, R8))
    post = np.tile(np.repeat(a["L1_attn_W_post_th"].T, R8, axis=1), (R8, 1))
    w = [wq.T, wq[swap].T, wk.T, wk[swap].T, wv.T, wo0,
         cols(a["L0_ffn_w1_s"]), cols(a["L0_ffn_w2_s"]), cols(a["L0_ffn_h1_s"]), cols(a["L0_ffn_h2_s"]),
         np.broadcast_to(a["L0_ffn_w3_s"], (P, D)),
         a["L1_attn_Wk"], a["L1_attn_Wq"], a["L1_attn_Wv"], a["L1_attn_Wg"], cols(a["L1_attn_bg"]), hs,
         chunked(a["L1_attn_Wo"]), memk, pre, post, a["L1_ffn_gate_w"].T]
    memv = a["L1_attn_mem_v"].transpose(1, 0, 2).reshape(MEM, H1 * HD1)
    ffn1 = [a["L0_ffn_w1_w"].T, a["L0_ffn_w2_w"].T, chunked(a["L0_ffn_h1_w"].T)]
    ffn2 = [chunked(a["L0_ffn_h2_w"].T), chunked(a["L0_ffn_w3_w"].T)]
    up = [np.concatenate([a[f"L1_ffn_{n}"].reshape(MC * P, D), a[f"L1_ffn_s{n}"]]).T for n in ("w1", "w3")]
    down = np.concatenate([a["L1_ffn_w2"].transpose(0, 2, 1).reshape(MC * P, D), a["L1_ffn_sw2"].T, np.zeros((HID1, D), np.float32)])
    return {
        "xT": np.pad(x.transpose(0, 2, 1), ((0, 1), (0, 0), (0, 0))),
        "x": np.pad(x.reshape(B, TT, P, D).transpose(0, 2, 1, 3).reshape(B, P, TT * D), ((0, 1), (0, 0), (0, 0))),
        "w": np.concatenate(w, 1), "memv": memv,
        "ffn1": np.concatenate(ffn1, 1), "ffn2": np.concatenate(ffn2, 1),
        "moe": np.concatenate(up + [chunked(down), constants()[2]], 1),
    }


def kernel(**inputs):
    import concourse.bacc as bacc
    from concourse.bass_utils import run_bass_kernel_spmd

    arrays = {k: np.ascontiguousarray(v) for k, v in laid_out({k: np.asarray(v) for k, v in inputs.items()}).items()}
    arrays["c"], arrays["cb"], _ = constants()
    nc = bacc.Bacc("TRN2", target_bir_lowering=False, num_devices=1)
    d = {k: nc.dram_tensor(f"{k}_dram", v.shape, mybir.dt.from_np(v.dtype), kind="ExternalInput").ap() for k, v in arrays.items()}
    parts = nc.dram_tensor("parts_dram", [2, P, 3 * S], BF16, kind="Internal").ap()
    maxes = nc.dram_tensor("maxes_dram", [SETS, HS, 3 * S], BF16, kind="Internal").ap()
    out = nc.dram_tensor("out_dram", [B, S, D], F32, kind="ExternalOutput").ap()
    network(nc, d["xT"], d["x"], d["w"], d["c"], d["cb"], d["memv"], d["ffn1"], d["ffn2"], d["moe"], parts, maxes, out)
    r = run_bass_kernel_spmd(nc, [{f"{k}_dram": v for k, v in arrays.items()}], core_ids=[0])
    return r.results[0]["out_dram"]
```

```python
from contextlib import ExitStack
from math import erf, exp, pi, sqrt

import numpy as np

import concourse.bass as bass
from concourse import mybir

F32 = mybir.dt.float32
BF16 = mybir.dt.bfloat16
ALU = mybir.AluOpType
ACT = mybir.ActivationFunctionType
X = mybir.AxisListType.X

P = 128
B, S, D = 8, 512, 128
TT = S // P
EPS = 1e-5
LOW = -1.0e30
LOWEST = -3.0e38

H0, HD0 = 16, 8
PAIRS = H0 // 2
SCALE0 = 1.0 / HD0 ** 0.5
SETS = 2
HS = H0 // SETS
SUM_COLS = 2 * HD0
V_COLS = 3 * SUM_COLS
Q_PARTS = (0, 0, 1, 1, 0, 2)
K_PARTS = (0, 1, 0, 1, 2, 0)
SLOTS = len(Q_PARTS)
MAX_ROW = SLOTS * HD0
STACK = MAX_ROW + 3
E_SLOTS = 3
HID0 = 512
KC = HID0 // P
H1, HD1, MEM, TOPK = 16, 64, 4, 64
NC = H1 * HD1 // P
J = MEM + S
QK_SCALE = 10.0
R8 = P // H1
SUBS = S // R8
PER_TILE = P // R8
GROUP = 4
RB = 64
PER_BLOCK = RB // R8
ROUNDS = TOPK // 8
TILE_ORDER = (3, 1, 0, 2)
SEQ = [PER_TILE * t + u for t in TILE_ORDER for u in range(PER_TILE)]
PAIR = 2
STEPS = SUBS // PAIR
STEPS_TILE, STEPS_BLOCK = PER_TILE // PAIR, PER_BLOCK // PAIR
SCORES_AT = {1: 0, 0: H1 * (MEM + P * 3), 2: 0, 3: 0}
SCORES_N = H1 * (MEM + P * 3) + H1 * (MEM + P)
MIX_SLOTS, X_SLOTS, E1_SLOTS, A_SLOTS = 4, 8, 4, 4
LIVE = 3
NARROW_FROM = 12
WINDOW = 16
AIM = TOPK - (WINDOW + 1) / 2
DAMP = (0.8, 0.6, 0.4)
COUNTS = len(DAMP)
EXPERTS, HID1, TOP_E = 16, 64, 4
MC = EXPERTS * HID1 // P
PAD_E = 8


def width(n):
    return MEM + GROUP * R8 * (n // GROUP + 1)


def narrow(n):
    return n >= NARROW_FROM


def ahead(s):
    out = [("vx", s)] if s <= TT else []
    for o in range(TT):
        t, at = TILE_ORDER[o], STEPS_TILE * (o - 1)
        if s == STEPS_TILE * o + STEPS_TILE // 2 + 1:
            out.append(("g", t))
        per, begin = (3, at) if o > 1 else (8, at + STEPS_TILE - 3)
        if o and s >= begin:
            out += [("qk", t, g) for g in range(H1) if g // per == s - begin]
    return out


def opening(full):
    out = []
    for g in range(H1):
        if g % 2 == 0 and not full:
            k = g // 2
            out += [("keys", 0), ("keys", 1), ("qnorm",)] if k == 0 else [("keys", k + 1)] if k + 1 < NC else []
        out.append(("qk", TILE_ORDER[0], g))
    return out


def pieces(w):
    return [(0, w)] if w <= 512 else [(0, w // 2), (w // 2, w - w // 2)]


class Ring:

    def __init__(self, keys):
        self.order = {k: n for n, k in enumerate(keys)}
        assert len(self.order) == len(keys)

    def bank(self, key):
        return self.order[key] % 2

    def nth(self, key):
        return self.order[key] + 1


def weight_layout():
    sizes = dict(wq=P, wqs=P, wk=P, wks=P, wv=P, wo0=SETS * P, w1s=KC, w2s=KC, h1s=KC, h2s=KC, w3s=P,
                 Wk=H1 * HD1, Wq=H1 * HD1, Wv=H1 * HD1, Wg=H1 * HD1, bg=NC, hs=P, Wo=NC * P, memk=NC * MEM,
                 pre=P, post=P, gate=EXPERTS)
    const = dict(rope_c=S, rope_s=S, ident=P, heads=P, sums=P, pick=2 * H1 - 2, first=SUBS, slope=SUBS, rank=WINDOW)
    return sizes, const


def columns(sizes):
    at, out = 0, {}
    for k, n in sizes.items():
        out[k] = (at, at + n)
        at += n
    return out, at


def network(nc, xT_d, x_d, w_d, c_d, cb_d, memv_d, ffn1_d, ffn2_d, moe_d, parts_d, maxes_d, out_d):
    W_AT, W_N = columns(weight_layout()[0])
    C_AT, C_N = columns(weight_layout()[1])
    F1_AT, F1_N = columns(dict(w1=HID0, w2=HID0, h1=KC * HID0))
    F2_AT, F2_N = columns(dict(h2=KC * HID0, w3=KC * P))
    M_AT, M_N = columns(dict(w1=MC * P + HID1, w3=MC * P + HID1, w2=(MC + 1) * P, spread=MC * P))

    with ExitStack() as ctx:
        def sb(name, shape, dt=F32):
            return ctx.enter_context(nc.sbuf_tensor(name, shape, dt))

        def sem(name):
            s = ctx.enter_context(nc.semaphore(name))
            sems.append(s)
            return s

        sems = []
        wts = sb("wts", [P, W_N])
        cst = sb("cst", [P, C_N])
        CB_N = 3 * P + GROUP * GROUP * R8
        cstb = sb("cstb", [P, CB_N], BF16)
        memv = sb("memv", [MEM, H1 * HD1])
        powers = sb("powers", [P, TT + 2 * PAIR])

        def w(name):
            a, b = W_AT[name]
            return wts[:, a:b]

        def c(name):
            a, b = C_AT[name]
            return cst[:, a:b]

        ident = c("ident")
        identb, mask_s, mask_t = cstb[:, 0:P], cstb[:, P:2 * P], cstb[:, 2 * P:3 * P]
        mix_mask = cstb[:, 3 * P:].rearrange("p (v j) -> p v j", v=GROUP)
        tokens = sb("tokens", [P, 3 * S])
        xT = tokens[:, 0:S]
        x0, x1 = (tokens[:, S * z:S * z + S].rearrange("p (t d) -> p t d", t=TT) for z in (1, 2))
        res = sb("res", [P, TT, D])
        x2 = sb("x2", [P, TT, D])
        xe = sb("xe", [P, MEM + S])
        stats = sb("stats", [P, TT, 6])
        mv = sb("mv", [P, TT, 2])
        var = sb("var", [P, TT])
        rstd = sb("rstd", [P, TT])
        xT1 = xT

        kT = sb("kT", [P, NC * J])
        qT = sb("qT", [P, NC * S])
        vx = sb("vx", [P, (TT + 1) * H1 * HD1])
        dots = sb("dots", [P, SCORES_N])
        at2 = sb("at2", [P, TT * H1 * RB])
        tail = sb("tail", [MEM, H1, RB // 2])
        gate = sb("gate", [P, NC, P])
        mixin = sb("mixin", [P, MIX_SLOTS, J])
        squares = sb("squares", [P, 4 * S])
        xs_own = sb("xs", [P, X_SLOTS - 2, J])
        xs = [xs_own[:, i] for i in range(X_SLOTS - 2)] + [tokens[:, J * i:J * i + J] for i in range(2)]
        ex_own = sb("ex", [P, E1_SLOTS - 2, J])
        ex = [ex_own[:, i] for i in range(E1_SLOTS - 2)] + [squares[:, J * i:J * i + J] for i in range(2)]
        left_own = sb("left", [P, J])
        left = [left_own[:, :], squares[:, 2 * J:3 * J]]
        attn = sb("attn", [P, A_SLOTS, J])
        wsc = sb("wsc", [P, A_SLOTS, P])
        og = sb("og", [P, NC, P])
        top = sb("top", [P, LIVE, PAIR, 8])
        negm = sb("negm", [P, LIVE, PAIR])
        moments = sb("moments", [P, LIVE, PAIR, 6])
        meanvar = sb("meanvar", [P, LIVE, PAIR, 2])
        spreads = sb("spreads", [P, LIVE, PAIR])
        slopes = sb("slopes", [P, LIVE, PAIR])
        shift = sb("shift", [P, LIVE, PAIR])
        thr = sb("thr", [P, LIVE, PAIR])
        signs = sb("signs", [P, LIVE, PAIR])
        best = sb("best", [P, PAIR, WINDOW])
        picked = sb("picked", [P, PAIR, WINDOW])
        bound = sb("bound", [P, PAIR])
        ssum = sb("ssum", [P, LIVE, PAIR])
        rsum = sb("rsum", [P, LIVE, PAIR])
        above = sb("above", [P, SUBS])
        off = sb("off", [P, SUBS])
        worst = sb("worst", [P, 1])
        flag_f = sb("flag_f", [1, 1])
        flag = sb("flag", [1, 1], mybir.dt.int32)
        rq = sb("rq", [P, TT, H1])
        mem_squares, mem_norms = (squares[:, NC * MEM * z:NC * MEM * (z + 1)] for z in range(2))
        kT_v = kT[:, :].rearrange("p (c j) -> p c j", c=NC)
        qT_v = qT[:, :].rearrange("p (c s) -> p c s", c=NC)
        vx_v = vx[:, :].rearrange("p (c n) -> p c n", c=TT + 1)
        at_v = at2[:, :].rearrange("p (c h i) -> p c h i", c=TT, h=H1)
        memk_n = sb("memk_n", [P, NC * MEM])
        pre_b = sb("pre_b", [P, P])
        post_b = sb("post_b", [P, P])

        x3, xT3 = og[:, 0:NC // 2], og[:, NC // 2:].rearrange("p c s -> p (c s)")
        x4 = gate[:, 0:NC // 2]

        stacks = kT[:, 0:PAIRS * S].bitcast(BF16).rearrange("p (z a s) -> p z a s", z=2, a=PAIRS)
        q_stack, k_stack = stacks[:, 0], stacks[:, 1]
        rope_t = at2[:, 0:2 * S].rearrange("p (z s) -> p z s", z=2)
        rot = at2[:, 2 * S:4 * S].rearrange("p (z s) -> p z s", z=2)
        parts = at2[:, 4 * S:7 * S].bitcast(BF16).rearrange("p (z k s) -> p z k s", z=2, k=3)
        part_t = at2[:, 7 * S:8 * S]
        E_N = S + 3 * P + 2 * P + P
        E_OFF = [0, S, S + 3 * P, S + 5 * P]
        exps = vx[:, 0:E_SLOTS * E_N].rearrange("p (z n) -> p z n", z=E_SLOTS)
        v_pad = dots[:, F1_N:F1_N + TT * PAIRS * V_COLS].rearrange("p (k a n) -> p k a n", k=TT, a=PAIRS)
        sums_in = og[:, :, :].rearrange("p (g c) s -> p g (c s)", g=SETS)
        free = F1_N + TT * PAIRS * V_COLS
        out0 = dots[:, free:free + SETS * S].rearrange("p (g s) -> p g s", g=SETS)
        rec0 = dots[:, free + SETS * S:free + 3 * S]
        row_max = dots[:, free + 3 * S:free + 3 * S + TT * H0].rearrange("p (t h) -> p t h", t=TT)
        k_rows = at2[:, 0:TT * H1 * HD1].rearrange("p (t n) -> p t n", t=TT)
        k_squares = squares[:, 0:H1 * HD1].rearrange("p (h d) -> p h d", h=H1)
        k_norm = og[:, 0, 0:TT * H1].rearrange("p (t h) -> p t h", t=TT)
        q_norm = og[0:H1, NC // 2:].rearrange("h c s -> h (c s)")
        Q_SLOTS = 4

        def squares_of(k):
            z = k % Q_SLOTS
            return squares[:, S * (2 + z):S * (3 + z)] if z < 2 else gate[:, 4 * z - 8:4 * z - 4].rearrange("p c s -> p (c s)")

        max_parts = squares[0:HS, 0:SETS * 3 * S // 2].bitcast(BF16).rearrange("h (g k s) -> h g k s", g=SETS, k=3)
        neg_rows = squares[0:HS, SETS * 3 * S // 2:]
        neg_left = rec0[0:HS]

        def f1(name):
            a, b = F1_AT[name]
            return dots[:, a:b]

        def f2(name):
            a, b = F2_AT[name]
            return at2[:, a:b]

        silu0 = kT[:, 0:KC * S].rearrange("p (c s) -> p c s", c=KC)
        hid = qT[:, 0:KC * S].rearrange("p (c s) -> p c s", c=KC)
        gelu1 = kT[:, KC * S:2 * KC * S].rearrange("p (c s) -> p c s", c=KC)
        gelu2 = qT[:, KC * S:2 * KC * S].rearrange("p (c s) -> p c s", c=KC)

        def mw(name):
            a, b = M_AT[name]
            return dots[:, a:b]

        silu1 = qT[:, 0:2 * S].rearrange("p (z s) -> p z s", z=2)
        gated = qT[:, 2 * S:4 * S].rearrange("p (z s) -> p z s", z=2)
        acts = vx[:, 0:(MC + 1) * S].rearrange("p (c s) -> p c s", c=MC + 1)
        comb_T = qT[0:EXPERTS, 4 * S:5 * S]
        logit_m = sb("logit_m", [P, TT])
        def small(z, n):
            return dots[:, M_N + P * z:M_N + P * z + TT * n].rearrange("p (t e) -> p t e", t=TT)

        logits, comb, top_e, rest_e = small(0, EXPERTS), small(1, EXPERTS), small(2, 8), small(3, EXPERTS + PAD_E)
        gates_e = sb("gates_e", [P, TT, EXPERTS + PAD_E])
        sum_e = sb("sum_e", [P, TT])
        rec_e = sb("rec_e", [P, TT])

        banks_a = [ctx.enter_context(nc.psum_tensor(f"pa{i}", [P, 512], F32)) for i in range(2)]
        banks_o = [ctx.enter_context(nc.psum_tensor(f"po{i}", [P, 512], F32)) for i in range(2)]
        banks_m = [ctx.enter_context(nc.psum_tensor(f"pm{i}", [P, 512], F32)) for i in range(2)]
        banks_t = [ctx.enter_context(nc.psum_tensor(f"pt{i}", [P, 512], F32)) for i in range(2)]
        def scores_keys(full):
            def banks(what):
                return [what + (z,) for z in range(len(pieces(MEM + P * (what[1] + 1))) if what[0] == "qk" else 2)]

            a = [x for what in opening(full) if what[0] == "qk" and what[2] % 2 == 0 for x in banks(what)]
            o = [x for what in opening(full) if what[0] != "qk" or what[2] % 2 for x in (banks(what) if what[0] == "qk" else [what])]
            for s in range(STEPS + 3):
                for what in ahead(s):
                    a += banks(what)
                if s >= 3 and has_tail(s - 3):
                    a.append(("tail", s - 3))
            o += [x for r in range(S // RB) for x in [("av", r)] + ([("wo", r // 2)] if r % 2 else [])]
            m = [("mix", i, z) for i in range(SUBS) for z in range(len(pieces(width(SEQ[i]))))]
            return a, o, m, [("post", i) for i in range(SUBS)]

        def has_tail(s):
            return SEQ[PAIR * s] % PER_TILE >= PER_TILE - GROUP

        KEYS, KEYS_AGAIN = scores_keys(False), scores_keys(True)
        FRONT_A = (["v"] + [("st", h, k) for h in range(H0) for k in range(TT)] + ["x1T"]
                   + [("f1", k) for k in range(KC)] + [("h1", k) for k in range(KC)] + [("h2", k) for k in range(KC)] + ["x2T"]
                   + [("k", t, z) for t in range(TT) for z in range(2)] + [("q", k) for k in range(NC)] + ["qs"])
        def abreast(i):
            return TT // (i + 1)

        S_FIRST, S_SECOND = ([(i, h) for i in range(TT) for h in range(HS * g, HS * (g + 1)) if (h - HS * g) // 2 % abreast(i) == 0]
                             for g in range(SETS))
        S_BESIDE = 6

        def after_product(t, k):
            n, i = (TT - 1) * (MC + 1), (MC + 1) * t + k
            return S_FIRST[len(S_FIRST) * i // n:len(S_FIRST) * (i + 1) // n]

        START_O = ["rq", "rqs", "rk", "rks"]
        FRONT_O = ([("s",) + k for k in S_SECOND] + [("mT", 1)]
                   + [("den", 0), ("den", 1), "y0"]
                   + [("f2", k) for k in range(KC)] + ["y1"])
        EXPERTS_A = ["x3T"] + [("m1", k) for k in range(MC + 1)] + ["y3"]
        EXPERTS_O = (["lg", "cT"] + [x for k in range(MC + 1) for x in [("m3", k)] + ([("cb", k)] if k < MC else [])]
                     + [("s",) + k for k in S_FIRST] + [("mT", 0)])
        RINGS = [Ring(FRONT_A + KEYS[0]), Ring(FRONT_O + KEYS[1] + ["bad"]), Ring(KEYS[2]), Ring(KEYS[3])]
        RINGS_AGAIN = [Ring(k) for k in KEYS_AGAIN]
        RING_START = Ring(START_O + [("s",) + k for k in S_FIRST] + [("mT", 0)])
        RINGS_EXPERTS = [Ring(EXPERTS_A), Ring(START_O + EXPERTS_O)]

        w_in = sem("w_in")
        init_done = sem("init_done")
        pre_done = sem("pre_done")
        x_in = sem("x_in")
        a_full, a_free = sem("a_full"), sem("a_free")
        o_full, o_free = sem("o_full"), sem("o_free")
        m_full, m_free = sem("m_full"), sem("m_free")
        t_full, t_free = sem("t_full"), sem("t_free")
        v_chain = sem("v_chain")
        g_chain = sem("g_chain")
        rot_done = sem("rot_done")
        parts_done = sem("parts_done")
        parts_out = sem("parts_out")
        stack_in = sem("stack_in")
        rows_done = sem("rows_done")
        rows_out = sem("rows_out")
        rows_in = sem("rows_in")
        av0_done = sem("av0_done")
        sums_done = sem("sums_done")
        out0_done = sem("out0_done")
        var_done = sem("var_done")
        rstd_done = sem("rstd_done")
        x1_done, x2_done, x3_done, x4_done = (sem(f"x{i}_done") for i in range(1, 5))
        ffn_in = sem("ffn_in")
        moe_in = sem("moe_in")
        k_summed = sem("k_summed")
        k_rooted = sem("k_rooted")
        k_normed = sem("k_normed")
        q_sq = sem("q_sq")
        q_summed = sem("q_summed")
        rq_done = sem("rq_done")
        mix_in = [sem(f"mix_in{i}") for i in range(MIX_SLOTS)]
        zero_done = sem("zero_done")
        negm_done = sem("negm_done")
        moments_done = sem("moments_done")
        thr_ready = sem("thr_ready")
        thr_done = [sem(f"thr_done{r}") for r in range(COUNTS)]
        worst_done = sem("worst_done")
        counted = [sem(f"counted{r}") for r in range(COUNTS)]
        ex_done = sem("ex_done")
        summed = sem("summed")
        attn_done = sem("attn_done")
        og_done = sem("og_done")
        ex_e_done = sem("ex_e_done")
        comb_done = sem("comb_done")
        y_out = sem("y_out")

        class Chain:

            def __init__(self, eng, s):
                self.eng, self.sem, self.n = eng, s, 0

            def mark(self, ins):
                self.n += 1
                ins.then_inc(self.sem, 1)
                return self.n

            def after(self, n):
                self.eng.wait_ge(self.sem, n)

            def link(self, ins):
                self.after(self.mark(ins))

        with nc.Block() as block:
            @block.sync
            def _(sp):
                sp.dma_start(wts[:, :], w_d).then_inc(w_in, 16)
                sp.dma_start(cst[:, :], c_d).then_inc(w_in, 16)
                sp.dma_start(dots[:, 0:CB_N + 2 * P], cb_d).then_inc(w_in, 16)
                sp.dma_start(memv[:, :], memv_d).then_inc(w_in, 16)

            @block.gpsimd
            def _(pool):
                nc.gpsimd.memset(xe[:, 0:MEM], 0.0)
                nc.gpsimd.memset(powers[:, 0:TT], -0.5)
                nc.gpsimd.memset(powers[:, TT:TT + PAIR], 0.5)
                nc.gpsimd.memset(powers[:, TT + PAIR:], -1.0)
                nc.gpsimd.memset(gates_e[:, :, :], -1.0).then_inc(init_done, 1)
                pool.wait_ge(w_in, 64)
                nc.gpsimd.tensor_tensor(mem_squares, w("memk"), w("memk"), ALU.mult).then_inc(pre_done, 1)

            @block.tensor
            def _(pe):
                pe.wait_ge(w_in, 64)
                pe.wait_ge(pre_done, 1)
                nc.tensor.matmul(banks_a[0][:, 0:NC * MEM], c("heads"), mem_squares, start=True,
                                 stop=True).then_inc(a_full, 1)

            @block.scalar
            def _(act):
                act.wait_ge(a_full, 1)
                nc.scalar.activation(mem_norms, banks_a[0][:, 0:NC * MEM], ACT.Sqrt).then_inc(a_free, 1)

            @block.vector
            def _(dve):
                chain = Chain(dve, v_chain)
                dve.wait_ge(w_in, 64)
                nc.vector.tensor_copy(cstb[:, :], dots[:, 0:CB_N])
                nc.vector.tensor_tensor(pre_b[:, :], w("pre"), dots[:, CB_N:CB_N + P], ALU.mult)
                nc.vector.tensor_scalar(w("bg"), w("bg"), 0.5, None, ALU.mult)
                chain.link(nc.vector.tensor_tensor(post_b[:, :], w("post"), dots[:, CB_N + P:CB_N + 2 * P], ALU.mult))
                nc.vector.scalar_tensor_tensor(out=post_b[:, :], in0=post_b[:, :], scalar=0.5, in1=w("hs"), op0=ALU.mult, op1=ALU.mult)
                dve.wait_ge(a_free, 1)
                chain.link(nc.vector.tensor_scalar(mem_norms, mem_norms, 1e-12, None, ALU.max))
                chain.link(nc.vector.reciprocal(mem_norms, mem_norms))
                chain.link(nc.vector.tensor_tensor(memk_n[:, :], w("memk"), mem_norms, ALU.mult))

        def clear_semaphores():
            engines = (nc.sync, nc.scalar, nc.vector, nc.gpsimd, nc.tensor)
            for i, s in enumerate(sems):
                engines[i % len(engines)].sem_clear(s)
            nc.all_engine_barrier()

        clear_semaphores()

        def empty_banks(pe, A, O):
            def a_bank(key):
                if A.nth(key) > 2:
                    pe.wait_ge(a_free, A.nth(key) - 2)
                return banks_a[A.bank(key)]

            def o_bank(key):
                if O.nth(key) > 2:
                    pe.wait_ge(o_free, O.nth(key) - 2)
                return banks_o[O.bank(key)]

            return a_bank, o_bank

        def turned(bank, src):
            for t in range(TT):
                ins = nc.tensor.transpose(bank[:, P * t:P * t + P], src[:, t, :], ident)
            ins.then_inc(a_full, 1)

        def inverse_root(pool, k):
            pool.wait_ge(var_done, k + 1)
            nc.gpsimd.tensor_tensor(rstd[:, :], var[:, :], powers[:, 0:TT], ALU.pow).then_inc(rstd_done, 1)

        def norm(dve, chain, k, dst, done):
            for t in range(TT):
                ins = nc.vector.bn_stats(stats[:, t], res[:, t])
            chain.link(ins)
            for t in range(TT):
                ins = nc.vector.bn_aggr(mv[:, t], stats[:, t])
            chain.link(ins)
            nc.vector.tensor_scalar(var[:, :], mv[:, :, 1], EPS, None, ALU.add).then_inc(var_done, 1)
            dve.wait_ge(rstd_done, k + 1)
            for t in range(TT):
                ins = nc.vector.tensor_scalar(dst[:, t], res[:, t], mv[:, t, 0:1], rstd[:, t:t + 1], ALU.subtract, ALU.mult)
            ins.then_inc(done, 1)
            dve.wait_ge(done, 1)

        def rows(bank):
            return bank[:, :].rearrange("p (t d) -> p t d", t=TT)

        def pair_of(s):
            return [(z, PAIR * s + z, SEQ[PAIR * s + z]) for z in range(PAIR)]

        def last_piece(n):
            return len(pieces(width(n))) - 1

        SEARCHED = [s for s in range(STEPS) if narrow(SEQ[PAIR * s])]

        def searched(s, full):
            return not full and s in SEARCHED

        def scores_sync(sp, R):
            A, O, M, T = R
            for m, n in enumerate(SEQ):
                t, u = divmod(n, PER_TILE)
                wt, wn = MEM + P * (t + 1), width(n)
                if u == 0:
                    opens, last = t == TILE_ORDER[0], len(pieces(wt)) - 1
                    sp.wait_ge(a_free, A.nth(("qk", t, H1 - 2 if opens else H1 - 1, last)))
                    if opens:
                        sp.wait_ge(o_free, O.nth(("qk", t, H1 - 1, last)))
                if m >= MIX_SLOTS:
                    sp.wait_ge(m_full, M.nth(("mix", m - MIX_SLOTS, last_piece(SEQ[m - MIX_SLOTS]))))
                tile = dots[R8 * u:R8 * u + R8, SCORES_AT[t]:SCORES_AT[t] + H1 * wt].rearrange("p (g j) -> p g j", g=H1)
                sp.dma_start(mixin[:, m % MIX_SLOTS, 0:wn], tile[:, :, 0:wn]).then_inc(mix_in[m % MIX_SLOTS], 16)

        def scores_gpsimd(pool, chain, R, full):
            nc.gpsimd.memset(attn[:, :, :], 0.0).then_inc(zero_done, 1)

            def scale(s):
                pool.wait_ge(summed, s + 1)
                p = s % LIVE
                if searched(s, full):
                    chain.link(nc.gpsimd.tensor_scalar(ssum[:, p], ssum[:, p], 0.5, None, ALU.max))
                chain.link(nc.gpsimd.tensor_tensor(rsum[:, p], ssum[:, p], powers[:, TT + PAIR:], ALU.pow))
                if PAIR * s >= A_SLOTS:
                    before = s - A_SLOTS // PAIR
                    pool.wait_ge(t_full, R[3].nth(("post", PAIR * before + PAIR - 1)))
                    if has_tail(before):
                        pool.wait_ge(a_full, R[0].nth(("tail", before)))
                for z, m, n in pair_of(s):
                    nc.gpsimd.tensor_scalar(wsc[:, m % A_SLOTS], post_b[:, :], rsum[:, p, z:z + 1], 1.0, ALU.mult, ALU.mult).then_inc(attn_done, 1)

            def first_threshold(s):
                q, p, n = SEARCHED.index(s), s % LIVE, SEQ[PAIR * s]
                pool.wait_ge(moments_done, q + 1)
                chain.link(nc.gpsimd.tensor_tensor(spreads[:, p], meanvar[:, p, :, 1], powers[:, TT:TT + PAIR], ALU.pow))
                nc.gpsimd.tensor_tensor(slopes[:, p], spreads[:, p], c("slope")[:, n:n + PAIR], ALU.mult)
                chain.link(nc.gpsimd.tensor_tensor(shift[:, p], spreads[:, p], c("first")[:, n:n + PAIR], ALU.mult))
                nc.gpsimd.tensor_tensor(thr[:, p], meanvar[:, p, :, 0], shift[:, p], ALU.add).then_inc(thr_ready, 1)

            def corrected(s, r):
                q, p, n = SEARCHED.index(s), s % LIVE, SEQ[PAIR * s]
                pool.wait_ge(counted[r], q + 1)
                chain.link(nc.gpsimd.tensor_scalar(shift[:, p], signs[:, p], 2 * AIM - width(n), DAMP[r], ALU.add, ALU.mult))
                chain.link(nc.gpsimd.tensor_tensor(shift[:, p], shift[:, p], slopes[:, p], ALU.mult))
                nc.gpsimd.tensor_tensor(thr[:, p], thr[:, p], shift[:, p], ALU.add).then_inc(thr_done[r], 1)

            for s in range(STEPS + 2):
                search = 1 <= s <= STEPS and searched(s - 1, full)
                if search:
                    corrected(s - 1, 0)
                if s < STEPS and searched(s, full):
                    first_threshold(s)
                if search:
                    corrected(s - 1, 1)
                    corrected(s - 1, 2)
                if s >= 2:
                    scale(s - 2)

        def scores_tensor(pe, R, full):
            A, O, M, T = R
            a_bank, o_bank = empty_banks(pe, A, O)

            def head(t, g, bank_of):
                at = HD1 * (g % 2)
                for z, (j0, jn) in enumerate(pieces(MEM + P * (t + 1))):
                    ins = nc.tensor.matmul(bank_of(("qk", t, g, z))[:, 0:jn], qT_v[at:at + HD1, g // 2, P * t:P * t + P],
                                           kT_v[at:at + HD1, g // 2, j0:j0 + jn], start=True, stop=True)
                    ins.then_inc(a_full if bank_of is a_bank else o_full, 1)

            def open_scores():
                for what in opening(full):
                    if what[0] == "keys":
                        k, bank = what[1], o_bank(what)
                        for t in range(TT):
                            ins = nc.tensor.transpose(bank[:, P * t:P * t + P], k_rows[:, t, P * k:P * k + P], ident)
                        ins.then_inc(o_full, 1)
                    elif what[0] == "qnorm":
                        pe.wait_ge(a_free, A.nth("qs"))
                        bank = o_bank(what)
                        for t in range(TT):
                            ins = nc.tensor.transpose(bank[:, H1 * t:H1 * t + H1], q_norm[:, P * t:P * t + P], ident[0:H1, 0:H1])
                        ins.then_inc(o_full, 1)
                    else:
                        if what[2] % 2 == 0 and not full:
                            pe.wait_ge(o_free, O.nth(("keys", what[2] // 2)))
                        head(what[1], what[2], o_bank if what[2] % 2 else a_bank)

            def gates_and_heads(s):
                for what in ahead(s):
                    t = what[1]
                    if what[0] == "vx":
                        rows = slice(P * t, min(P * t + P, J))
                        for z in range(2):
                            bank = a_bank(("vx", t, z))[0:rows.stop - rows.start, :]
                            half = slice(512 * z, 512 * z + 512)
                            ins = nc.tensor.matmul(bank, xe[:, rows], w("Wv")[:, half], start=True, stop=t > 0)
                            if t == 0:
                                ins = nc.tensor.matmul(bank, ident[0:MEM, :], memv[:, half], start=False, stop=True)
                            ins.then_inc(a_full, 1)
                    elif what[0] == "g":
                        rows = slice(MEM + P * t, MEM + P * t + P)
                        for z in range(2):
                            bank = a_bank(("g", t, z))
                            for k in range(NC // 2):
                                kk = NC // 2 * z + k
                                ins = nc.tensor.matmul(bank[:, P * k:P * k + P], w("Wg")[:, P * kk:P * kk + P], xe[:, rows],
                                                       start=True, stop=True)
                            ins.then_inc(a_full, 1)
                    else:
                        head(t, what[2], a_bank)

            def mix(m, n):
                pe.wait_ge(mix_in[m % MIX_SLOTS], 16 * (m // MIX_SLOTS + 1))
                for z, (j0, jn) in enumerate(pieces(width(n))):
                    last = z == last_piece(n)
                    if M.nth(("mix", m, z)) > 2:
                        pe.wait_ge(m_free, M.nth(("mix", m, z)) - 2)
                    bank = banks_m[M.bank(("mix", m, z))]
                    ins = nc.tensor.matmul(bank[:, 0:jn], pre_b[:, :], mixin[:, m % MIX_SLOTS, j0:j0 + jn], start=True, stop=not last)
                    if last:
                        ins = nc.tensor.matmul(bank[:, jn - GROUP * R8:jn], identb, mix_mask[:, n % GROUP], start=False, stop=True)
                    ins.then_inc(m_full, 1)

            def post(s):
                for z, m, n in pair_of(s):
                    pe.wait_ge(attn_done, m + 1)
                    if T.nth(("post", m)) > 2:
                        pe.wait_ge(t_free, T.nth(("post", m)) - 2)
                    bank = banks_t[T.bank(("post", m))]
                    for k in range(n // PER_TILE + 1):
                        ins = nc.tensor.matmul(bank[:, P * k:P * k + P], attn[:, m % A_SLOTS, P * k:P * k + P], wsc[:, m % A_SLOTS],
                                               start=True, stop=True)
                    ins.then_inc(t_full, 1)
                if has_tail(s):
                    bank = a_bank(("tail", s))
                    for z, m, n in pair_of(s):
                        j0 = P * (n // PER_TILE + 1)
                        ins = nc.tensor.matmul(bank[0:MEM, P * z:P * z + P], attn[:, m % A_SLOTS, j0:j0 + MEM], wsc[:, m % A_SLOTS],
                                               start=True, stop=True)
                    ins.then_inc(a_full, 1)

            def values(r):
                t, odd = divmod(SEQ[PER_BLOCK * r] // PER_BLOCK, 2)
                pe.wait_ge(t_free, T.nth(("post", PER_BLOCK * r + PER_BLOCK - 1)))
                if odd:
                    pe.wait_ge(a_free, A.nth(("tail", STEPS_BLOCK * (r + 1) - 1)))
                if r == 0:
                    pe.wait_ge(a_free, A.nth(("vx", TT, 1)))
                bank = o_bank(("av", r))
                for h in range(H1):
                    at, col = HD1 * (h % 2), RB * (h // 2)
                    for k in range(t + 1):
                        ins = nc.tensor.matmul(bank[at:at + HD1, col:col + RB], vx_v[:, k, HD1 * h:HD1 * h + HD1], at_v[:, k, h, :],
                                               start=k == 0, stop=k == t and not odd)
                    if odd:
                        ins = nc.tensor.matmul(bank[at:at + HD1, col + RB // 2:col + RB], vx_v[0:MEM, t + 1, HD1 * h:HD1 * h + HD1],
                                               tail[:, h, :], start=False, stop=True)
                ins.then_inc(o_full, 1)

            def project(o):
                pe.wait_ge(o_free, O.nth(("av", 2 * o + 1)))
                bank = o_bank(("wo", o))
                for k in range(NC):
                    ins = nc.tensor.matmul(bank[:, 0:P], og[:, k, :], w("Wo")[:, P * k:P * k + P], start=k == 0, stop=k == NC - 1)
                ins.then_inc(o_full, 1)

            open_scores()
            for s in range(-1, STEPS + STEPS_BLOCK + 2):
                first = s + 1 < STEPS and last_piece(SEQ[PAIR * (s + 1)]) == 0
                if s >= 0 and not first:
                    gates_and_heads(s)
                if s + 1 < STEPS:
                    for z, m, n in pair_of(s + 1):
                        mix(m, n)
                if s >= 0 and first:
                    gates_and_heads(s)
                if s >= STEPS_BLOCK + 3 and (s - 3) % STEPS_BLOCK == 0:
                    values((s - 3) // STEPS_BLOCK - 1)
                if 3 <= s < STEPS + 3:
                    post(s - 3)
                if s > STEPS_TILE and (s - 5) % STEPS_TILE == 0:
                    project((s - 5) // STEPS_TILE - 1)

        def scores_scalar(act, R, full):
            A, O, M, T = R

            def gates(t):
                o = TILE_ORDER.index(t)
                if o:
                    act.wait_ge(o_free, O.nth(("av", 2 * o - 1)))
                for z in range(2):
                    act.wait_ge(a_full, A.nth(("g", t, z)))
                    bank = banks_a[A.bank(("g", t, z))]
                    for k in range(NC // 2):
                        kk = NC // 2 * z + k
                        ins = nc.scalar.activation(gate[:, kk], bank[:, P * k:P * k + P], ACT.Tanh, scale=0.5, bias=w("bg")[:, kk:kk + 1])
                    ins.then_inc(a_free, 1)

            def values(k):
                rows = min(P, J - P * k)
                for z in range(2):
                    act.wait_ge(a_full, A.nth(("vx", k, z)))
                    nc.scalar.copy(vx_v[0:rows, k, 512 * z:512 * z + 512], banks_a[A.bank(("vx", k, z))][0:rows, :]).then_inc(a_free, 1)

            def head(t, g):
                o = TILE_ORDER.index(t)
                wt = MEM + P * (t + 1)
                if g == 0 and o:
                    for s in mix_in:
                        act.wait_ge(s, 16 * max(o - 1, 1) * PER_TILE // MIX_SLOTS)
                for z, (j0, jn) in enumerate(pieces(wt)):
                    key = ("qk", t, g, z)
                    act.wait_ge(a_full, A.nth(key))
                    at = SCORES_AT[t] + g * wt + j0
                    nc.scalar.activation(dots[:, at:at + jn], banks_a[A.bank(key)][:, 0:jn], ACT.Copy,
                                         scale=rq[:, t, g:g + 1]).then_inc(a_free, 1)

            def gates_and_heads(s):
                for what in ahead(s):
                    if what[0] == "g":
                        gates(what[1])
                    elif what[0] == "vx":
                        values(what[1])
                    else:
                        head(what[1], what[2])

            def mixed(s):
                if PAIR * s >= X_SLOTS:
                    act.wait_ge(summed, s + 1 - X_SLOTS // PAIR)
                for y, m, n in pair_of(s):
                    for z, (j0, jn) in enumerate(pieces(width(n))):
                        act.wait_ge(m_full, M.nth(("mix", m, z)))
                        nc.scalar.copy(xs[m % X_SLOTS][:, j0:j0 + jn], banks_m[M.bank(("mix", m, z))][:, 0:jn]).then_inc(m_free, 1)

            def count(s, r):
                q = SEARCHED.index(s)
                act.wait_ge(thr_done[r - 1] if r else thr_ready, q + 1)
                if r == 0 and PAIR * s >= E1_SLOTS:
                    act.wait_ge(summed, s + 1 - E1_SLOTS // PAIR)
                for z, m, n in pair_of(s):
                    ins = nc.scalar.activation(ex[m % E1_SLOTS][:, 0:width(n)], xs[m % X_SLOTS][:, 0:width(n)], ACT.Sign, scale=-1.0,
                                               bias=thr[:, s % LIVE, z:z + 1], accum_out=signs[:, s % LIVE, z:z + 1])
                ins.then_inc(counted[r], 1)

            def exponentials(s):
                act.wait_ge(negm_done, s + 1)
                if searched(s, full):
                    act.wait_ge(thr_done[-1], SEARCHED.index(s) + 1)
                elif PAIR * s >= E1_SLOTS:
                    act.wait_ge(summed, s + 1 - E1_SLOTS // PAIR)
                for z, m, n in pair_of(s):
                    nc.scalar.activation(ex[m % E1_SLOTS][:, 0:width(n)], xs[m % X_SLOTS][:, 0:width(n)], ACT.Exp,
                                         bias=negm[:, s % LIVE, z:z + 1]).then_inc(ex_done, 1)

            def posted(s):
                r = s // STEPS_BLOCK
                if s % STEPS_BLOCK == 0 and r:
                    act.wait_ge(o_full, O.nth(("av", r - 1)))
                for z, m, n in pair_of(s):
                    t, u = n // PER_TILE, n % PER_BLOCK
                    act.wait_ge(t_full, T.nth(("post", m)))
                    bank = banks_t[T.bank(("post", m))]
                    nc.scalar.copy(at_v[:, 0:t + 1, :, R8 * u:R8 * u + R8],
                                   bank[:, 0:P * (t + 1)].rearrange("p (k h i) -> p k h i", k=t + 1, h=H1)).then_inc(t_free, 1)
                if has_tail(s):
                    act.wait_ge(a_full, A.nth(("tail", s)))
                    bank = banks_a[A.bank(("tail", s))]
                    v = R8 * (SEQ[PAIR * s] % GROUP)
                    nc.scalar.copy(tail[:, :, v:v + PAIR * R8].rearrange("p h (z i) -> p z h i", z=PAIR),
                                   bank[0:MEM, 0:PAIR * P].rearrange("p (z h i) -> p z h i", z=PAIR, h=H1)).then_inc(a_free, 1)

            for what in opening(full):
                if what[0] == "qk" and what[2] % 2 == 0:
                    head(what[1], what[2])
            for s in range(STEPS + 4):
                if s < STEPS:
                    mixed(s)
                search = 1 <= s <= STEPS and searched(s - 1, full)
                if search:
                    count(s - 1, 0)
                if s >= 4:
                    posted(s - 4)
                if search:
                    count(s - 1, 1)
                if 2 <= s < STEPS + 2:
                    exponentials(s - 2)
                gates_and_heads(s)
                if search:
                    count(s - 1, 2)

        def scores_vector(dve, chain, R, full):
            A, O, M, T = R

            def maxima(s):
                p, search = s % LIVE, searched(s, full)
                for z, m, n in pair_of(s):
                    dve.wait_ge(m_free, M.nth(("mix", m, last_piece(n))))
                    found = chain.mark(nc.vector.max(out=top[:, p, z], in_=xs[m % X_SLOTS][:, 0:width(n)]))
                    if search:
                        seen = chain.mark(nc.vector.bn_stats(moments[:, p, z], xs[m % X_SLOTS][:, 0:width(n) - GROUP * R8:2]))
                chain.after(found)
                nc.vector.tensor_scalar(negm[:, p], top[:, p, :, 0], -1.0, None, ALU.mult).then_inc(negm_done, 1)
                if search:
                    chain.after(seen)
                    for z in range(PAIR):
                        ins = nc.vector.bn_aggr(meanvar[:, p, z], moments[:, p, z])
                    ins.then_inc(moments_done, 1)

            def in_turn(s):
                wn = width(SEQ[PAIR * s])
                src = [xs[m % X_SLOTS][:, 0:wn] for z, m, n in pair_of(s)]
                t8 = [top[:, s % LIVE, z] for z in range(PAIR)]
                done = [None] * PAIR
                for _ in range(ROUNDS - 1):
                    for z in range(PAIR):
                        if done[z]:
                            chain.after(done[z])
                        done[z] = chain.mark(nc.vector.match_replace(out=left[z][:, 0:wn], in_to_replace=t8[z], in_values=src[z], imm_value=LOWEST))
                        src[z], t8[z] = left[z][:, 0:wn], best[:, z, 0:8]
                    for z in range(PAIR):
                        chain.after(done[z])
                        done[z] = chain.mark(nc.vector.max(out=t8[z], in_=src[z]))
                chain.after(done[-1])
                return [best[:, z, 7:8] for z in range(PAIR)]

            def near_threshold(s):
                wn = width(SEQ[PAIR * s])
                dve.wait_ge(thr_done[-1], SEARCHED.index(s) + 1)
                done = [None] * PAIR
                for z, m, n in pair_of(s):
                    done[z] = chain.mark(nc.vector.tensor_scalar(left[z][:, 0:wn], xs[m % X_SLOTS][:, 0:wn], thr[:, s % LIVE, z:z + 1], None,
                                                                 ALU.is_gt, ALU.add, accum_out=above[:, n:n + 1]))
                for z, m, n in pair_of(s):
                    chain.after(done[z])
                    done[z] = chain.mark(nc.vector.scalar_tensor_tensor(out=left[z][:, 0:wn], in0=left[z][:, 0:wn], scalar=LOWEST,
                                                                        in1=xs[m % X_SLOTS][:, 0:wn], op0=ALU.mult, op1=ALU.add))
                for k in range(WINDOW // 8):
                    for z in range(PAIR):
                        chain.after(done[z])
                        done[z] = chain.mark(nc.vector.max(out=best[:, z, 8 * k:8 * k + 8], in_=left[z][:, 0:wn]))
                    if k < WINDOW // 8 - 1:
                        for z in range(PAIR):
                            chain.after(done[z])
                            done[z] = chain.mark(nc.vector.match_replace(out=left[z][:, 0:wn], in_to_replace=best[:, z, 8 * k:8 * k + 8],
                                                                         in_values=left[z][:, 0:wn], imm_value=LOWEST))
                for z, m, n in pair_of(s):
                    chain.after(done[z])
                    done[z] = chain.mark(nc.vector.scalar_tensor_tensor(out=picked[:, z], in0=c("rank"), scalar=above[:, n:n + 1], in1=best[:, z],
                                                                        op0=ALU.is_equal, op1=ALU.mult, accum_out=bound[:, z:z + 1]))
                chain.after(done[-1])
                return [bound[:, z:z + 1] for z in range(PAIR)]

            def select(s):
                if searched(s, full):
                    bounds = near_threshold(s)
                else:
                    bounds = in_turn(s) if width(SEQ[PAIR * s]) >= TOPK else [LOWEST] * PAIR
                for z, m, n in pair_of(s):
                    wn = width(n)
                    dve.wait_ge(ex_done, m + 1)
                    if m >= A_SLOTS:
                        before = m - A_SLOTS
                        dve.wait_ge(t_full, T.nth(("post", before)))
                        if has_tail(before // PAIR):
                            dve.wait_ge(a_full, A.nth(("tail", before // PAIR)))
                    full_width = MEM + P * (n // PER_TILE + 1)
                    if m >= PER_TILE and wn < full_width:
                        nc.vector.memset(attn[:, m % A_SLOTS, wn:full_width], 0.0)
                    ins = nc.vector.scalar_tensor_tensor(out=attn[:, m % A_SLOTS, 0:wn], in0=xs[m % X_SLOTS][:, 0:wn], scalar=bounds[z],
                                                         in1=ex[m % E1_SLOTS][:, 0:wn], op0=ALU.is_ge, op1=ALU.mult,
                                                         accum_out=ssum[:, s % LIVE, z:z + 1])
                ins.then_inc(summed, 1)

            def gated_rows(r):
                o, odd = divmod(r, 2)
                dve.wait_ge(o_full, O.nth(("av", r)))
                dve.wait_ge(a_free, A.nth(("g", TILE_ORDER[o], 1)))
                bank = banks_o[O.bank(("av", r))]
                nc.vector.scalar_tensor_tensor(out=og[:, :, RB * odd:RB * odd + RB], in0=gate[:, :, RB * odd:RB * odd + RB], scalar=1.0,
                                               in1=bank[:, :].rearrange("p (c i) -> p c i", c=NC), op0=ALU.add, op1=ALU.mult).then_inc(o_free, 1)

            def residual(o):
                t = TILE_ORDER[o]
                dve.wait_ge(o_full, O.nth(("wo", o)))
                nc.vector.tensor_tensor(res[:, t], banks_o[O.bank(("wo", o))][:, 0:P], x2[:, t], ALU.add).then_inc(o_free, 1)

            for what in opening(full):
                if what[0] == "keys":
                    dve.wait_ge(o_full, O.nth(what))
                    nc.vector.tensor_copy(kT_v[:, what[1], MEM:J], banks_o[O.bank(what)][:, :]).then_inc(o_free, 1)
                elif what[0] == "qnorm":
                    r = rq[:, :, :].rearrange("p t h -> p (t h)")
                    dve.wait_ge(o_full, O.nth(what))
                    nc.vector.tensor_scalar(r, banks_o[O.bank(what)][:, 0:TT * H1], 1e-12, None, ALU.max).then_inc(o_free, 1)
                    dve.wait_ge(o_free, O.nth(what))
                    chain.link(nc.vector.reciprocal(r, r))
                    nc.vector.tensor_scalar(r, r, QK_SCALE, None, ALU.mult).then_inc(rq_done, 1)
                    dve.wait_ge(rq_done, 1)
                elif what[2] % 2:
                    t, g = what[1:]
                    for z, (j0, jn) in enumerate(pieces(MEM + P * (t + 1))):
                        at = SCORES_AT[t] + g * (MEM + P * (t + 1)) + j0
                        dve.wait_ge(o_full, O.nth(what + (z,)))
                        nc.vector.tensor_scalar(dots[:, at:at + jn], banks_o[O.bank(what + (z,))][:, 0:jn], rq[:, t, g:g + 1], None,
                                                ALU.mult).then_inc(o_free, 1)
            dve.wait_ge(zero_done, 1)
            for s in range(STEPS + STEPS_BLOCK + 3):
                if s < STEPS:
                    maxima(s)
                if 2 <= s < STEPS + 2:
                    select(s - 2)
                if s >= STEPS_BLOCK + 4 and (s - 4) % STEPS_BLOCK == 0:
                    gated_rows((s - 4) // STEPS_BLOCK - 1)
                if s > STEPS_TILE and (s - 6) % STEPS_TILE == 0:
                    residual((s - 6) // STEPS_TILE - 1)

        def start_sync(sp, b):
            sp.dma_start(xT, xT_d[b]).then_inc(x_in, 16)
            sp.dma_start(x0, x_d[b].rearrange("p (t d) -> p t d", t=TT)).then_inc(x_in, 16)

        def stack_sync(sp):
            for z, (stack, slots) in enumerate(((q_stack, Q_PARTS), (k_stack, K_PARTS))):
                sp.wait_ge(parts_done, z + 1)
                sp.dma_start(parts_d[z], parts[:, z].rearrange("p k s -> p (k s)")).then_inc(parts_out, 16)
                sp.wait_ge(parts_out, 16 * (z + 1))
                for slot, part in enumerate(slots):
                    heads = parts_d[z][:, part * S:(part + 1) * S].rearrange("(a h d) s -> h d a s", h=2, d=HD0)
                    for hp in range(2):
                        at = RB * hp + HD0 * slot
                        sp.dma_start(stack[at:at + HD0], heads[hp]).then_inc(stack_in, 16)
            sp.wait_ge(stack_in, 16 * 4 * SLOTS)

        def start_gpsimd(chain, pool):
            for z in range(2):
                pool.wait_ge(rot_done, z + 1)
                chain.link(nc.gpsimd.tensor_copy(parts[:, z, 0], rot[:, z]))
                chain.link(nc.gpsimd.tensor_tensor(part_t, rot[:, z], parts[:, z, 0], ALU.subtract))
                chain.link(nc.gpsimd.tensor_copy(parts[:, z, 1], part_t))
                chain.link(nc.gpsimd.tensor_tensor(part_t, part_t, parts[:, z, 1], ALU.subtract))
                nc.gpsimd.tensor_copy(parts[:, z, 2], part_t).then_inc(parts_done, 1)

        def start_tensor(pe, o_bank):
            pe.wait_ge(x_in, 32)
            for key, name in (("rq", "wq"), ("rqs", "wqs"), ("rk", "wk"), ("rks", "wks")):
                nc.tensor.matmul(o_bank(key)[:, :], w(name), xT[:, :], start=True, stop=True).then_inc(o_full, 1)

        def start_vector(dve, filled, O):
            for z, (k0, k1) in enumerate((("rq", "rqs"), ("rk", "rks"))):
                bank = filled(k0)
                if z:
                    dve.wait_ge(rot_done, z)
                nc.vector.tensor_tensor(rope_t[:, 0], bank[:, :], c("rope_c"), ALU.mult).then_inc(o_free, 1)
                bank = filled(k1)
                nc.vector.tensor_tensor(rope_t[:, 1], bank[:, :], c("rope_s"), ALU.mult).then_inc(o_free, 1)
                dve.wait_ge(o_free, O.nth(k1))
                nc.vector.tensor_tensor(rot[:, z], rope_t[:, 0], rope_t[:, 1], ALU.add).then_inc(rot_done, 1)

        def rows_sync(sp, g):
            sp.wait_ge(rows_done, 1)
            sp.dma_start(maxes_d[g], max_parts[:, g].rearrange("h k s -> h (k s)")).then_inc(rows_out, 16)
            sp.wait_ge(rows_out, 16)
            rows = maxes_d[g].rearrange("(a h) (k s) -> h k a s", h=2, k=3)
            for hp in range(2):
                at = RB * hp + MAX_ROW
                sp.dma_start(q_stack[at:at + 3, HS // 2 * g:HS // 2 * (g + 1)], rows[hp]).then_inc(rows_in, 16)

        def rows_scores(o_bank, i, h):
            bank, w = o_bank(("s", i, h)), P * (i + 1)
            for n in range(abreast(i)):
                a, odd = divmod(h + 2 * n, 2)
                nc.tensor.matmul(bank[:, w * n:w * n + w], q_stack[RB * odd:RB * odd + MAX_ROW, a, P * i:P * i + P],
                                 k_stack[RB * odd:RB * odd + MAX_ROW, a, 0:w], start=True, stop=False)
                ins = nc.tensor.matmul(bank[:, w * n + P * i:w * n + w], identb, mask_s, start=False, stop=True)
            ins.then_inc(o_full, 1)

        def maxima(pe, O, o_bank, g):
            pe.wait_ge(o_free, O.nth(("s", TT - 1, HS * (g + 1) - 1)))
            bank = o_bank(("mT", g))
            for i in range(TT):
                ins = nc.tensor.transpose(bank[0:HS, P * i:P * i + P], row_max[:, i, HS * g:HS * (g + 1)], ident)
            ins.then_inc(o_full, 1)

        def row_maximum(filled, i, h):
            bank, n = filled(("s", i, h)), abreast(i)
            scores = bank[:, 0:P * (i + 1) * n].rearrange("p (h w) -> p h w", h=n)
            nc.vector.tensor_reduce(row_max[:, i, h:h + 2 * n - 1:2], scores, X, ALU.max).then_inc(o_free, 1)

        def split_maxima(dve, chain, O, filled, g):
            bank = filled(("mT", g))
            nc.vector.tensor_scalar(neg_rows, bank[0:HS, :], -1.0, None, ALU.mult).then_inc(o_free, 1)
            dve.wait_ge(o_free, O.nth(("mT", g)))
            chain.link(nc.vector.tensor_copy(max_parts[:, g, 0], neg_rows))
            chain.link(nc.vector.tensor_tensor(neg_left, neg_rows, max_parts[:, g, 0], ALU.subtract))
            chain.link(nc.vector.tensor_copy(max_parts[:, g, 1], neg_left))
            chain.link(nc.vector.tensor_tensor(neg_left, neg_left, max_parts[:, g, 1], ALU.subtract))
            nc.vector.tensor_copy(max_parts[:, g, 2], neg_left).then_inc(rows_done, 1)

        def start(block):
            @block.sync
            def _(sp):
                start_sync(sp, 0)
                stack_sync(sp)
                rows_sync(sp, 0)
                sp.wait_ge(rows_in, 32)

            @block.gpsimd
            def _(pool):
                nc.gpsimd.memset(k_stack, 1.0)
                start_gpsimd(Chain(pool, g_chain), pool)

            @block.tensor
            def _(pe):
                o_bank = empty_banks(pe, None, RING_START)[1]
                start_tensor(pe, o_bank)
                pe.wait_ge(stack_in, 16 * 4 * SLOTS)
                for i, h in S_FIRST:
                    rows_scores(o_bank, i, h)
                maxima(pe, RING_START, o_bank, 0)

            @block.vector
            def _(dve):
                def filled(key):
                    dve.wait_ge(o_full, RING_START.nth(key))
                    return banks_o[RING_START.bank(key)]

                start_vector(dve, filled, RING_START)
                for i, h in S_FIRST:
                    row_maximum(filled, i, h)
                split_maxima(dve, Chain(dve, v_chain), RING_START, filled, 0)

        def front(block):
            A, O, M, T = RINGS

            @block.sync
            def _(sp):
                sp.dma_start(dots[:, 0:F1_N], ffn1_d).then_inc(ffn_in, 16)
                sp.dma_start(at2[:, 0:F2_N], ffn2_d).then_inc(ffn_in, 16)
                rows_sync(sp, 1)
                scores_sync(sp, RINGS)

            @block.gpsimd
            def _(pool):
                chain = Chain(pool, g_chain)

                nc.gpsimd.memset(v_pad[:, :, :, SUM_COLS:2 * SUM_COLS], 0.0)
                nc.gpsimd.memset(v_pad[:, :, :, HD0:SUM_COLS], 1.0)
                nc.gpsimd.memset(v_pad[:, :, :, 2 * SUM_COLS + HD0:V_COLS], 1.0).then_inc(init_done, 1)
                inverse_root(pool, 0)
                inverse_root(pool, 1)
                for k in range(NC):
                    pool.wait_ge(a_free, A.nth(("q", k)))
                    if k >= Q_SLOTS:
                        pool.wait_ge(q_summed, k - Q_SLOTS + 1)
                    nc.gpsimd.tensor_tensor(squares_of(k), qT_v[:, k, :], qT_v[:, k, :], ALU.mult).then_inc(q_sq, 1)

                scores_gpsimd(pool, chain, RINGS, False)

            @block.tensor
            def _(pe):
                a_bank, o_bank = empty_banks(pe, A, O)

                bank = a_bank("v")
                for t in range(TT):
                    ins = nc.tensor.matmul(bank[:, P * t:P * t + P], xT[:, P * t:P * t + P], w("wv"), start=True, stop=True)
                ins.then_inc(a_full, 1)
                def columns_scores(h):
                    at = RB * (h % 2)
                    for k in range(TT):
                        bank = a_bank(("st", h, k))
                        nc.tensor.matmul(bank[:, 0:S - P * k], k_stack[at:at + STACK, h // 2, P * k:P * k + P],
                                         q_stack[at:at + STACK, h // 2, P * k:S], start=True, stop=False)
                        nc.tensor.matmul(bank[:, 0:P], identb, mask_t, start=False, stop=True).then_inc(a_full, 1)

                def values0(h):
                    pe.wait_ge(a_free, A.nth(("st", h, TT - 1)))
                    a, odd = divmod(h, 2)
                    at = 2 * SUM_COLS * (a % (HS // 2))
                    for k in range(TT):
                        ins = nc.tensor.matmul(banks_t[h // HS][at:at + 2 * SUM_COLS, P * k:S],
                                               v_pad[:, k, a, SUM_COLS * odd:SUM_COLS * odd + 2 * SUM_COLS],
                                               exps[:, h % E_SLOTS, E_OFF[k]:E_OFF[k] + S - P * k],
                                               start=not odd and k == 0, stop=odd == 1 and k == TT - 1)
                    ins.then_inc(av0_done, 1)

                def sums_beside(g):
                    pe.wait_ge(sums_done, g + 1)
                    nc.tensor.matmul(o_bank(("den", g))[:, :], c("sums"), sums_in[:, g], start=True, stop=True).then_inc(o_full, 1)

                pe.wait_ge(init_done, 1)
                for h in range(H0 + 1):
                    if h < H0:
                        if h == HS:
                            pe.wait_ge(rows_in, 32)
                        columns_scores(h)
                    for i, h2 in S_SECOND[S_BESIDE * h:S_BESIDE * (h + 1)]:
                        rows_scores(o_bank, i, h2)
                    if S_BESIDE * h < len(S_SECOND) <= S_BESIDE * (h + 1):
                        maxima(pe, O, o_bank, 1)
                    if h:
                        values0(h - 1)
                    if h == HS + 1:
                        sums_beside(0)
                sums_beside(1)
                pe.wait_ge(out0_done, SETS)
                bank = o_bank("y0")
                for t in range(TT):
                    for g in range(SETS):
                        ins = nc.tensor.matmul(bank[:, P * t:P * t + P], out0[:, g, P * t:P * t + P], w("wo0")[:, P * g:P * g + P],
                                               start=g == 0, stop=g == SETS - 1)
                ins.then_inc(o_full, 1)
                pe.wait_ge(x1_done, 1)
                turned(a_bank("x1T"), x1)

                pe.wait_ge(ffn_in, 32)
                pe.wait_ge(a_free, A.nth("x1T"))
                for k in range(KC):
                    nc.tensor.matmul(a_bank(("f1", k))[:, :], f1("w1")[:, P * k:P * k + P], xT1[:, :], start=True,
                                     stop=True).then_inc(a_full, 1)
                    nc.tensor.matmul(o_bank(("f2", k))[:, :], f1("w2")[:, P * k:P * k + P], xT1[:, :], start=True,
                                     stop=True).then_inc(o_full, 1)
                pe.wait_ge(o_free, O.nth(("f2", KC - 1)))

                def hidden(name, wgt, src):
                    for k in range(KC):
                        bank = a_bank((name, k))
                        for j in range(KC):
                            ins = nc.tensor.matmul(bank[:, :], wgt[:, HID0 * j + P * k:HID0 * j + P * k + P], src[:, j, :],
                                                   start=j == 0, stop=j == KC - 1)
                        ins.then_inc(a_full, 1)

                hidden("h1", f1("h1"), hid)
                pe.wait_ge(a_free, A.nth(("h1", KC - 1)))
                hidden("h2", f2("h2"), gelu1)
                pe.wait_ge(a_free, A.nth(("h2", KC - 1)))
                bank = o_bank("y1")
                for t in range(TT):
                    for j in range(KC):
                        ins = nc.tensor.matmul(bank[:, P * t:P * t + P], gelu2[:, j, P * t:P * t + P], f2("w3")[:, P * j:P * j + P],
                                               start=j == 0, stop=j == KC - 1)
                ins.then_inc(o_full, 1)
                pe.wait_ge(x2_done, 1)
                turned(a_bank("x2T"), x2)

                pe.wait_ge(a_free, A.nth("x2T"))
                for t in range(TT):
                    for z in range(2):
                        nc.tensor.matmul(a_bank(("k", t, z))[:, :], xe[:, MEM + P * t:MEM + P * t + P], w("Wk")[:, 512 * z:512 * z + 512],
                                         start=True, stop=True).then_inc(a_full, 1)
                for k in range(NC):
                    nc.tensor.matmul(a_bank(("q", k))[:, :], w("Wq")[:, P * k:P * k + P], xe[:, MEM:J], start=True,
                                     stop=True).then_inc(a_full, 1)
                bank = a_bank("qs")
                for k in range(NC):
                    pe.wait_ge(q_sq, k + 1)
                    at = H1 - 2 - 2 * k
                    ins = nc.tensor.matmul(bank[0:H1, :], c("pick")[:, at:at + H1], squares_of(k), start=k == 0, stop=k == NC - 1)
                    ins.then_inc(q_summed if k < NC - 1 else a_full, 1)
                pe.wait_ge(k_normed, TT)

                scores_tensor(pe, RINGS, False)
                pe.wait_ge(worst_done, 1)
                nc.tensor.matmul(o_bank("bad")[0:1, 0:P], worst[:, :], ident, start=True, stop=True).then_inc(o_full, 1)

            @block.scalar
            def _(act):
                def filled(key):
                    act.wait_ge(a_full, A.nth(key))
                    return banks_a[A.bank(key)]

                def copied(key, dst, src=slice(0, 512)):
                    nc.scalar.copy(dst, filled(key)[:, src]).then_inc(a_free, 1)

                copied_v = filled("v")
                for odd in range(2):
                    ins = nc.scalar.copy(v_pad[:, :, :, 2 * SUM_COLS * odd:2 * SUM_COLS * odd + HD0],
                                         copied_v[:, :].rearrange("p (k a n) -> p k a n", k=TT, a=PAIRS)[:, :, :, HD0 * odd:HD0 * odd + HD0])
                ins.then_inc(a_free, 1)
                for h in range(H0):
                    if h >= E_SLOTS:
                        act.wait_ge(av0_done, h - E_SLOTS + 1)
                    for k in range(TT):
                        bank = filled(("st", h, k))
                        nc.scalar.activation(exps[:, h % E_SLOTS, E_OFF[k]:E_OFF[k] + S - P * k], bank[:, 0:S - P * k], ACT.Exp,
                                             scale=SCALE0).then_inc(a_free, 1)
                copied("x1T", xT1[:, :])
                for k in range(KC):
                    nc.scalar.activation(silu0[:, k], filled(("f1", k))[:, :], ACT.Silu, scale=w("w1s")[:, k:k + 1]).then_inc(a_free, 1)
                for k in range(KC):
                    nc.scalar.activation(gelu1[:, k], filled(("h1", k))[:, :], ACT.Gelu, scale=w("h1s")[:, k:k + 1]).then_inc(a_free, 1)
                for k in range(KC):
                    nc.scalar.activation(gelu2[:, k], filled(("h2", k))[:, :], ACT.Gelu, scale=w("h2s")[:, k:k + 1]).then_inc(a_free, 1)
                copied("x2T", xe[:, MEM:J])
                for t in range(TT):
                    for z in range(2):
                        copied(("k", t, z), k_rows[:, t, 512 * z:512 * z + 512])
                for k in range(NC):
                    copied(("q", k), qT_v[:, k, :])
                act.wait_ge(k_summed, 1)
                nc.scalar.activation(k_norm, k_norm, ACT.Sqrt).then_inc(k_rooted, 1)
                nc.scalar.activation(q_norm, filled("qs")[0:H1, :], ACT.Sqrt).then_inc(a_free, 1)
                act.wait_ge(rq_done, 1)

                scores_scalar(act, RINGS, False)

            @block.vector
            def _(dve):
                chain = Chain(dve, v_chain)

                def filled(key):
                    dve.wait_ge(o_full, O.nth(key))
                    return banks_o[O.bank(key)]

                for i, h in S_SECOND:
                    row_maximum(filled, i, h)
                split_maxima(dve, chain, O, filled, 1)
                for g in range(SETS):
                    dve.wait_ge(av0_done, HS * (g + 1))
                    nc.vector.tensor_copy(sums_in[:, g], banks_t[g][:, :]).then_inc(sums_done, 1)
                    bank = filled(("den", g))
                    nc.vector.reciprocal(rec0, bank[:, :]).then_inc(o_free, 1)
                    dve.wait_ge(o_free, O.nth(("den", g)))
                    nc.vector.tensor_tensor(out0[:, g], sums_in[:, g], rec0, ALU.mult).then_inc(out0_done, 1)
                    dve.wait_ge(out0_done, g + 1)
                bank = filled("y0")
                nc.vector.tensor_tensor(res[:, :, :], rows(bank), x0[:, :, :], ALU.add).then_inc(o_free, 1)
                dve.wait_ge(o_free, O.nth("y0"))
                norm(dve, chain, 0, x1, x1_done)
                for k in range(KC):
                    bank = filled(("f2", k))
                    dve.wait_ge(a_free, A.nth(("f1", k)))
                    nc.vector.scalar_tensor_tensor(out=hid[:, k], in0=bank[:, :], scalar=w("w2s")[:, k:k + 1], in1=silu0[:, k],
                                                   op0=ALU.mult, op1=ALU.mult).then_inc(o_free, 1)
                bank = filled("y1")
                nc.vector.tensor_tensor(res[:, :, :], rows(bank), w("w3s").unsqueeze(1).to_broadcast([P, TT, D]),
                                        ALU.mult).then_inc(o_free, 1)
                dve.wait_ge(o_free, O.nth("y1"))
                chain.link(nc.vector.tensor_tensor(res[:, :, :], res[:, :, :], x1[:, :, :], ALU.add))
                norm(dve, chain, 1, x2, x2_done)
                nc.vector.tensor_copy(kT_v[:, :, 0:MEM], memk_n[:, :].rearrange("p (c m) -> p c m", c=NC))
                by_head = [k_rows[:, t].rearrange("p (h d) -> p h d", h=H1) for t in range(TT)]
                for t in range(TT):
                    dve.wait_ge(a_free, A.nth(("k", t, 1)))
                    chain.link(nc.vector.tensor_tensor(k_squares, by_head[t], by_head[t], ALU.mult))
                    ins = nc.vector.tensor_reduce(k_norm[:, t], k_squares, X, ALU.add)
                    if t < TT - 1:
                        chain.link(ins)
                ins.then_inc(k_summed, 1)
                dve.wait_ge(k_rooted, 1)
                chain.link(nc.vector.tensor_scalar(k_norm, k_norm, 1e-12, None, ALU.max))
                chain.link(nc.vector.reciprocal(k_norm, k_norm))
                for t in range(TT):
                    nc.vector.tensor_tensor(by_head[t], by_head[t], k_norm[:, t].unsqueeze(2).to_broadcast([P, H1, HD1]),
                                            ALU.mult).then_inc(k_normed, 1)
                nc.vector.memset(above[:, 0:NARROW_FROM], AIM)
                scores_vector(dve, chain, RINGS, False)
                chain.link(nc.vector.tensor_scalar(off[:, :], above[:, :], -AIM, None, ALU.add))
                chain.link(nc.vector.tensor_tensor(off[:, :], off[:, :], off[:, :], ALU.mult))
                nc.vector.tensor_reduce(worst[:, :], off[:, :], X, ALU.max).then_inc(worst_done, 1)
                bank = filled("bad")
                chain.link(nc.vector.tensor_reduce(flag_f[:, :], bank[0:1, 0:P], X, ALU.max))
                chain.link(nc.vector.tensor_scalar(flag[:, :], flag_f[:, :], (WINDOW / 2) ** 2, None, ALU.is_gt))

        def again(block):
            @block.sync
            def _(sp):
                scores_sync(sp, RINGS_AGAIN)

            @block.gpsimd
            def _(pool):
                scores_gpsimd(pool, Chain(pool, g_chain), RINGS_AGAIN, True)

            @block.tensor
            def _(pe):
                scores_tensor(pe, RINGS_AGAIN, True)

            @block.scalar
            def _(act):
                scores_scalar(act, RINGS_AGAIN, True)

            @block.vector
            def _(dve):
                scores_vector(dve, Chain(dve, v_chain), RINGS_AGAIN, True)

        def experts(b, block):
            A, O = RINGS_EXPERTS

            @block.sync
            def _(sp):
                start_sync(sp, b + 1)
                sp.dma_start(dots[:, 0:M_N], moe_d).then_inc(moe_in, 16)
                stack_sync(sp)
                rows_sync(sp, 0)
                sp.wait_ge(x4_done, 1)
                sp.dma_start(out_d[b].rearrange("(t p) d -> p t d", p=P), x4[:, :, :]).then_inc(y_out, 16)
                sp.wait_ge(y_out, 16)
                sp.wait_ge(rows_in, 32)

            @block.gpsimd
            def _(pool):
                inverse_root(pool, 0)
                nc.gpsimd.memset(k_stack, 1.0)
                start_gpsimd(Chain(pool, g_chain), pool)
                inverse_root(pool, 1)

            @block.tensor
            def _(pe):
                a_bank, o_bank = empty_banks(pe, A, O)
                start_tensor(pe, o_bank)
                pe.wait_ge(x3_done, 1)
                turned(a_bank("x3T"), x3)
                pe.wait_ge(a_free, A.nth("x3T"))
                bank = o_bank("lg")
                for t in range(TT):
                    ins = nc.tensor.matmul(bank[:, EXPERTS * t:EXPERTS * (t + 1)], xT3[:, P * t:P * t + P], w("gate"), start=True, stop=True)
                ins.then_inc(o_full, 1)
                pe.wait_ge(moe_in, 16)
                pe.wait_ge(comb_done, 1)
                bank = o_bank("cT")
                for t in range(TT):
                    ins = nc.tensor.transpose(bank[0:EXPERTS, P * t:P * t + P], comb[:, t, :], ident)
                ins.then_inc(o_full, 1)
                pe.wait_ge(o_free, O.nth("cT"))
                for k in range(MC + 1):
                    n = P if k < MC else HID1
                    nc.tensor.matmul(a_bank(("m1", k))[0:n, :], mw("w1")[:, P * k:P * k + n], xT3[:, :], start=True,
                                     stop=True).then_inc(a_full, 1)
                    nc.tensor.matmul(o_bank(("m3", k))[0:n, :], mw("w3")[:, P * k:P * k + n], xT3[:, :], start=True,
                                     stop=True).then_inc(o_full, 1)
                    if k < MC:
                        nc.tensor.matmul(o_bank(("cb", k))[:, :], mw("spread")[0:EXPERTS, P * k:P * k + P], comb_T, start=True,
                                         stop=True).then_inc(o_full, 1)
                pe.wait_ge(o_free, O.nth(("m3", MC)))
                pe.wait_ge(stack_in, 16 * 4 * SLOTS)
                bank = a_bank("y3")
                for t in range(TT):
                    if t == TT - 1:
                        maxima(pe, O, o_bank, 0)
                    for k in range(MC + 1):
                        n = P if k < MC else HID1
                        ins = nc.tensor.matmul(bank[:, P * t:P * t + P], acts[0:n, k, P * t:P * t + P], mw("w2")[0:n, P * k:P * k + P],
                                               start=k == 0, stop=k == MC)
                        for i, h in after_product(t, k):
                            rows_scores(o_bank, i, h)
                ins.then_inc(a_full, 1)

            @block.scalar
            def _(act):
                def filled(key):
                    act.wait_ge(a_full, A.nth(key))
                    return banks_a[A.bank(key)]

                nc.scalar.copy(xT3[:, :], filled("x3T")[:, :]).then_inc(a_free, 1)
                act.wait_ge(o_free, O.nth("lg"))
                nc.scalar.activation(gates_e[:, :, 0:EXPERTS], logits[:, :, :], ACT.Exp).then_inc(ex_e_done, 1)
                for k in range(MC + 1):
                    n = P if k < MC else HID1
                    bank = filled(("m1", k))
                    if k >= 2:
                        act.wait_ge(o_free, O.nth(("m3", k - 2)))
                    nc.scalar.activation(silu1[0:n, k % 2], bank[0:n, :], ACT.Silu).then_inc(a_free, 1)

            @block.vector
            def _(dve):
                chain = Chain(dve, v_chain)

                def filled(key):
                    dve.wait_ge(o_full, O.nth(key))
                    return banks_o[O.bank(key)]

                norm(dve, chain, 0, x3, x3_done)
                start_vector(dve, filled, O)
                bank = filled("lg")
                lg = bank[:, 0:TT * EXPERTS].rearrange("p (t e) -> p t e", t=TT)
                chain.link(nc.vector.tensor_reduce(logit_m[:, :], lg, X, ALU.max))
                nc.vector.tensor_tensor(logits[:, :, :], lg, logit_m[:, :].unsqueeze(2).to_broadcast([P, TT, EXPERTS]),
                                        ALU.subtract).then_inc(o_free, 1)
                dve.wait_ge(ex_e_done, 1)
                for t in range(TT):
                    ins = nc.vector.max(out=top_e[:, t], in_=gates_e[:, t, 0:EXPERTS])
                chain.link(ins)
                chain.link(nc.vector.memset(top_e[:, :, TOP_E:8], -1.0))
                for t in range(TT):
                    ins = nc.vector.match_replace(out=rest_e[:, t], in_to_replace=top_e[:, t], in_values=gates_e[:, t], imm_value=0.0)
                chain.link(ins)
                chain.link(nc.vector.tensor_tensor(comb[:, :, :], gates_e[:, :, 0:EXPERTS], rest_e[:, :, 0:EXPERTS], ALU.subtract))
                chain.link(nc.vector.tensor_reduce(sum_e[:, :], comb[:, :, :], X, ALU.add))
                chain.link(nc.vector.reciprocal(rec_e[:, :], sum_e[:, :]))
                nc.vector.tensor_tensor(comb[:, :, :], comb[:, :, :], rec_e[:, :].unsqueeze(2).to_broadcast([P, TT, EXPERTS]),
                                        ALU.mult).then_inc(comb_done, 1)
                bank = filled("cT")
                nc.vector.tensor_copy(comb_T, bank[0:EXPERTS, :]).then_inc(o_free, 1)
                for k in range(MC + 1):
                    n = P if k < MC else HID1
                    bank = filled(("m3", k))
                    dve.wait_ge(a_free, A.nth(("m1", k)))
                    dst = gated[:, k % 2] if k < MC else acts[0:n, k]
                    nc.vector.tensor_tensor(dst, bank[0:n, :], silu1[0:n, k % 2], ALU.mult).then_inc(o_free, 1)
                    if k < MC:
                        bank = filled(("cb", k))
                        dve.wait_ge(o_free, O.nth(("m3", k)))
                        nc.vector.tensor_tensor(acts[:, k], bank[:, :], gated[:, k % 2], ALU.mult).then_inc(o_free, 1)
                for i, h in S_FIRST:
                    row_maximum(filled, i, h)
                split_maxima(dve, chain, O, filled, 0)
                dve.wait_ge(a_full, A.nth("y3"))
                chain.link(nc.vector.tensor_tensor(res[:, :, :], rows(banks_a[A.bank("y3")]), x3[:, :, :], ALU.add))
                norm(dve, chain, 1, x4, x4_done)

        with nc.Block() as block:
            start(block)
        clear_semaphores()
        with nc.Fori(0, B) as b:
            with nc.Block() as block:
                front(block)
            clear_semaphores()
            missed = nc.values_load(flag[:, :], min_val=0, max_val=1)
            with nc.If(missed > 0):
                with nc.Block() as block:
                    again(block)
                clear_semaphores()
            with nc.Block() as block:
                experts(b, block)
            clear_semaphores()


def constants():
    f = np.float32
    half = HD0 // 2
    inv = (1.0 / f(10000.0) ** (np.arange(half, dtype=f) / f(half))).astype(f)
    freqs = np.arange(S, dtype=f)[:, None] * inv[None, :]
    d = np.arange(P) % HD0
    cos, sin = np.cos(freqs)[:, d % half].T, np.sin(freqs)[:, d % half].T
    sin = np.where((d < half)[:, None], -sin, sin)
    q = np.arange(P)
    pick = q[:, None] // HD1 == np.arange(2 * H1 - 2)[None, :] - (H1 - 2)
    sums = q[:, None] == q[None, :] // SUM_COLS * SUM_COLS + HD0 + q[None, :] % HD0
    heads = (q[:, None] // HD1 == q[None, :] // HD1)
    dpre = (q[:, None] // H1 == q[None, :] // H1)
    dpost = (q[:, None] // H1 == q[None, :] % R8)
    spread = np.zeros((P, MC * P))
    spread[:EXPERTS] = np.arange(EXPERTS)[:, None] == np.arange(MC * P)[None, :] // HID1
    rank = np.broadcast_to(TOPK - 1 - np.arange(WINDOW), (P, WINDOW))
    c = np.concatenate([cos, sin, np.eye(P), heads, sums, pick, *thresholds(), rank], 1).astype(f)
    mask_s = np.where(q[None, :] > q[:, None], LOW, 0.0)
    mix = [np.where(np.arange(GROUP * R8)[None, :] > R8 * v + q[:, None] // H1, LOW, 0.0) for v in range(GROUP)]
    cb = np.concatenate([np.eye(P), mask_s, mask_s.T] + mix + [dpre, dpost], 1).astype(f)
    return c, cb, spread.astype(f)


def thresholds():
    first, slope = np.zeros((P, SUBS), np.float32), np.zeros((P, SUBS), np.float32)

    def quantile(share):
        lo, hi = -10.0, 10.0
        for _ in range(60):
            mid = (lo + hi) / 2
            lo, hi = (mid, hi) if (1 + erf(mid / sqrt(2))) / 2 < share else (lo, mid)
        return lo

    for n in range(NARROW_FROM, SUBS):
        for q in range(P):
            seen = R8 * n + q // H1 + 1 + MEM
            first[q, n] = quantile(1 - (AIM + 0.5) / seen)
            slope[q, n] = -1 / (2 * seen * exp(-first[q, n] ** 2 / 2) / sqrt(2 * pi))
    return first, slope


def laid_out(a):
    x = a["L0_attn_x"]
    qkv = a["L0_attn_w_qkv"]
    wq, wk, wv = qkv[:D], qkv[D:2 * D], qkv[2 * D:]
    swap = (np.arange(D) // HD0) * HD0 + (np.arange(D) + HD0 // 2) % HD0

    def cols(v):
        return v.reshape(-1, P).T

    def chunked(m):
        return m.reshape(-1, P, m.shape[1]).transpose(1, 0, 2).reshape(P, -1)

    hs = np.broadcast_to(np.repeat(a["L1_attn_head_scale_params"].reshape(H1), R8), (P, P))
    wo0 = np.pad(a["L0_attn_w_out"].T.reshape(SETS, HS, HD0, D), ((0, 0), (0, 0), (0, SUM_COLS - HD0), (0, 0)))
    wo0 = wo0.reshape(SETS, P, D).transpose(1, 0, 2).reshape(P, SETS * D)
    memk = a["L1_attn_mem_k"].reshape(NC, 2, MEM, HD1).transpose(1, 3, 0, 2).reshape(P, NC * MEM)
    pre = np.tile(a["L1_attn_W_pre_th"].T, (R8, R8))
    post = np.tile(np.repeat(a["L1_attn_W_post_th"].T, R8, axis=1), (R8, 1))
    w = [wq.T, wq[swap].T, wk.T, wk[swap].T, wv.T, wo0,
         cols(a["L0_ffn_w1_s"]), cols(a["L0_ffn_w2_s"]), cols(a["L0_ffn_h1_s"]), cols(a["L0_ffn_h2_s"]),
         np.broadcast_to(a["L0_ffn_w3_s"], (P, D)),
         a["L1_attn_Wk"], a["L1_attn_Wq"], a["L1_attn_Wv"], a["L1_attn_Wg"], cols(a["L1_attn_bg"]), hs,
         chunked(a["L1_attn_Wo"]), memk, pre, post, a["L1_ffn_gate_w"].T]
    memv = a["L1_attn_mem_v"].transpose(1, 0, 2).reshape(MEM, H1 * HD1)
    ffn1 = [a["L0_ffn_w1_w"].T, a["L0_ffn_w2_w"].T, chunked(a["L0_ffn_h1_w"].T)]
    ffn2 = [chunked(a["L0_ffn_h2_w"].T), chunked(a["L0_ffn_w3_w"].T)]
    up = [np.concatenate([a[f"L1_ffn_{n}"].reshape(MC * P, D), a[f"L1_ffn_s{n}"]]).T for n in ("w1", "w3")]
    down = np.concatenate([a["L1_ffn_w2"].transpose(0, 2, 1).reshape(MC * P, D), a["L1_ffn_sw2"].T, np.zeros((HID1, D), np.float32)])
    return {
        "xT": np.pad(x.transpose(0, 2, 1), ((0, 1), (0, 0), (0, 0))),
        "x": np.pad(x.reshape(B, TT, P, D).transpose(0, 2, 1, 3).reshape(B, P, TT * D), ((0, 1), (0, 0), (0, 0))),
        "w": np.concatenate(w, 1), "memv": memv,
        "ffn1": np.concatenate(ffn1, 1), "ffn2": np.concatenate(ffn2, 1),
        "moe": np.concatenate(up + [chunked(down), constants()[2]], 1),
    }


def kernel(**inputs):
    import concourse.bacc as bacc
    from concourse.bass_utils import run_bass_kernel_spmd

    arrays = {k: np.ascontiguousarray(v) for k, v in laid_out({k: np.asarray(v) for k, v in inputs.items()}).items()}
    arrays["c"], arrays["cb"], _ = constants()
    nc = bacc.Bacc("TRN2", target_bir_lowering=False, num_devices=1)
    d = {k: nc.dram_tensor(f"{k}_dram", v.shape, mybir.dt.from_np(v.dtype), kind="ExternalInput").ap() for k, v in arrays.items()}
    parts = nc.dram_tensor("parts_dram", [2, P, 3 * S], BF16, kind="Internal").ap()
    maxes = nc.dram_tensor("maxes_dram", [SETS, HS, 3 * S], BF16, kind="Internal").ap()
    out = nc.dram_tensor("out_dram", [B, S, D], F32, kind="ExternalOutput").ap()
    network(nc, d["xT"], d["x"], d["w"], d["c"], d["cb"], d["memv"], d["ffn1"], d["ffn2"], d["moe"], parts, maxes, out)
    r = run_bass_kernel_spmd(nc, [{f"{k}_dram": v for k, v in arrays.items()}], core_ids=[0])
    return r.results[0]["out_dram"]
```
